# Optimizing a Trainium2 kernel written in Bass

```python
import numpy as np
import jax
import jax.numpy as jnp

def _softmax(x, axis=-1):
    return jax.nn.softmax(x, axis=axis)

def _gelu(x):
    return jax.nn.gelu(x, approximate=True)

def _silu(x):
    return jax.nn.silu(x)

def _sigmoid(x):
    return jax.nn.sigmoid(x)

def _layernorm(x, axis=-1, eps=1e-05):
    m = jnp.mean(x, axis=axis, keepdims=True)
    v = jnp.var(x, axis=axis, keepdims=True)
    return (x - m) / jnp.sqrt(v + eps)

def _scatter_add(tgt, idx, src, axis=0):
    return tgt.at[idx].add(src)

def _segment_sum(src, seg, n):
    return jax.ops.segment_sum(src, seg, n)
kernel_name = 'mk_conv_attn_hybrid_d2_conv_nchw256_r4_58e235'

def setup_inputs(seed: int=0):
    np.random.seed(seed)
    _w = jnp.asarray

    def _rec_inputs():
        import jax
        import jax.numpy as jnp
        _gk = jax.random.key(seed)
        x = -8.268e-05 + 0.9999 * jax.random.normal(jax.random.fold_in(_gk, 1), (16, 64, 56, 56), jnp.float32)
        return x
    x = _rec_inputs()

    def _L0_conv_setup():
        import jax, jax.numpy as jnp
        import numpy as np
        from jax import lax
        EPS = 1e-05

        @jax.custom_vjp
        def binarize(x):
            return jnp.sign(x)

        def _bin_fwd(x):
            return (jnp.sign(x), x)

        def _bin_bwd(x, g):
            return (g * (jnp.abs(x) <= 1.0).astype(g.dtype),)
        binarize.defvjp(_bin_fwd, _bin_bwd)

        def bconv(x, w, stride=1, pad=0):
            return lax.conv_general_dilated(binarize(x), binarize(w), window_strides=(stride, stride), padding=[(pad, pad), (pad, pad)], dimension_numbers=('NCHW', 'OIHW', 'NCHW'))

        def bn(x, gamma, beta):
            mean = x.mean(axis=(0, 2, 3), keepdims=True)
            var = ((x - mean) ** 2).mean(axis=(0, 2, 3), keepdims=True)
            return gamma * (x - mean) * lax.rsqrt(var + EPS) + beta

        def hardtanh(x):
            return jnp.clip(x, -1.0, 1.0)
        key = jax.random.key(seed)
        ks = jax.random.split(key, 4)
        N, Cin, H, W = (16, 64, 56, 56)
        P = 16
        return {'x': jax.random.normal(ks[0], (N, Cin, H, W), dtype=jnp.float32), 'w1': jax.random.normal(ks[1], (P, Cin, 1, 1), dtype=jnp.float32), 'w2': jax.random.normal(ks[2], (P, P, 3, 3), dtype=jnp.float32), 'w3': jax.random.normal(ks[3], (Cin, P, 1, 1), dtype=jnp.float32), 'g1': jnp.ones((1, P, 1, 1), jnp.float32), 'b1': jnp.zeros((1, P, 1, 1), jnp.float32), 'g2': jnp.ones((1, P, 1, 1), jnp.float32), 'b2': jnp.zeros((1, P, 1, 1), jnp.float32), 'g3': jnp.ones((1, Cin, 1, 1), jnp.float32), 'b3': jnp.zeros((1, Cin, 1, 1), jnp.float32)}
    _L0_conv_all = _L0_conv_setup()
    _L0_conv_in = {k: v for k, v in _L0_conv_all.items() if k in ('w1', 'w2', 'w3', 'g1', 'b1', 'g2', 'b2', 'g3', 'b3')}
    del _L0_conv_all

    def _L1_attn_setup():
        import jax, jax.numpy as jnp
        import numpy as np
        DIM = 64
        HEADS = 4
        WIN = 64
        RADIUS = 32
        HEAD_DIM = DIM // HEADS
        SCALE = HEAD_DIM ** (-0.5)
        NEG_INF = -1e+30

        def _band_mask(T, radius):
            i = jnp.arange(T)[:, None]
            j = jnp.arange(T)[None, :]
            d = i - j
            return jnp.where((d >= 0) & (d <= radius), 0.0, -jnp.inf).astype(jnp.float32)
        key = jax.random.key(seed)
        k1, k2, k3 = jax.random.split(key, 3)
        B, T, C = (16, 1024, DIM)
        x = jax.random.normal(k1, (B, T, C), dtype=jnp.float32)
        Wqkv = jax.random.normal(k2, (C, 3 * C), dtype=jnp.float32) * 0.02
        Wproj = jax.random.normal(k3, (C, C), dtype=jnp.float32) * 0.02
        bproj = jnp.zeros((C,), dtype=jnp.float32)
        return {'x': x, 'Wqkv': Wqkv, 'Wproj': Wproj, 'bproj': bproj}
    _L1_attn_all = _L1_attn_setup()
    _L1_attn_in = {k: v for k, v in _L1_attn_all.items() if k in ('Wqkv', 'Wproj', 'bproj')}
    del _L1_attn_all

    def _L1_ffn_setup():
        import math
        import jax, jax.numpy as jnp
        import numpy as np
        CAPACITY_FACTOR = 1.25
        key = jax.random.key(seed)
        ks = jax.random.split(key, 5)
        B, L, D, F, E = (8, 2048, 64, 256, 8)
        h = jax.random.normal(ks[0], (B, L, D), dtype=jnp.float32)
        gate_w = jax.random.normal(ks[1], (D, E), dtype=jnp.float32) * 0.02
        gate_b = jnp.zeros((E,), dtype=jnp.float32)
        w1 = jax.random.normal(ks[2], (E, D, F), dtype=jnp.float32) * (1.0 / math.sqrt(D))
        b1 = jnp.zeros((E, F), dtype=jnp.float32)
        w2 = jax.random.normal(ks[3], (E, F, D), dtype=jnp.float32) * (1.0 / math.sqrt(F))
        b2 = jnp.zeros((E, D), dtype=jnp.float32)
        return {'h': h, 'gate_w': gate_w, 'gate_b': gate_b, 'w1': w1, 'b1': b1, 'w2': w2, 'b2': b2}
    _L1_ffn_all = _L1_ffn_setup()
    _L1_ffn_in = {k: v for k, v in _L1_ffn_all.items() if k in ('gate_w', 'gate_b', 'w1', 'b1', 'w2', 'b2')}
    del _L1_ffn_all
    return {'x': x, 'L0_conv_w1': _L0_conv_in['w1'], 'L0_conv_w2': _L0_conv_in['w2'], 'L0_conv_w3': _L0_conv_in['w3'], 'L0_conv_g1': _L0_conv_in['g1'], 'L0_conv_b1': _L0_conv_in['b1'], 'L0_conv_g2': _L0_conv_in['g2'], 'L0_conv_b2': _L0_conv_in['b2'], 'L0_conv_g3': _L0_conv_in['g3'], 'L0_conv_b3': _L0_conv_in['b3'], 'L1_attn_Wqkv': _L1_attn_in['Wqkv'], 'L1_attn_Wproj': _L1_attn_in['Wproj'], 'L1_attn_bproj': _L1_attn_in['bproj'], 'L1_ffn_gate_w': _L1_ffn_in['gate_w'], 'L1_ffn_gate_b': _L1_ffn_in['gate_b'], 'L1_ffn_w1': _L1_ffn_in['w1'], 'L1_ffn_b1': _L1_ffn_in['b1'], 'L1_ffn_w2': _L1_ffn_in['w2'], 'L1_ffn_b2': _L1_ffn_in['b2']}

def reference(x, L0_conv_w1, L0_conv_w2, L0_conv_w3, L0_conv_g1, L0_conv_b1, L0_conv_g2, L0_conv_b2, L0_conv_g3, L0_conv_b3, L1_attn_Wqkv, L1_attn_Wproj, L1_attn_bproj, L1_ffn_gate_w, L1_ffn_gate_b, L1_ffn_w1, L1_ffn_b1, L1_ffn_w2, L1_ffn_b2):
    import jax
    import jax.numpy as jnp

    def _L0_conv_ref(x, w1, w2, w3, g1, b1, g2, b2, g3, b3):
        import jax, jax.numpy as jnp
        import numpy as np
        from jax import lax
        EPS = 1e-05

        @jax.custom_vjp
        def binarize(x):
            return jnp.sign(x)

        def _bin_fwd(x):
            return (jnp.sign(x), x)

        def _bin_bwd(x, g):
            return (g * (jnp.abs(x) <= 1.0).astype(g.dtype),)
        binarize.defvjp(_bin_fwd, _bin_bwd)

        def bconv(x, w, stride=1, pad=0):
            return lax.conv_general_dilated(binarize(x), binarize(w), window_strides=(stride, stride), padding=[(pad, pad), (pad, pad)], dimension_numbers=('NCHW', 'OIHW', 'NCHW'))

        def bn(x, gamma, beta):
            mean = x.mean(axis=(0, 2, 3), keepdims=True)
            var = ((x - mean) ** 2).mean(axis=(0, 2, 3), keepdims=True)
            return gamma * (x - mean) * lax.rsqrt(var + EPS) + beta

        def hardtanh(x):
            return jnp.clip(x, -1.0, 1.0)
        out = hardtanh(bn(bconv(x, w1), g1, b1))
        out = hardtanh(bn(bconv(out, w2, stride=1, pad=1), g2, b2))
        out = bn(bconv(out, w3), g3, b3)
        out = out + x
        return hardtanh(out)

    def _L1_attn_ref(x, Wqkv, Wproj, bproj):
        import jax, jax.numpy as jnp
        import numpy as np
        DIM = 64
        HEADS = 4
        WIN = 64
        RADIUS = 32
        HEAD_DIM = DIM // HEADS
        SCALE = HEAD_DIM ** (-0.5)
        NEG_INF = -1e+30

        def _band_mask(T, radius):
            i = jnp.arange(T)[:, None]
            j = jnp.arange(T)[None, :]
            d = i - j
            return jnp.where((d >= 0) & (d <= radius), 0.0, -jnp.inf).astype(jnp.float32)
        B_prev, T_prev, C = x.shape
        xw = x.reshape(-1, WIN, C)
        Bw = xw.shape[0]
        qkv = xw @ Wqkv
        qkv = qkv.reshape(Bw, WIN, 3, HEADS, HEAD_DIM)
        qkv = qkv.transpose(2, 0, 3, 1, 4)
        q, k, v = (qkv[0], qkv[1], qkv[2])
        attn = jnp.einsum('bhid,bhjd->bhij', q, k) * SCALE
        attn = attn + _band_mask(WIN, RADIUS)[None, None]
        attn = jax.nn.softmax(attn, axis=-1)
        out = jnp.einsum('bhij,bhjd->bhid', attn, v)
        out = out.transpose(0, 2, 1, 3).reshape(Bw, WIN, C)
        out = out @ Wproj + bproj
        return out.reshape(B_prev, T_prev, C)

    def _L1_ffn_ref(h, gate_w, gate_b, w1, b1, w2, b2):
        import math
        import jax, jax.numpy as jnp
        import numpy as np
        CAPACITY_FACTOR = 1.25
        B, L, D = h.shape
        E = gate_w.shape[1]
        T = B * L
        C = max(1, math.ceil(CAPACITY_FACTOR * T / E))
        x = h.reshape(T, D)
        logits = x @ gate_w + gate_b
        probs = jax.nn.softmax(logits, axis=-1)
        idx = jnp.argmax(probs, axis=-1)
        prb = jnp.take_along_axis(probs, idx[:, None], axis=1)[:, 0]
        one_hot = jax.nn.one_hot(idx, E, dtype=jnp.float32)
        pos = (jnp.cumsum(one_hot, axis=0) * one_hot).sum(-1).astype(jnp.int32) - 1
        kept = pos < C
        pos_safe = jnp.where(kept, pos, C)
        buf = jnp.zeros((E, C, D), dtype=h.dtype).at[idx, pos_safe].set(x, mode='drop')
        hmid = jax.nn.relu(jnp.einsum('ecd,edf->ecf', buf, w1) + b1[:, None, :])
        ybuf = jnp.einsum('ecf,efd->ecd', hmid, w2) + b2[:, None, :]
        pos_g = jnp.minimum(pos, C - 1)
        y_tok = ybuf[idx, pos_g] * (prb * kept)[:, None]
        y = y_tok.reshape(B, L, D)
        y = jnp.nan_to_num(y, nan=0.0, posinf=10000.0, neginf=-10000.0)
        return y

    def _gn(v, G=32, eps=1e-05):
        B_, C_, H_, W_ = v.shape
        g = v.reshape(B_, G, C_ // G, H_, W_)
        m = jnp.mean(g, axis=(2, 3, 4), keepdims=True)
        s = jnp.var(g, axis=(2, 3, 4), keepdims=True)
        return ((g - m) / jnp.sqrt(s + eps)).reshape(v.shape)

    def _ln_c(v, eps=1e-06):
        m = jnp.mean(v, axis=1, keepdims=True)
        s = jnp.var(v, axis=1, keepdims=True)
        return (v - m) / jnp.sqrt(s + eps)

    def _ln_t(v, eps=1e-05):
        m = jnp.mean(v, axis=-1, keepdims=True)
        s = jnp.var(v, axis=-1, keepdims=True)
        return (v - m) / jnp.sqrt(s + eps)

    def _to_tokens(v):
        B_, C_, H_, W_ = v.shape
        return v.reshape(B_, C_, H_ * W_).transpose(0, 2, 1)

    def _from_tokens(t, like):
        B_, C_, H_, W_ = like.shape
        return t.transpose(0, 2, 1).reshape(B_, C_, H_, W_)
    x = _L0_conv_ref(x, L0_conv_w1, L0_conv_w2, L0_conv_w3, L0_conv_g1, L0_conv_b1, L0_conv_g2, L0_conv_b2, L0_conv_g3, L0_conv_b3)
    t = _to_tokens(x)
    t = t + _L1_attn_ref(_ln_t(t), L1_attn_Wqkv, L1_attn_Wproj, L1_attn_bproj)
    t = t + _L1_ffn_ref(_ln_t(t), L1_ffn_gate_w, L1_ffn_gate_b, L1_ffn_w1, L1_ffn_b1, L1_ffn_w2, L1_ffn_b2)
    x = _from_tokens(t, x)
    return x

_drawn_inputs = setup_inputs


def setup_inputs(seed=0):
    import zlib

    import numpy as np

    out = dict(_drawn_inputs(seed))
    spreads = {'L0_conv_g1': (1.0, 0.2),
     'L0_conv_b1': (0.0, 0.1),
     'L0_conv_g2': (1.0, 0.2),
     'L0_conv_b2': (0.0, 0.1),
     'L0_conv_g3': (1.0, 0.2),
     'L0_conv_b3': (0.0, 0.1),
     'L1_attn_bproj': (0.0, 0.1),
     'L1_ffn_gate_b': (0.0, 0.1),
     'L1_ffn_b1': (0.0, 0.605),
     'L1_ffn_b2': (0.0, 0.415)}
    factors = {'L1_attn_Wqkv': 3.889, 'L1_attn_Wproj': 3.779}
    for name, (base, spread) in spreads.items():
        noise = np.random.default_rng([zlib.crc32(name.encode()), seed]).standard_normal(out[name].shape)
        drawn = base * np.exp(spread * noise) if base else spread * noise
        out[name] = jnp.asarray(drawn.astype(out[name].dtype))
    for name, factor in factors.items():
        out[name] = (out[name] * factor).astype(out[name].dtype)
    return out
```

```python
from contextlib import ExitStack

import concourse.bass as bass
from concourse import mybir

ALU = mybir.AluOpType
ACT = mybir.ActivationFunctionType
AX = mybir.AxisListType
F32 = mybir.dt.float32
BF16 = mybir.dt.bfloat16
I32 = mybir.dt.int32

P = 128
NIMG, CIN, H, W = 16, 64, 56, 56
PIX = H * W
TOK = NIMG * PIX
CB = 16
NQ = 4
HC = 448
RPC = HC // W
NCH = 2 * PIX // HC
HEADS, HD, WIN, RADIUS = 4, 16, 64, 32
SCALE = HD ** -0.5
NEG = -1e30
VW = HD + 1
NB = 7
GT = 2 * NB
GW = NB * P
NG = TOK // (GT * P)
E, F = 8, 256
CAP = -(-5 * TOK // (4 * E))
TPE = -(-CAP // (2 * P)) * 2
ES = TPE * P
SLOTS = E * ES
NOWHERE = 1048576.0
ROW = CIN + 4
RP, RI, RM, RS = CIN, CIN + 1, CIN + 2, CIN + 3
CHUNKS = ((0, 4), (4, 3))
BN_EPS = LN_EPS = 1e-5
FLT_MAX = 3.4028235e38


def pieces(start, length):
    out, at = [], 0
    while at < length:
        image, pixel = divmod(start + at, PIX)
        n = min(length - at, PIX - pixel)
        out.append((image, pixel, at, n))
        at += n
    return out


def spread(a, axis, count):
    a = a.unsqueeze(axis)
    shape = list(a.shape)
    shape[axis] = count
    return a.broadcast_to(shape)


ARRAYS = ("x", "w1", "w2", "w3", "gb12", "g3", "b3", "w_qkv", "w_proj", "b_proj", "gate_w", "gate_bias",
          "e_w1", "e_b1", "e_w2", "e_b2", "out")


class Net:

    def __init__(self, a):
        (self.x, self.w1, self.w2, self.w3, self.gb12, self.g3, self.b3, self.w_qkv, self.w_proj, self.b_proj,
         self.gate_w, self.gate_bias, self.e_w1, self.e_b1, self.e_w2, self.e_b2, self.out) = (a[k] for k in ARRAYS)


def conv_stage(nc, n):
    with ExitStack() as ctx:
        def sb(name, shape, dt=F32):
            return ctx.enter_context(nc.sbuf_tensor(name, shape, dt))

        def sem(name):
            return ctx.enter_context(nc.semaphore(name))

        XR = 3
        xc = sb("xc", [P, XR, NQ, HC])
        xs = sb("xs", [P, 2, NQ, HC], BF16)
        y = sb("y", [P, NCH, HC], BF16)
        sp_ = sb("signs_padded", [P, 2, H + 2, W + 2], BF16)
        s2 = sb("s2", [P, NCH * HC], BF16)
        s2T = sb("s2T", [P, 2, NB, P], BF16)
        w1f = sb("w1f", [P, 32])
        w1s = sb("w1s", [P, 32], BF16)
        w2f = sb("w2f", [P, 9, P])
        w2s = sb("w2s", [P, 9, P], BF16)
        w3f = sb("w3f", [P, CIN])
        w3s = sb("w3s", [P, CIN])
        gb = sb("gb", [P, 4])
        gb3 = sb("gb3", [P, 2, CIN])
        same = sb("same_channel", [P, P])
        pi = sb("pi", [P, P])
        pj = sb("pj", [P, 1])
        blk = sb("same_group", [P, P])
        st = sb("st", [P, NCH, 6])
        agg = sb("agg", [P, 2])
        mom = sb("mom", [P, 2])
        mv = sb("mv", [P, 6])
        ab = sb("ab", [P, 2])
        s2sum = sb("s2sum", [P, NCH])
        s2tot = sb("s2tot", [P, 1])
        gram = sb("gram", [P, P])
        t1 = sb("t1", [P, CIN])
        t3 = sb("t3", [P, CIN])
        row = sb("row", [P, 8, CIN])
        ones = sb("ones", [P, P])
        junk = sb("empty_rows", [P, 16, ROW])
        zero = sb("zero_rows", [P, 16, CIN])
        c1 = sb("c1", [P, 3, P])
        pmod = sb("pmod", [P, 1])
        ps = [ctx.enter_context(nc.psum_tensor(f"cps{i}", [P, 512], F32)) for i in range(4)]
        psT = [ctx.enter_context(nc.psum_tensor(f"cpt{i}", [P, NB * P], BF16)) for i in range(2)]
        psG = ctx.enter_context(nc.psum_tensor("cpg", [P, 512], F32))
        psS = ctx.enter_context(nc.psum_tensor("cpsm", [P, 512], F32))

        xin = [sem(f"x_in{i}") for i in range(XR)]
        w_in, zeroed, iot, cst = sem("w_in"), sem("w_zeroed"), sem("iota_done"), sem("consts")
        w_signs, x_signs, conv_done, y_done = sem("w_signs"), sem("x_signs"), sem("conv_done"), sem("y_done")
        bn_step, bn_pow, bn_mm, act_sign = sem("bn_step"), sem("bn_pow"), sem("bn_mm"), sem("act_sign")
        tr, trc, gdone, s2_out, init = sem("s2_transposed"), sem("s2T_done"), sem("gram_done"), sem("s2_out"), sem("init")
        pconst = sem("pool_const")
        tail = sem("tail")
        block = ctx.enter_context(nc.Block())

        @block.sync
        def _(sp):
            for c in range(NCH):
                if c >= XR:
                    sp.wait_ge(x_signs, c - XR + 1)
                image, pixel = divmod(c * HC, PIX)
                for j in range(2):
                    sp.dma_start(xc[64 * j:64 * j + 64, c % XR, :, :],
                                 n.x.rearrange("(q j i) c p -> j i c q p", q=NQ, j=2)[j, image, :, :, pixel:pixel + HC]
                                 ).then_inc(xin[c % XR], 16)
                if c == 1:
                    sp.wait_ge(zeroed, 2)
                    for j in range(2):
                        sp.dma_start(w1f[64 * j:64 * j + 64, 16 * j:16 * j + 16], n.w1).then_inc(w_in, 16)
                    for g in range(8):
                        r = slice(16 * g, 16 * g + 16)
                        sp.dma_start(w2f[r, :, r], n.w2).then_inc(w_in, 16)
                        sp.dma_start(w3f[r, :], n.w3).then_inc(w_in, 16)
                        sp.dma_start(gb[r, :], n.gb12).then_inc(w_in, 16)
                    sp.dma_start(gb3[:, 0, :], n.g3.broadcast_to([P, n.g3.shape[1]])).then_inc(w_in, 16)
                    sp.dma_start(gb3[:, 1, :], n.b3.broadcast_to([P, n.b3.shape[1]])).then_inc(w_in, 16)
            sp.wait_ge(pconst, 5)
            for k in range(SLOTS // (P * 16)):
                sp.dma_start(n.slots[k * P * 16:(k + 1) * P * 16, :].rearrange("(p r) d -> p (r d)", p=P),
                             junk[:, :, :].rearrange("p r d -> p (r d)")).then_inc(init, 16)
            rows, k = P * 16, 0
            while k < TOK:
                m = min(rows, TOK - k) // P
                sp.dma_start(n.y_tok[k:k + m * P, :].rearrange("(p r) d -> p (r d)", p=P),
                             zero[:, 0:m, :].rearrange("p r d -> p (r d)")).then_inc(init, 16)
                k += m * P
            n_init = SLOTS // rows + -(-TOK // rows)
            for q in range(2):
                sp.wait_ge(act_sign, 2 + 7 * (q + 1))
                w = slice(q * PIX, (q + 1) * PIX)
                for i in range(8):
                    sp.dma_start(n.s2_dram[2 * i + q, :, :], s2[16 * i:16 * i + 16, w]).then_inc(s2_out, 16)
            sp.wait_ge(s2_out, 16 * 16)
            sp.wait_ge(init, 16 * n_init)

        @block.gpsimd
        def _(pool):
            pool.memset(w2f[:, :, :], 0.0).then_inc(zeroed, 1)
            pool.memset(w1f[:, :], 0.0).then_inc(zeroed, 1)
            pool.memset(junk[:, :, :], 0.0).then_inc(pconst, 1)
            pool.memset(zero[:, :, :], 0.0).then_inc(pconst, 1)
            pool.memset(sp_[:, :, :, :], 0.0).then_inc(pconst, 1)
            pool.wait_ge(pconst, 3)
            pool.memset(junk[:, :, RI:RI + 1], NOWHERE).then_inc(pconst, 1)
            pool.memset(ones[:, :], 1.0).then_inc(pconst, 1)
            pool.iota(c1[:, 0, :], [[0, 8], [1, 16]], base=0, channel_multiplier=0,
                      allow_small_or_imprecise_dtypes=True).then_inc(iot, 1)
            pool.iota(c1[:, 1, :], [[1, 8], [0, 16]], base=0, channel_multiplier=0,
                      allow_small_or_imprecise_dtypes=True).then_inc(iot, 1)
            pool.iota(pj[:, :], [[0, 1]], base=0, channel_multiplier=1,
                      allow_small_or_imprecise_dtypes=True).then_inc(iot, 1)
            for k in range(3):
                pool.wait_ge(bn_step, (4, 10, 19)[k])
                if k < 2:
                    pool.tensor_tensor(mv[:, 3:4], mv[:, 2:3], n.mhalf[:, 0:1], ALU.pow).then_inc(bn_pow, 1)
                else:
                    pool.tensor_tensor(row[:, 3, :], row[:, 2, :], n.mhalf[:, 0:CIN], ALU.pow).then_inc(bn_pow, 1)

        @block.tensor
        def _(pe):
            pe.wait_ge(w_signs, 1)
            for c in range(NCH):
                pe.wait_ge(x_signs, c + 1)
                if c >= 2:
                    pe.wait_ge(y_done, c - 1)
                for q in range(NQ):
                    mm = pe.matmul(ps[c % 2][32 * q:32 * q + 32, 0:HC], w1s[:, :], xs[:, c % 2, q, :],
                                   start=True, stop=True)
                mm.then_inc(conv_done, 1)
            pe.wait_ge(cst, 2)
            pe.wait_ge(bn_step, 2)
            pe.matmul(psS[:, 0:2], same[:, :], mom[:, :], start=True, stop=True).then_inc(bn_mm, 1)
            pe.wait_ge(w_signs, 2)
            for c in range(NCH):
                pe.wait_ge(act_sign, 1 + (1 if c < 7 else 2) - 1)
                pe.wait_ge(y_done, NCH + max(c - 1, 0))
                for k in range(9):
                    dy, dx = divmod(k, 3)
                    i, r = divmod(c * RPC, H)
                    mm = pe.matmul(ps[c % 2][:, 0:HC], w2s[:, k, :], sp_[:, i, r + dy:r + dy + RPC, dx:dx + W],
                                   start=(k == 0), stop=(k == 8))
                mm.then_inc(conv_done, 1)
            pe.wait_ge(bn_step, 8)
            pe.matmul(psS[:, 2:4], same[:, :], mom[:, :], start=True, stop=True).then_inc(bn_mm, 1)

            def transposes(g):
                pe.wait_ge(act_sign, 2 + 2 * g + 2)
                if g >= 2:
                    pe.wait_ge(trc, g - 1)
                for b in range(NB):
                    mm = pe.transpose(psT[g % 2][:, b * P:(b + 1) * P], s2[:, (g * NB + b) * P:(g * NB + b + 1) * P],
                                      n.ident_b[:, :])
                mm.then_inc(tr, 1)

            transposes(0)
            for g in range(NB):
                if g + 1 < NB:
                    transposes(g + 1)
                pe.wait_ge(trc, g + 1)
                for b in range(NB):
                    mm = pe.matmul(psG[:, 0:P], s2T[:, g % 2, b, :], s2T[:, g % 2, b, :],
                                   start=(g == 0 and b == 0), stop=(g == NB - 1 and b == NB - 1))
                mm.then_inc(gdone, 1)
            pe.wait_ge(bn_step, 13)
            pe.matmul(psS[:, 64:128], gram[:, :], w3s[:, :], start=True, stop=True).then_inc(bn_mm, 1)
            pe.wait_ge(bn_step, 15)
            pe.matmul(psS[:, 128:192], ones[:, :], t1[:, :], start=True, stop=True)
            pe.matmul(psS[:, 192:256], ones[:, :], t3[:, :], start=True, stop=True).then_inc(bn_mm, 1)

        @block.scalar
        def _(act):
            act.wait_ge(w_in, 16 * 28)
            act.activation(w1s[:, :], w1f[:, :], ACT.Sign).then_inc(w_signs, 1)
            act.activation(w2s[:, :, :], w2f[:, :, :], ACT.Sign).then_inc(w_signs, 1)
            act.activation(w3s[:, :], w3f[:, :], ACT.Sign).then_inc(w_signs, 1)
            for c in range(NCH):
                act.wait_ge(xin[c % XR], 32 * (c // XR + 1))
                if c >= 2:
                    act.wait_ge(conv_done, c - 1)
                act.activation(xs[:, c % 2, :, :], xc[:, c % XR, :, :], ACT.Sign).then_inc(x_signs, 1)
            act.wait_ge(pconst, 3)
            act.wait_ge(bn_step, 6)
            for i in range(2):
                act.activation(sp_[:, i, 1:H + 1, 1:W + 1],
                               y[:, 7 * i:7 * i + 7, :].rearrange("p c (r w) -> p (c r) w", w=W),
                               ACT.Sign, bias=ab[:, 1:2], scale=ab[:, 0:1]).then_inc(act_sign, 1)
            act.wait_ge(bn_step, 12)
            for c in range(NCH):
                act.activation(s2[:, c * HC:(c + 1) * HC], y[:, c, :], ACT.Sign, bias=ab[:, 1:2], scale=ab[:, 0:1],
                               accum_out=s2sum[:, c:c + 1]).then_inc(act_sign, 1)

        @block.vector
        def _(dve):
            step = [0]

            def link(ins):
                step[0] += 1
                ins.then_inc(bn_step, 1)
                dve.wait_ge(bn_step, step[0])

            dve.wait_ge(iot, 3)
            k = [0]

            def local(ins):
                k[0] += 1
                ins.then_inc(tail, 1)
                dve.wait_ge(tail, k[0])

            local(dve.tensor_scalar(blk[:, :], c1[:, 1, :], 16.0, None, ALU.mult))
            local(dve.tensor_scalar(pi[:, :], blk[:, :], pj[:, 0:1], -1.0, ALU.subtract, ALU.mult))
            local(dve.tensor_scalar(blk[:, :], pi[:, :], 15.5, None, ALU.is_lt))
            local(dve.scalar_tensor_tensor(blk[:, :], pi[:, :], -0.5, blk[:, :], ALU.is_gt, ALU.mult))
            local(dve.tensor_tensor(pi[:, :], pi[:, :], blk[:, :], ALU.mult))
            local(dve.tensor_reduce(pmod[:, :], pi[:, :], AX.X, ALU.add))
            local(dve.tensor_scalar(pmod[:, :], pmod[:, :], 1.0 / 16, None, ALU.mult))
            dve.tensor_scalar(same[:, :], c1[:, 0, :], pmod[:, 0:1], 0.125, ALU.is_equal, ALU.mult).then_inc(cst, 1)
            dve.memset(t1[:, :], 0.0).then_inc(cst, 1)

            for conv in range(2):
                for c in range(NCH):
                    dve.wait_ge(conv_done, NCH * conv + c + 1)
                    if conv and c == 0:
                        dve.wait_ge(act_sign, 2)
                    dve.bn_stats(st[:, c, :], ps[c % 2][:, 0:HC]).then_inc(tail, 1)
                    dve.tensor_copy(y[:, c, :], ps[c % 2][:, 0:HC]).then_inc(y_done, 1)
                k[0] += NCH
                dve.wait_ge(tail, k[0])
                link(dve.bn_aggr(agg[:, :], st[:, :, :]))
                local(dve.tensor_tensor(mv[:, 5:6], agg[:, 0:1], agg[:, 0:1], ALU.mult))
                local(dve.tensor_copy(mom[:, 0:1], agg[:, 0:1]))
                link(dve.tensor_tensor(mom[:, 1:2], agg[:, 1:2], mv[:, 5:6], ALU.add))
                dve.wait_ge(bn_mm, conv + 1)
                local(dve.tensor_copy(mv[:, 0:2], psS[:, 2 * conv:2 * conv + 2]))
                local(dve.tensor_tensor(mv[:, 4:5], mv[:, 0:1], mv[:, 0:1], ALU.mult))
                link(dve.tensor_tensor(mv[:, 2:3], mv[:, 1:2], mv[:, 4:5], ALU.subtract))
                link(dve.tensor_scalar(mv[:, 2:3], mv[:, 2:3], BN_EPS, None, ALU.add))
                dve.wait_ge(bn_pow, conv + 1)
                if conv:
                    dve.wait_ge(act_sign, 2)
                link(dve.tensor_tensor(ab[:, 0:1], mv[:, 3:4], gb[:, 2 * conv:2 * conv + 1], ALU.mult))
                local(dve.tensor_tensor(mv[:, 5:6], ab[:, 0:1], mv[:, 0:1], ALU.mult))
                link(dve.tensor_tensor(ab[:, 1:2], gb[:, 2 * conv + 1:2 * conv + 2], mv[:, 5:6], ALU.subtract))
            for g in range(NB):
                dve.wait_ge(tr, g + 1)
                if g >= 2:
                    dve.wait_ge(gdone, g - 1)
                dve.tensor_copy(s2T[:, g % 2, :, :].rearrange("p b t -> p (b t)"), psT[g % 2][:, :]).then_inc(trc, 1)
            dve.wait_ge(gdone, NB)
            dve.wait_ge(w_signs, 3)
            dve.wait_ge(act_sign, 2 + NCH)
            local(dve.tensor_reduce(s2tot[:, :], s2sum[:, :], AX.X, ALU.add))
            link(dve.tensor_tensor(gram[:, :], psG[:, 0:P], blk[:, :], ALU.mult))
            dve.wait_ge(bn_mm, 3)
            link(dve.tensor_tensor(t1[:, :], psS[:, 64:128], w3s[:, :], ALU.mult))
            link(dve.tensor_scalar(t3[:, :], w3s[:, :], s2tot[:, 0:1], None, ALU.mult))
            dve.wait_ge(bn_mm, 4)
            link(dve.tensor_scalar(row[:, 0, :], psS[:, 192:256], 1.0 / TOK, None, ALU.mult))
            link(dve.tensor_tensor(row[:, 1, :], row[:, 0, :], row[:, 0, :], ALU.mult))
            link(dve.scalar_tensor_tensor(row[:, 2, :], psS[:, 128:192], 1.0 / TOK, row[:, 1, :],
                                          ALU.mult, ALU.subtract))
            link(dve.tensor_scalar(row[:, 2, :], row[:, 2, :], BN_EPS, None, ALU.add))
            dve.wait_ge(bn_pow, 3)
            link(dve.tensor_tensor(row[:, 4, :], row[:, 3, :], gb3[:, 0, :], ALU.mult))
            link(dve.tensor_tensor(row[:, 5, :], row[:, 4, :], row[:, 0, :], ALU.mult))
            link(dve.tensor_tensor(row[:, 5, :], gb3[:, 1, :], row[:, 5, :], ALU.subtract))
            link(dve.tensor_tensor(row[:, 6, :], w3s[:, :], row[:, 4, :], ALU.mult))
            link(dve.tensor_scalar(row[:, 6, :], row[:, 6, :], n.pcol[:, 2:3], None, ALU.mult))
            link(dve.scalar_tensor_tensor(row[:, 6, :], row[:, 5, :], n.pcol[:, 3:4], row[:, 6, :], ALU.mult, ALU.add))
            for part in range(3):
                for j in range(2):
                    link(dve.tensor_scalar(n.w3p[:, part, CIN * j:CIN * j + CIN], row[0:33, 6, :],
                                           n.pcol[0:33, j:j + 1], None, ALU.mult))
                link(dve.tensor_copy(row[:, 7, :], row[:, 6, :]))
                link(dve.tensor_copy(n.part_b[:, :], row[:, 7, :]))
                link(dve.tensor_tensor(row[:, 6, :], row[:, 7, :], n.part_b[:, :], ALU.subtract))


def build(nc, a):
    with ExitStack() as ctx:
        def sb(name, shape, dt=F32):
            return ctx.enter_context(nc.sbuf_tensor(name, shape, dt))

        def sem(name):
            return ctx.enter_context(nc.semaphore(name))

        n = Net(a)
        n.slots = nc.dram_tensor("slots", (SLOTS, ROW), F32, kind="Internal").ap()
        n.y_tok = nc.dram_tensor("y_tok", (TOK, CIN), F32, kind="Internal").ap()
        n.s2_dram = nc.dram_tensor("s2_dram", (NIMG, CB, PIX), BF16, kind="Internal").ap()
        n.ident = sb("ident", [P, P])
        n.ident_b = sb("ident_b", [P, P], BF16)
        n.mhalf = sb("minus_half", [P, CIN])
        n.pcol = sb("pcol", [P, 4])
        n.w3p = sb("w3p", [33, 3, P], BF16)
        n.part_b = sb("part_b", [P, CIN], BF16)
        n.mask = sb("mask", [P, 2, HEADS, WIN], BF16)
        n.hmask = sb("hmask", [P, HEADS])
        n.jmask = sb("jmask", [P, 2])
        n.wqkv = sb("wqkv", [P, 3, P])
        n.wp = sb("wp", [P, P])
        n.gate = sb("gate", [P, 2 * E])
        n.bp = sb("bp", [3, 4 * P], BF16)
        n.ones3 = sb("ones3", [3, P], BF16)
        n.gate_b = sb("gate_b", [P, E])
        n.tri = sb("tri", [P, P], BF16)
        n.ones_b = sb("ones_b", [P, P], BF16)
        n.em8 = sb("em8", [P, E])
        n.t2 = sb("t2", [P, NG, NB, 2, ROW])
        const_stage(nc, n)
        conv_stage(nc, n)
        attention_stage(nc, n)
        expert_stage(nc, n)


def const_stage(nc, n):
    with ExitStack() as ctx:
        def sb(name, shape, dt=F32):
            return ctx.enter_context(nc.sbuf_tensor(name, shape, dt))

        def sem(name):
            return ctx.enter_context(nc.semaphore(name))

        brow = sb("brow", [1, 2, P])
        bpart = sb("bpart", [1, 3, 4, P], BF16)
        z, s, dz, w_in, d, moved = sem("k_memsets"), sem("k_selects"), sem("k_zeroed"), sem("k_weights"), sem("k_dve"), sem("k_moved")
        block = ctx.enter_context(nc.Block())

        @block.vector
        def _(dve):
            for t in (n.wqkv[:, :, :], n.wp[:, :], n.gate[:, :]):
                dve.memset(t, 0.0).then_inc(dz, 1)
            dve.memset(n.ones3[:, :], 1.0).then_inc(dz, 1)
            dve.wait_ge(w_in, 16 * 12)
            k = 0
            for part in range(3):
                ins = dve.tensor_copy(bpart[:, part, 0, :], brow[:, 0, :])
                k += 1
                ins.then_inc(d, 1)
                dve.wait_ge(d, k)
                for r in range(1, 4):
                    dve.tensor_copy(bpart[:, part, r, :], bpart[:, part, 0, :]).then_inc(d, 1)
                k += 3
                dve.tensor_tensor(brow[:, 1, :], brow[:, 0, :], bpart[:, part, 0, :], ALU.subtract).then_inc(d, 1)
                k += 1
                dve.wait_ge(d, k)
                dve.tensor_copy(brow[:, 0, :], brow[:, 1, :]).then_inc(d, 1)
                k += 1
                dve.wait_ge(d, k)

        @block.sync
        def _(sp):
            sp.wait_ge(dz, 3)
            for j in range(2):
                r = slice(64 * j, 64 * j + 64)
                for k in range(3):
                    sp.dma_start(n.wqkv[r, k, r], n.w_qkv[:, 64 * k:64 * k + 64]).then_inc(w_in, 16)
                sp.dma_start(n.wp[r, r], n.w_proj).then_inc(w_in, 16)
                sp.dma_start(n.gate[r, E * j:E * j + E], n.gate_w).then_inc(w_in, 16)
                sp.dma_start(brow[:, 0, r], n.b_proj).then_inc(w_in, 16)
            sp.dma_start(n.gate_b[:, :], n.gate_bias.broadcast_to([P, n.gate_bias.shape[1]])).then_inc(moved, 16)
            sp.wait_ge(d, 18)
            for part in range(3):
                sp.dma_start(n.bp[part:part + 1, :], bpart[:, part, :, :].rearrange("o r c -> o (r c)")).then_inc(moved, 16)
            sp.wait_ge(moved, 16 * 4)

        @block.gpsimd
        def _(pool):
            def select(out, pattern, op, base, mult, fill):
                select.k += 1
                pool.affine_select(out=out, in_=out, compare_op=op, fill=fill, base=base, pattern=pattern,
                                   channel_multiplier=mult).then_inc(s, 1)
                pool.wait_ge(s, select.k)
            select.k = 0
            ts = [(n.ident[:, :], 0.0), (n.ident_b[:, :], 0.0), (n.mhalf[:, :], -0.5), (n.mask[:, :, :, :], 0.0),
                  (n.hmask[:, :], 1.0), (n.tri[:, :], 1.0), (n.ones_b[:, :], 1.0), (n.pcol[:, :], 1.0), (n.jmask[:, :], 1.0)]
            for t, v in ts:
                pool.memset(t, v).then_inc(z, 1)
            pool.wait_ge(z, len(ts))
            for t in (n.ident, n.ident_b):
                select(t[:, :], [[-1, P]], ALU.not_equal, 0, 1, 1.0)
            for w in range(2):
                m = n.mask[64 * w:64 * w + 64, :, :, :]
                select(m, [[0, 2], [0, HEADS], [-1, WIN]], ALU.is_ge, 0, 1, NEG)
                select(m, [[0, 2], [0, HEADS], [1, WIN]], ALU.is_ge, RADIUS, -1, NEG)
            for j in range(2):
                m = n.hmask[64 * j:64 * j + 64, :]
                select(m, [[-HD, HEADS]], ALU.is_ge, 0, 1, 0.0)
                select(m, [[HD, HEADS]], ALU.is_ge, HD - 1, -1, 0.0)
            select(n.jmask[:, 0:1], [[0, 1]], ALU.is_ge, 63, -1, 0.0)
            select(n.jmask[:, 1:2], [[0, 1]], ALU.is_ge, -64, 1, 0.0)
            select(n.tri[:, :], [[1, P]], ALU.is_gt, 0, -1, 0.0)
            select(n.pcol[:, 0:1], [[0, 1]], ALU.is_ge, CB - 1, -1, 0.0)
            select(n.pcol[:, 0:1], [[0, 1]], ALU.not_equal, -32, 1, 1.0)
            select(n.pcol[:, 1:2], [[0, 1]], ALU.is_ge, -CB, 1, 0.0)
            select(n.pcol[:, 1:2], [[0, 1]], ALU.is_ge, 32, -1, 0.0)
            select(n.pcol[:, 2:3], [[0, 1]], ALU.is_ge, 31, -1, 0.0)
            select(n.pcol[:, 3:4], [[0, 1]], ALU.is_ge, -32, 1, 0.0)
            pool.iota(n.em8[:, :], [[1, E]], base=-E, channel_multiplier=0,
                      allow_small_or_imprecise_dtypes=True).then_inc(s, 1)
            pool.wait_ge(s, select.k + 1)


ORDER = ("t0", "t1", "rank", "ot0", "ot1", "xt0", "xt1", "pr0", "pr1", "q0", "q1", "k0", "k1", "v0", "v1",
         "zt0", "zt1", "gate")


def part_of(op):
    return "R" if op == "rank" else "Z" if op[:2] in ("ot", "pr", "zt", "ga") else "X"


def attention_stage(nc, n):
    with ExitStack() as ctx:
        def sb(name, shape, dt=F32):
            return ctx.enter_context(nc.sbuf_tensor(name, shape, dt))

        def sem(name):
            return ctx.enter_context(nc.semaphore(name))

        xg = sb("xg", [P, GW])
        s2g = sb("s2g", [33, GW], BF16)
        xn = sb("xn", [P, NB, 2, CIN])
        sq = sb("sq", [P, NB, 2, CIN])
        xnT = sb("xnT", [P, GW])
        actT = sb("actT", [P, GW])
        qT = sb("qT", [P, 2, 2, GW])
        kx = sb("kx", [P, 2, HEADS, GW])
        vs = sb("vs", [P, NB, 2, 2, 2, HD])
        vw = sb("vw", [P, NB, 2, 2, 2, HD])
        vb = sb("vb", [P, 2, NB, 2, 2, 2, VW])
        pb = sb("pb", [P, 2, 2, HEADS, WIN])
        pT = sb("pT", [P, 2, 4, P])
        ob = sb("ob", [P, 2, NB, 2 * HEADS, HD])
        mx = sb("mx", [P, 2, 2 * HEADS])
        rl = sb("rl", [P, 2, 2 * HEADS])
        sx = sb("sx", [P, 6, GT])
        sz = sb("sz", [P, 6, GT])
        lg = sb("lg", [P, GT, E])
        lw = sb("lw", [P, 2, GT, E])
        rt = sb("rt", [P, 8, GT])
        oh = sb("oh", [P, GT, E], BF16)
        ohf = sb("ohf", [P, GT, E])
        cnt = sb("cnt", [P, E, GT])
        inc = sb("inc", [P, E, GT])
        sd = sb("sd", [P, E, GT])
        notfirst = sb("notfirst", [P, E, GT])
        carry = sb("carry", [P, E])
        ids = sb("ids", [P, NB, 2])
        szk = sb("szk", [P, 2, 2, GT])
        dest = sb("dest", [P, 2, NB, 2], I32)
        S = [ctx.enter_context(nc.psum_tensor(f"S{i}", [P, 512], F32)) for i in range(2)]
        PT = ctx.enter_context(nc.psum_tensor("PT", [P, 512], F32))
        O = [ctx.enter_context(nc.psum_tensor(f"O{i}", [P, 512], F32)) for i in range(2)]
        M = [ctx.enter_context(nc.psum_tensor(f"M{i}", [P, 512], F32)) for i in range(3)]

        x_in, s_in, const = sem("x_in"), sem("s_in"), sem("a_const")
        s_ready, s_max, s_sub, s_exp = sem("s_ready"), sem("s_max"), sem("s_sub"), sem("s_exp")
        pt_ready, pt_copied, o_ready, o_recip, o_done = (sem("pt_ready"), sem("pt_copied"), sem("o_ready"),
                                                         sem("o_recip"), sem("o_done"))
        ready = {op: sem(f"{op}_ready") for op in ("t", "rank", "ot", "xt", "pr", "q", "k", "v", "zt", "gate")}
        taken = {op: sem(f"{op}_taken") for op in ("t", "rank", "ot", "xt", "pr", "q", "kd", "ka", "v", "zt", "gate")}
        ln = {(w, k): sem(f"{w}_{k}") for w in ("x", "z") for k in ("sum", "mean", "centered", "square", "sum2", "var", "rstd", "norm")}
        v_sw, v_built = sem("v_swapped"), sem("v_built")
        logit, r_step, r_exp, ranked, ids_step, scat = (sem("logit"), sem("r_step"), sem("r_exp"), sem("ranked"),
                                                        sem("ids_step"), [sem("scattered0"), sem("scattered1")])
        rank_q = sem("rank_wanted")
        kept = sem("z_stats_kept")
        block = ctx.enter_context(nc.Block())

        NBLK = NG * NB
        BODIES = range(-1, NG + 2)
        R_STEPS = 21

        def has_x(i):
            return i + 1 < NG

        def has_z(i):
            return 0 <= i - 1 < NG

        def has_r(i):
            return 0 <= i - 2 < NG

        def chunk(c):
            b0, nb = CHUNKS[c]
            return b0, nb, nb * P

        plan, last = {}, [None, None, None]
        turn = 0
        for i in BODIES:
            for op in ORDER:
                part = part_of(op)
                if not {"X": has_x, "Z": has_z, "R": has_r}[part](i):
                    continue
                g = {"X": i + 1, "Z": i - 1, "R": i - 2}[part]
                bank = turn % 3
                turn += 1
                plan[(op, g)] = (bank, last[bank])
                if op[0] == "k":
                    last[bank] = ("kd" if op == "k0" else "ka", g + 1)
                elif op in ("rank", "gate"):
                    last[bank] = (op, g + 1)
                else:
                    last[bank] = (op[:-1], 2 * g + int(op[-1]) + 1)

        def bank_of(op, g):
            return M[plan[(op, g)][0]]

        def swap(sp, g):
            sp.wait_ge(taken["v"], 2 * g + 2)
            if g >= 1:
                sp.wait_ge(v_built, 4 * g)
            for w in range(2):
                sp.dma_start(vw[64 * w:64 * w + 64, :, :, :, :, :].rearrange("p b j r h d -> p (b j r h d)"),
                             vs[64 - 64 * w:128 - 64 * w, :, :, :, :, :].rearrange("p b j r h d -> p (b j r h d)")
                             ).then_inc(v_sw, 16)

        @block.sync
        def _(sp):
            for g in range(NG):
                if g >= 1:
                    sp.wait_ge(ready["t"], 2 * g)
                for j in range(2):
                    for image, pixel, at, m in pieces((2 * g + j) * GW, GW):
                        sp.dma_start(xg[64 * j:64 * j + 64, at:at + m], n.x[image, :, pixel:pixel + m]).then_inc(x_in, 16)
                        sp.dma_start(s2g[16 * j:16 * j + 16, at:at + m],
                                     n.s2_dram[image, :, pixel:pixel + m]).then_inc(s_in, 16)
                if g >= 1:
                    swap(sp, g - 1)
            swap(sp, NG - 1)

        n_pieces = [sum(len(pieces((2 * g + j) * GW, GW)) for j in range(2)) for g in range(NG)]

        def loaded(eng, g):
            eng.wait_ge(x_in, 16 * sum(n_pieces[:g + 1]))
            eng.wait_ge(s_in, 16 * sum(n_pieces[:g + 1]))

        @block.tensor
        def _(pe):
            def free(op, g):
                before = plan[(op, g)][1]
                if before:
                    pe.wait_ge(taken[before[0]], before[1])
                return bank_of(op, g)

            def t(g, c):
                b0, nb, w = chunk(c)
                bank = free(f"t{c}", g)
                if c == 0:
                    loaded(pe, g)
                    pe.wait_ge(const, 3)
                for b in range(nb):
                    cols = slice((b0 + b) * P, (b0 + b + 1) * P)
                    out = bank[:, b * P:(b + 1) * P]
                    pe.matmul(out, xg[:, cols], n.ident[:, :], start=True, stop=False)
                    for part in range(3):
                        mm = pe.matmul(out, s2g[:, cols], n.w3p[:, part, :], start=False, stop=(part == 2))
                mm.then_inc(ready["t"], 1)

            def transposed(op, src, g, c, wait):
                b0, nb, w = chunk(c)
                bank = free(f"{op}{c}", g)
                if c == 0:
                    wait()
                for b in range(nb):
                    mm = pe.transpose(bank[:, b * P:(b + 1) * P], src(b0 + b), n.ident[:, :])
                mm.then_inc(ready[op], 1)

            def qk(g, c, which):
                b0, nb, w = chunk(c)
                bank = free(f"{'qk'[which]}{c}", g)
                pe.wait_ge(taken["xt"], 2 * g + c + 1)
                pe.matmul(bank[:, 0:w], n.wqkv[:, which, :], xnT[:, b0 * P:b0 * P + w],
                          start=True, stop=True).then_inc(ready["qk"[which]], 1)

            def v(g, c):
                b0, nb, w = chunk(c)
                bank = free(f"v{c}", g)
                pe.wait_ge(taken["xt"], 2 * g + c + 1)
                for b in range(nb):
                    mm = pe.matmul(bank[:, b * P:(b + 1) * P], xnT[:, (b0 + b) * P:(b0 + b + 1) * P], n.wqkv[:, 2, :],
                                   start=True, stop=True)
                mm.then_inc(ready["v"], 1)

            def pr(g, c):
                b0, nb, w = chunk(c)
                bank = free(f"pr{c}", g)
                pe.wait_ge(taken["ot"], 2 * g + c + 1)
                pe.matmul(bank[:, 0:w], n.ones3[:, :], n.bp[:, 0:w], start=True, stop=False, skip_group_check=True)
                for b in range(nb):
                    mm = pe.matmul(bank[:, b * P:(b + 1) * P], actT[:, (b0 + b) * P:(b0 + b + 1) * P], n.wp[:, :],
                                   start=False, stop=(b == nb - 1), skip_group_check=True)
                mm.then_inc(ready["pr"], 1)

            def gate(g):
                bank = free("gate", g)
                pe.wait_ge(taken["zt"], 2 * g + 2)
                for b in range(NB):
                    mm = pe.matmul(bank[:, b * 2 * E:(b + 1) * 2 * E], actT[:, b * P:(b + 1) * P], n.gate[:, :],
                                   start=True, stop=True)
                mm.then_inc(ready["gate"], 1)

            def rank(g):
                bank = free("rank", g)
                pe.wait_ge(rank_q, g + 1)
                flat = oh[:, :, :].rearrange("p t e -> p (t e)")
                pe.matmul(bank[:, 0:GT * E], n.tri[:, :], flat, start=True, stop=True)
                pe.matmul(bank[:, GT * E:2 * GT * E], n.ones_b[:, :], flat, start=True, stop=True)\
                    .then_inc(ready["rank"], 1)

            def scores(B):
                g, b = divmod(B, NB)
                if b == 0:
                    pe.wait_ge(taken["q"], 2 * g + 2)
                    pe.wait_ge(taken["kd"], g + 1)
                    pe.wait_ge(taken["ka"], g + 1)
                if B >= 2:
                    pe.wait_ge(s_sub, B - 1)
                bank = S[B % 2]
                pe.matmul(bank[:, :], n.ident_b[:, :], n.mask[:, :, :, :].rearrange("p j h k -> p (j h k)"),
                          start=True, stop=False, skip_group_check=True)
                for j in range(2):
                    for w in range(2):
                        cols = slice(b * P + 64 * w, b * P + 64 * w + 64)
                        mm = pe.matmul(bank[64 * w:64 * w + 64, 256 * j:256 * j + 256], qT[:, g % 2, j, cols],
                                       kx[:, g % 2, :, cols], start=False, stop=(j == 1), skip_group_check=True)
                mm.then_inc(s_ready, 1)

            def turn_probs(B):
                pe.wait_ge(s_exp, B + 1)
                if B >= 1:
                    pe.wait_ge(pt_copied, B)
                for j in range(2):
                    for r in range(2):
                        mm = pe.transpose(PT[:, (2 * j + r) * P:(2 * j + r + 1) * P],
                                          pb[:, B % 2, j, 2 * r:2 * r + 2, :], n.ident[:, :])
                mm.then_inc(pt_ready, 1)

            def values(B):
                g, b = divmod(B, NB)
                if b == 0:
                    pe.wait_ge(v_built, 4 * g + 4)
                pe.wait_ge(pt_copied, B + 1)
                if B >= 2:
                    pe.wait_ge(o_done, B - 1)
                for w in range(2):
                    for j in range(2):
                        for r in range(2):
                            at = (2 * j + r) * 2 * VW
                            mm = pe.matmul(O[B % 2][64 * w:64 * w + 64, at:at + 2 * VW],
                                           pT[:, B % 2, 2 * j + r, 64 * w:64 * w + 64],
                                           vb[:, w, b, j, r, :, :], start=True, stop=True)
                mm.then_inc(o_ready, 1)

            for i in BODIES:
                for s in range(NB):
                    B = i * NB + s
                    if 0 <= B < NBLK:
                        scores(B)
                    if 0 < B <= NBLK:
                        turn_probs(B - 1)
                    if s == 0 and has_x(i):
                        t(i + 1, 0)
                        t(i + 1, 1)
                    if s == 1 and has_r(i):
                        rank(i - 2)
                    if s == 2 and has_z(i):
                        for c in range(2):
                            transposed("ot", lambda b: ob[:, (i - 1) % 2, b, :, :].rearrange("p h d -> p (h d)"), i - 1, c,
                                       lambda: pe.wait_ge(o_done, i * NB))
                    if s == 3:
                        if has_x(i):
                            for c in range(2):
                                transposed("xt", lambda b: xn[:, b, :, :].rearrange("p j c -> p (j c)"), i + 1, c,
                                           lambda: pe.wait_ge(ln["x", "norm"], i + 2))
                        if has_z(i):
                            pr(i - 1, 0)
                            pr(i - 1, 1)
                    if s == 4 and has_x(i):
                        for which in range(2):
                            for c in range(2):
                                qk(i + 1, c, which)
                    if s == 5 and has_x(i):
                        v(i + 1, 0)
                        v(i + 1, 1)
                    if s == 6 and has_z(i):
                        for c in range(2):
                            transposed("zt", lambda b: xn[:, b, :, :].rearrange("p j c -> p (j c)"), i - 1, c,
                                       lambda: pe.wait_ge(ln["z", "norm"], i))
                    if 0 < B <= NBLK:
                        values(B - 1)
                    if s == 6 and has_z(i):
                        gate(i - 1)

        @block.scalar
        def _(act):
            def build_values(g):
                act.wait_ge(v_sw, 32 * (g + 1))
                act.wait_ge(ids_step, 4)
                if g >= 1:
                    act.wait_ge(o_ready, NB * g)
                for hh in range(2):
                    for w in range(2):
                        r = slice(64 * hh, 64 * hh + 64)
                        src = (vs if hh == w else vw)[r, :, :, :, hh, :].rearrange("p b j r d -> p (b j r) d")
                        act.activation(vb[r, w, :, :, :, hh, 0:HD].rearrange("p b j r d -> p (b j r) d"),
                                       src, ACT.Copy).then_inc(v_built, 1)

            def take(op, g, c, dst, wait=None):
                b0, nb, w = chunk(c)
                act.wait_ge(ready[op], 2 * g + c + 1)
                if wait:
                    act.wait_ge(*wait)
                act.activation(dst(b0, nb, w), bank_of(f"{op}{c}", g)[:, 0:w], ACT.Copy).then_inc(taken[op], 1)

            def cols(t):
                return lambda b0, nb, w: t[:, b0 * P:b0 * P + w]

            for i in BODIES:
                for s in range(NB):
                    B = i * NB + s
                    if 0 < B <= NBLK:
                        act.wait_ge(pt_ready, B)
                        if B >= 3:
                            act.wait_ge(o_ready, B - 2)
                        act.activation(pT[:, (B - 1) % 2, :, :].rearrange("p r t -> p (r t)"), PT[:, :],
                                       ACT.Copy).then_inc(pt_copied, 1)
                    if 0 <= B < NBLK:
                        act.wait_ge(s_sub, B + 1)
                        act.activation(pb[:, B % 2, :, :, :], pb[:, B % 2, :, :, :], ACT.Exp,
                                       scale=SCALE).then_inc(s_exp, 1)
                    if s == 0 and 0 <= i < NG:
                        build_values(i)
                    if s == 1 and has_x(i):
                        act.wait_ge(ln["x", "centered"], i + 2)
                        if i >= 1:
                            act.wait_ge(ln["z", "sum2"], i - 1)
                        act.activation(sq[:, :, :, :], xn[:, :, :, :], ACT.Square).then_inc(ln["x", "square"], 1)
                    if s == 2 and has_z(i):
                        for c in range(2):
                            take("ot", i - 1, c, cols(actT), (ready["gate"], i - 1))
                    if s == 3 and has_x(i):
                        for c in range(2):
                            take("xt", i + 1, c, cols(xnT), (ready["v"], 2 * i + 2))
                    if s == 4 and has_x(i):
                        if i >= 1:
                            act.wait_ge(s_ready, i * NB)
                        for c in range(2):
                            b0, nb, w = chunk(c)
                            act.wait_ge(ready["q"], 2 * (i + 1) + c + 1)
                            for j in range(2):
                                ins = act.activation(qT[:, (i + 1) % 2, j, b0 * P:b0 * P + w],
                                                     bank_of(f"q{c}", i + 1)[:, 0:w], ACT.Copy,
                                                     scale=n.jmask[:, j:j + 1])
                            ins.then_inc(taken["q"], 1)
                        b0, nb, w = chunk(1)
                        act.wait_ge(ready["k"], 2 * (i + 1) + 2)
                        for h in range(HEADS):
                            ins = act.activation(kx[:, (i + 1) % 2, h, b0 * P:b0 * P + w], bank_of("k1", i + 1)[:, 0:w],
                                                 ACT.Copy, scale=n.hmask[:, h:h + 1])
                        ins.then_inc(taken["ka"], 1)
                    if s == 5:
                        if has_z(i):
                            act.wait_ge(ln["z", "centered"], i)
                            if has_x(i):
                                act.wait_ge(ln["x", "sum2"], i + 2)
                            else:
                                act.wait_ge(ln["z", "sum2"], i - 1)
                            act.activation(sq[:, :, :, :], xn[:, :, :, :], ACT.Square).then_inc(ln["z", "square"], 1)
                        if has_x(i):
                            for c in range(2):
                                take("v", i + 1, c,
                                     lambda b0, nb, w: vs[:, b0:b0 + nb, :, :, :, :].rearrange("p b j r h d -> p (b j r h d)"),
                                     (v_built, 4 * (i + 1)) if c == 0 else None)
                    if s == 6 and has_z(i):
                        for c in range(2):
                            take("zt", i - 1, c, cols(actT), (ready["pr"], 2 * i))
                    if s == 0 and has_r(i):
                        act.wait_ge(r_step, R_STEPS * (i - 2) + 3)
                        act.activation(lw[:, 0, :, :], lw[:, 0, :, :], ACT.Exp).then_inc(r_exp, 1)

        @block.vector
        def _(dve):
            dve.memset(notfirst[:, :, :], 1.0).then_inc(const, 1)
            dve.memset(carry[:, :], 0.0).then_inc(const, 1)
            dve.memset(s2g[32:33, :], 1.0).then_inc(const, 1)
            dve.wait_ge(const, 3)
            dve.memset(notfirst[:, :, 0:1], 0.0).then_inc(const, 1)
            dve.wait_ge(const, 4)

            def ln_mean(w, src, st, g):
                dve.wait_ge(ln[w, "rstd"], g)
                dve.tensor_reduce(st[:, 0, :].rearrange("p (b j) -> p b j", j=2), src, AX.X, ALU.add)\
                    .then_inc(ln[w, "sum"], 1)
                dve.wait_ge(ln[w, "sum"], g + 1)
                dve.wait_ge(ln[w, "norm"], g)
                dve.tensor_scalar(st[:, 1, :], st[:, 0, :], 1.0 / CIN, None, ALU.mult).then_inc(ln[w, "mean"], 1)

            def ln_var(w, st, g):
                dve.wait_ge(ln[w, "square"], g + 1)
                dve.tensor_reduce(st[:, 2, :].rearrange("p (b j) -> p b j", j=2), sq[:, :, :, :], AX.X, ALU.add)\
                    .then_inc(ln[w, "sum2"], 1)
                dve.wait_ge(ln[w, "sum2"], g + 1)
                dve.tensor_scalar(st[:, 3, :], st[:, 2, :], 1.0 / CIN, LN_EPS, ALU.mult, ALU.add)\
                    .then_inc(ln[w, "var"], 1)

            def t_clip(g):
                for c in range(2):
                    b0, nb, w = chunk(c)
                    dve.wait_ge(ready["t"], 2 * g + c + 1)
                    dve.tensor_scalar(n.t2[:, g, b0:b0 + nb, :, 0:CIN],
                                      bank_of(f"t{c}", g)[:, 0:w].rearrange("p (b j c) -> p b j c", j=2, c=CIN),
                                      -1.0, 1.0, ALU.max, ALU.min).then_inc(taken["t"], 1)
                dve.wait_ge(taken["t"], 2 * g + 2)
                ln_mean("x", n.t2[:, g, :, :, 0:CIN], sx, g)

            def residual(g):
                for c in range(2):
                    b0, nb, w = chunk(c)
                    dve.wait_ge(ready["pr"], 2 * g + c + 1)
                    tt = n.t2[:, g, b0:b0 + nb, :, 0:CIN]
                    dve.tensor_tensor(tt, bank_of(f"pr{c}", g)[:, 0:w].rearrange("p (b j c) -> p b j c", j=2, c=CIN),
                                      tt, ALU.add).then_inc(taken["pr"], 1)
                dve.wait_ge(taken["pr"], 2 * g + 2)
                ln_mean("z", n.t2[:, g, :, :, 0:CIN], sz, g)

            def keys(g):
                b0, nb, w = chunk(0)
                dve.wait_ge(ready["k"], 2 * g + 1)
                src = spread(bank_of("k0", g)[:, 0:w], 1, HEADS)
                dve.tensor_tensor(kx[:, g % 2, :, b0 * P:b0 * P + w], src,
                                  spread(n.hmask[:, :], 2, w), ALU.mult).then_inc(taken["kd"], 1)

            step = [0]

            def link(ins):
                step[0] += 1
                ins.then_inc(r_step, 1)
                dve.wait_ge(r_step, step[0])

            def route_a(g):
                assert step[0] == R_STEPS * g
                L = lg[:, :, :]
                dve.wait_ge(ready["gate"], g + 1)
                dve.tensor_tensor(L, bank_of("gate", g)[:, 0:GT * E].rearrange("p (t e) -> p t e", e=E),
                                  spread(n.gate_b[:, :], 1, GT), ALU.add).then_inc(taken["gate"], 1)
                dve.wait_ge(taken["gate"], g + 1)

            def route_b(g):
                L = lg[:, :, :]
                top = rt[:, 0, :]
                link(dve.tensor_reduce(top, L, AX.X, ALU.max))
                link(dve.tensor_tensor(lw[:, 1, :, :], L, spread(top, 2, E), ALU.is_ge))
                link(dve.tensor_tensor(lw[:, 0, :, :], L, spread(top, 2, E), ALU.subtract))
                link(dve.tensor_tensor(lw[:, 1, :, :], lw[:, 1, :, :], spread(n.em8[:, :], 1, GT), ALU.mult))
                link(dve.tensor_reduce(rt[:, 1, :], lw[:, 1, :, :], AX.X, ALU.min))
                link(dve.tensor_tensor(ohf[:, :, :], spread(n.em8[:, :], 1, GT),
                                       spread(rt[:, 1, :], 2, E), ALU.is_equal))
                dve.tensor_copy(oh[:, :, :], ohf[:, :, :]).then_inc(rank_q, 1)
                dve.wait_ge(r_exp, g + 1)
                link(dve.tensor_reduce(rt[:, 2, :], lw[:, 0, :, :], AX.X, ALU.add))
                link(dve.reciprocal(n.t2[:, g, :, :, RP], rt[:, 2, :].rearrange("p (b j) -> p b j", j=2)))
                link(dve.tensor_copy(n.t2[:, g, :, :, RM], sz_keep(g, 0)))
                link(dve.tensor_copy(n.t2[:, g, :, :, RS], sz_keep(g, 1)))

            def route_c(g):
                dve.wait_ge(ready["rank"], g + 1)
                bank = bank_of("rank", g)

                def by_expert(a):
                    return a.rearrange("p (b j e) -> p e j b", b=NB, j=2)

                def ordered(a):
                    return a.rearrange("p e (j b) -> p e j b", j=2)
                link(dve.tensor_copy(flat4(cnt), by_expert(bank[:, GT * E:2 * GT * E])))
                link(dve.tensor_copy(sd[:, :, :], cnt[:, :, :]))
                link(dve.tensor_tensor(sd[:, :, 0], sd[:, :, 0], carry[:, :], ALU.add))
                link(dve.tensor_tensor_scan(inc[:, :, :].rearrange("p e t -> p (e t)"),
                                            notfirst[:, :, :].rearrange("p e t -> p (e t)"),
                                            sd[:, :, :].rearrange("p e t -> p (e t)"), 0.0, ALU.mult, ALU.add))
                link(dve.tensor_copy(carry[:, :], inc[:, :, GT - 1]))
                link(dve.tensor_tensor(cnt[:, :, :], inc[:, :, :], cnt[:, :, :], ALU.subtract))
                dve.tensor_tensor(flat4(sd), by_expert(bank[:, 0:GT * E]), flat4(cnt), ALU.add).then_inc(taken["rank"], 1)
                dve.wait_ge(taken["rank"], g + 1)
                link(dve.tensor_tensor(flat4(sd), flat4(sd), by_expert(ohf[:, :, :].rearrange("p t e -> p (t e)")), ALU.mult))
                link(dve.tensor_reduce(rt[:, 3, :], sd[:, :, :].rearrange("p e t -> p t e"), AX.X, ALU.add))
                link(dve.tensor_scalar(rt[:, 4, :], rt[:, 3, :], CAP - 0.5, NOWHERE, ALU.is_gt, ALU.mult))
                link(dve.tensor_tensor(rt[:, 4, :], rt[:, 4, :], rt[:, 3, :], ALU.add))
                link(dve.tensor_scalar(rt[:, 5, :], rt[:, 1, :], float(ES), float(E * ES), ALU.mult, ALU.add))
                if g >= 2:
                    dve.wait_ge(scat[g % 2], 16 * GT * (g // 2))
                dve.tensor_tensor(dest[:, g % 2, :, :], rt[:, 5, :].rearrange("p (b j) -> p b j", j=2),
                                  rt[:, 4, :].rearrange("p (j b) -> p b j", j=2), ALU.add).then_inc(ranked, 1)

            def flat4(t):
                return t[:, :, :].rearrange("p e (j b) -> p e j b", j=2)

            def sz_keep(g, k):
                return szk[:, g % 2, k, :].rearrange("p (b j) -> p b j", j=2)

            def keep(g):
                dve.wait_ge(ln["z", "rstd"], g + 1)
                dve.tensor_copy(szk[:, g % 2, 0, :], sz[:, 1, :]).then_inc(kept, 1)
                dve.tensor_copy(szk[:, g % 2, 1, :], sz[:, 4, :]).then_inc(kept, 1)

            def norm(B):
                g, b = divmod(B, NB)
                dve.wait_ge(o_ready, B + 1)
                if b == 0 and g >= 2:
                    dve.wait_ge(ready["ot"], 2 * (g - 1))
                o = O[B % 2][:, 0:8 * VW].rearrange("p (h v) -> p h v", v=VW)
                if B >= 2:
                    dve.wait_ge(o_done, B - 1)
                dve.reciprocal(rl[:, B % 2, :], o[:, :, HD]).then_inc(o_recip, 1)
                dve.wait_ge(o_recip, B + 1)
                dve.tensor_tensor(ob[:, g % 2, b, :, :], o[:, :, 0:HD], spread(rl[:, B % 2, :], 2, HD),
                                  ALU.mult).then_inc(o_done, 1)

            for i in BODIES:
                for s in range(NB):
                    B = i * NB + s
                    if 0 <= B < NBLK:
                        sc = S[B % 2][:, :].rearrange("p (h k) -> p h k", k=WIN)
                        dve.wait_ge(s_ready, B + 1)
                        if B >= 2:
                            dve.wait_ge(s_sub, B - 1)
                        dve.tensor_reduce(mx[:, B % 2, :], sc, AX.X, ALU.max).then_inc(s_max, 1)
                        if B >= 2:
                            dve.wait_ge(pt_ready, B - 1)
                        dve.wait_ge(s_max, B + 1)
                        dve.tensor_tensor(pb[:, B % 2, :, :, :].rearrange("p j h k -> p (j h) k"), sc,
                                          spread(mx[:, B % 2, :], 2, WIN), ALU.subtract).then_inc(s_sub, 1)
                    if 0 <= B - 2 < NBLK:
                        norm(B - 2)
                    if s == 0:
                        if has_r(i):
                            route_a(i - 2)
                        if has_x(i):
                            t_clip(i + 1)
                        if has_r(i):
                            route_b(i - 2)
                    if s == 1:
                        if has_r(i):
                            route_c(i - 2)
                    if s == 2 and has_x(i):
                        ln_var("x", sx, i + 1)
                    if s == 3 and has_z(i):
                        residual(i - 1)
                    if s == 4 and has_x(i):
                        keys(i + 1)
                    if s == 5 and has_z(i):
                        ln_var("z", sz, i - 1)
                    if s == 6 and has_z(i):
                        dve.wait_ge(ln["z", "rstd"], i)
                        keep(i - 1)

        @block.gpsimd
        def _(pool):
            pool.memset(vb[:, :, :, :, :, :, :], 0.0).then_inc(ids_step, 1)
            pool.iota(ids[:, :, :], [[P, NB], [GW, 2]], base=0, channel_multiplier=1,
                      allow_small_or_imprecise_dtypes=True).then_inc(ids_step, 1)
            pool.wait_ge(ids_step, 2)
            for hh in range(2):
                pool.memset(vb[64 * hh:64 * hh + 64, :, :, :, :, hh, HD:VW].rearrange("p w b j r o -> p (w b j r) o"),
                            1.0).then_inc(ids_step, 1)
            pool.wait_ge(ids_step, 4)
            for g in range(NG):
                pool.tensor_scalar(n.t2[:, g, :, :, RI], ids[:, :, :], float(g * GT * P), None, ALU.add).then_inc(ids_step, 1)

            pool.wait_ge(ids_step, 4 + NG)

            def center(w, g, dst, st):
                pool.wait_ge(ln[w, "mean"], g + 1)
                if w == "z":
                    pool.wait_ge(ready["xt"], 2 * min(g + 3, NG))
                elif g >= 3:
                    pool.wait_ge(ready["zt"], 2 * (g - 2))
                if w == "z" and g >= 1:
                    pool.wait_ge(ready["zt"], 2 * g)
                pool.tensor_tensor(dst[:, :, :, :], n.t2[:, g, :, :, 0:CIN],
                                   spread(st[:, 1, :].rearrange("p (b j) -> p b j", j=2), 3, CIN),
                                   ALU.subtract).then_inc(ln[w, "centered"], 1)

            def scale(w, g, dst, st):
                pool.wait_ge(ln[w, "var"], g + 1)
                if w == "z":
                    pool.wait_ge(kept, 2 * g)
                pool.tensor_tensor(st[:, 4, :], st[:, 3, :], n.mhalf[:, 0:GT], ALU.pow).then_inc(ln[w, "rstd"], 1)
                pool.wait_ge(ln[w, "rstd"], g + 1)
                pool.tensor_tensor(dst[:, :, :, :], dst[:, :, :, :],
                                   spread(st[:, 4, :].rearrange("p (b j) -> p b j", j=2), 3, CIN),
                                   ALU.mult).then_inc(ln[w, "norm"], 1)

            def scatter(g, lo, hi):
                if lo == 0:
                    pool.wait_ge(ranked, g + 1)
                for k in range(lo, hi):
                    b, j = divmod(k, 2)
                    pool.indirect_dma_start(n.slots, bass.IndirectOffsetOnAxis(ap=dest[:, g % 2, b, j:j + 1], axis=0),
                                            n.t2[:, g, b, j, :], None, bounds_check=SLOTS - 1,
                                            oob_is_err=False).then_inc(scat[g % 2], 16)

            for i in BODIES:
                for s in range(NB):
                    if s == 0 and has_x(i):
                        center("x", i + 1, xn, sx)
                    if s == 2 and has_x(i):
                        scale("x", i + 1, xn, sx)
                    if s == 3 and has_z(i):
                        center("z", i - 1, xn, sz)
                    if s == 5 and has_z(i):
                        scale("z", i - 1, xn, sz)
                    if has_r(i):
                        lo, hi = {1: (0, 2), 2: (2, 5), 3: (5, 8), 4: (8, 11), 5: (11, 12), 6: (12, 14)}.get(s, (0, 0))
                        scatter(i - 2, lo, hi)
            for q in range(2):
                pool.wait_ge(scat[q], 16 * GT * ((NG + 1 - q) // 2))


def expert_stage(nc, n):
    with ExitStack() as ctx:
        def sb(name, shape, dt=F32):
            return ctx.enter_context(nc.sbuf_tensor(name, shape, dt))

        def sem(name):
            return ctx.enter_context(nc.semaphore(name))

        PPE = TPE // 2
        NP = E * PPE
        RR, YR = 6, 3
        rows = sb("rows", [P, RR, 2, ROW])
        xe = sb("xe", [P, 2, 2, CIN])
        xeT = sb("xeT", [P, 2, P])
        idx = sb("idx", [P, YR, 2], I32)
        w1 = sb("w1", [P, 2, F])
        w2 = sb("w2", [P, 2, 2, CIN])
        b1 = sb("b1", [P, 2, 2])
        b2 = sb("b2", [CIN, 2])
        h = sb("h", [P, 2, 2, 2, P])
        yT = sb("yT", [CIN, 2, 2 * P])
        ye = sb("ye", [P, YR, 2, CIN])
        lim = sb("lim", [P, 2, CIN])
        bad = sb("bad", [P, 2, 2, CIN], I32)
        zero = sb("zero", [P, 2, CIN])
        yt = sb("yt", [P, 3, NB, 2, CIN])
        fin = sb("fin", [P, 2, NB, 2, CIN])
        out = sb("out", [P, 2, GW])
        A = [ctx.enter_context(nc.psum_tensor(f"A{i}", [P, 512], F32)) for i in range(2)]
        Hh = [[ctx.enter_context(nc.psum_tensor(f"H{i}{u}", [P, 512], F32)) for u in range(2)] for i in range(2)]
        Y = ctx.enter_context(nc.psum_tensor("Y", [P, 512], F32))
        Z = ctx.enter_context(nc.psum_tensor("Z", [P, 512], F32))

        row_in = [sem(f"row_in{k}") for k in range(RR)]
        w_in = [sem("ew_in0"), sem("ew_in1")]
        xe_done, xt_ready, xt_taken = sem("xe_done"), sem("xeT_ready"), sem("xeT_taken")
        h_ready, h_act, h_dve = sem("h_ready"), sem("h_act"), sem("h_dve")
        y_ready, y_taken, z_ready, z_step, y_full = sem("y_ready"), sem("y_taken"), sem("z_ready"), sem("z_step"), sem("y_full")
        idx_done, idx_zero = sem("idx_done"), sem("zeroed")
        sent = [sem(f"sent{k}") for k in range(YR)]
        all_sent = sem("all_sent")
        yt_in = [sem(f"yt_in{k}") for k in range(3)]
        summed, o_ready, o_taken = sem("summed"), sem("out_ready"), sem("out_taken")
        stored = [sem("stored0"), sem("stored1")]
        block = ctx.enter_context(nc.Block())
        Z_STEPS = 6

        def n_sent(k, upto):
            return 32 * len(range(k, upto, YR))

        n_out = [sum(len(pieces((2 * g + j) * GW, GW)) for j in range(2)) for g in range(NG)]

        @block.sync
        def _(sp):
            def weights(e):
                q = e % 2
                for u in range(2):
                    sp.dma_start(w1[64 * u:64 * u + 64, q, :], n.e_w1[e]).then_inc(w_in[q], 16)
                sp.dma_start(w2[:, q, :, :], n.e_w2[e].rearrange("(c f) d -> f c d", c=2)).then_inc(w_in[q], 16)
                sp.dma_start(b1[:, q, :], n.e_b1[e]).then_inc(w_in[q], 16)
                sp.dma_start(b2[:, q:q + 1], n.e_b2[e]).then_inc(w_in[q], 16)

            weights(0)
            for g in range(NP):
                e, k = divmod(g, PPE)
                if k == 2 and e + 1 < E:
                    if e >= 1:
                        sp.wait_ge(y_taken, e * PPE)
                        sp.wait_ge(h_dve, e * PPE)
                    weights(e + 1)
                if g >= RR:
                    sp.wait_ge(z_step, Z_STEPS * (g - RR) + 1)
                    sp.wait_ge(idx_done, g - RR + 1)
                sp.dma_start(rows[:, g % RR, :, :],
                             n.slots[g * 2 * P:(g + 1) * 2 * P, :].rearrange("(u p) d -> p u d", p=P)
                             ).then_inc(row_in[g % RR], 16)
            for k in range(YR):
                sp.wait_ge(sent[k], n_sent(k, NP))

            def load(g):
                if g >= 3:
                    sp.wait_ge(summed, g - 2)
                for j in range(2):
                    sp.dma_start(yt[:, g % 3, :, j, :],
                                 n.y_tok[(2 * g + j) * GW:(2 * g + j + 1) * GW, :].rearrange("(b p) d -> p b d", p=P)
                                 ).then_inc(yt_in[g % 3], 16)

            load(0)
            load(1)
            for g in range(NG):
                if g + 2 < NG:
                    load(g + 2)
                sp.wait_ge(o_taken, 2 * g + 2)
                for j in range(2):
                    for image, pixel, at, m in pieces((2 * g + j) * GW, GW):
                        sp.dma_start(n.out[image, :, pixel:pixel + m],
                                     out[64 * j:64 * j + 64, g % 2, at:at + m]).then_inc(stored[g % 2], 16)
            for q in range(2):
                sp.wait_ge(stored[q], 16 * sum(n_out[q::2]))

        @block.tensor
        def _(pe):
            def turn(g):
                pe.wait_ge(xe_done, 2 * g + 2)
                if g >= 2:
                    pe.wait_ge(xt_taken, g - 1)
                pe.transpose(A[g % 2][:, 0:P], xe[:, g % 2, :, :].rearrange("p u c -> p (u c)"), n.ident[:, :])\
                    .then_inc(xt_ready, 1)

            def first(g):
                q = (g // PPE) % 2
                if g % PPE == 0:
                    pe.wait_ge(w_in[q], 80 * (g // PPE // 2 + 1))
                pe.wait_ge(xt_taken, g + 1)
                if g >= 2:
                    pe.wait_ge(h_act, g - 1)
                    pe.wait_ge(h_dve, g - 1)
                for u in range(2):
                    for c in range(2):
                        mm = pe.matmul(Hh[g % 2][u][:, c * P:(c + 1) * P], w1[64 * u:64 * u + 64, q, c * P:(c + 1) * P],
                                       xeT[64 * u:64 * u + 64, g % 2, :], start=True, stop=True)
                mm.then_inc(h_ready, 1)

            def second(g):
                q = (g // PPE) % 2
                pe.wait_ge(h_act, g + 1)
                pe.wait_ge(h_dve, g + 1)
                if g >= 1:
                    pe.wait_ge(y_taken, g)
                for c in range(2):
                    mm = pe.matmul(Y[0:CIN, 0:2 * P], w2[:, q, c, :], h[:, g % 2, :, c, :],
                                   start=(c == 0), stop=(c == 1))
                mm.then_inc(y_ready, 1)

            def back(g):
                pe.wait_ge(y_taken, g + 1)
                if g >= 1:
                    pe.wait_ge(z_step, Z_STEPS * (g - 1) + 1)
                for u in range(2):
                    mm = pe.transpose(Z[:, u * CIN:(u + 1) * CIN], yT[:, g % 2, u * P:(u + 1) * P],
                                      n.ident[0:CIN, 0:CIN])
                mm.then_inc(z_ready, 1)

            for k in range(-2, NP + 1):
                if k + 2 < NP:
                    turn(k + 2)
                if 0 <= k + 1 < NP:
                    first(k + 1)
                if 0 <= k < NP:
                    second(k)
                if 0 <= k - 1:
                    back(k - 1)
            for g in range(NG):
                pe.wait_ge(summed, g + 1)
                for c, (b0, nb) in enumerate(CHUNKS):
                    if g >= 1:
                        pe.wait_ge(o_taken, 2 * g - 1 + c)
                    for b in range(nb):
                        mm = pe.transpose(A[c][:, b * P:(b + 1) * P],
                                          fin[:, g % 2, b0 + b, :, :].rearrange("p j c -> p (j c)"), n.ident[:, :])
                    mm.then_inc(o_ready, 1)

        @block.scalar
        def _(act):
            for k in range(-2, NP):
                if k + 2 < NP:
                    g = k + 2
                    act.wait_ge(xt_ready, g + 1)
                    if g >= 2:
                        act.wait_ge(h_ready, g - 1)
                    act.activation(xeT[:, g % 2, :], A[g % 2][:, 0:P], ACT.Copy).then_inc(xt_taken, 1)
                if 0 <= k + 1 < NP:
                    g = k + 1
                    q = (g // PPE) % 2
                    act.wait_ge(h_ready, g + 1)
                    if g >= 2:
                        act.wait_ge(y_ready, g - 1)
                    for c in range(2):
                        ins = act.activation(h[:, g % 2, 0, c, :], Hh[g % 2][0][:, c * P:(c + 1) * P], ACT.Relu,
                                             bias=b1[:, q, c:c + 1])
                    ins.then_inc(h_act, 1)
                if 0 <= k:
                    q = (k // PPE) % 2
                    act.wait_ge(y_ready, k + 1)
                    if k >= 2:
                        act.wait_ge(z_ready, k - 1)
                    act.activation(yT[:, k % 2, :], Y[0:CIN, 0:2 * P], ACT.Identity,
                                   bias=b2[:, q:q + 1]).then_inc(y_taken, 1)
            for g in range(NG):
                for c, (b0, nb) in enumerate(CHUNKS):
                    act.wait_ge(o_ready, 2 * g + c + 1)
                    if g >= 2 and c == 0:
                        act.wait_ge(stored[g % 2], 16 * sum(n_out[g % 2:g:2]))
                    act.activation(out[:, g % 2, b0 * P:(b0 + nb) * P], A[c][:, 0:nb * P], ACT.Copy).then_inc(o_taken, 1)

        @block.vector
        def _(dve):
            dve.memset(zero[:, :, :], 0.0).then_inc(idx_zero, 1)
            dve.wait_ge(idx_zero, 1)
            step = [0]

            def link(ins):
                step[0] += 1
                ins.then_inc(z_step, 1)
                dve.wait_ge(z_step, step[0])

            for k in range(-2, NP + 1):
                if k + 2 < NP:
                    g = k + 2
                    dve.wait_ge(row_in[g % RR], 16 * (g // RR + 1))
                    if g >= 2:
                        dve.wait_ge(xt_ready, g - 1)
                    for u in range(2):
                        r = rows[:, g % RR, u, :]
                        dve.tensor_scalar(xe[:, g % 2, u, :], r[:, 0:CIN], r[:, RM:RM + 1], r[:, RS:RS + 1],
                                          ALU.subtract, ALU.mult).then_inc(xe_done, 1)
                if 0 <= k + 1 < NP:
                    g = k + 1
                    q = (g // PPE) % 2
                    dve.wait_ge(h_ready, g + 1)
                    if g >= 2:
                        dve.wait_ge(y_ready, g - 1)
                    for c in range(2):
                        ins = dve.tensor_scalar(h[:, g % 2, 1, c, :], Hh[g % 2][1][:, c * P:(c + 1) * P],
                                                b1[:, q, c:c + 1], 0.0, ALU.add, ALU.max)
                    ins.then_inc(h_dve, 1)
                if 0 <= k - 1:
                    g = k - 1
                    r = rows[:, g % RR, :, :]
                    yy = ye[:, g % YR, :, :]
                    if g >= YR:
                        dve.wait_ge(sent[g % YR], n_sent(g % YR, g))
                    dve.tensor_copy(idx[:, g % YR, :], r[:, :, RI]).then_inc(idx_done, 1)
                    dve.wait_ge(z_ready, g + 1)
                    link(dve.tensor_tensor(yy, Z[:, 0:2 * CIN].rearrange("p (u c) -> p u c", u=2),
                                           spread(r[:, :, RP], 2, CIN), ALU.mult))
                    link(dve.tensor_scalar(lim[:, :, :], yy, -FLT_MAX, FLT_MAX, ALU.max, ALU.min))
                    link(dve.tensor_tensor(bad[:, 0, :, :], yy, lim[:, :, :], ALU.not_equal))
                    link(dve.tensor_scalar(lim[:, :, :], yy, -1e4, 1e4, ALU.max, ALU.min))
                    link(dve.tensor_tensor(bad[:, 1, :, :], yy, yy, ALU.not_equal))
                    link(dve.copy_predicated(yy, bad[:, 0, :, :], lim[:, :, :]))
                    dve.copy_predicated(yy, bad[:, 1, :, :], zero[:, :, :]).then_inc(y_full, 1)
            for g in range(NG):
                dve.wait_ge(yt_in[g % 3], 32 * (g // 3 + 1))
                if g >= 2:
                    dve.wait_ge(o_ready, 2 * (g - 1))
                dve.tensor_tensor(fin[:, g % 2, :, :, :], n.t2[:, g, :, :, 0:CIN], yt[:, g % 3, :, :, :],
                                  ALU.add).then_inc(summed, 1)

        @block.gpsimd
        def _(pool):
            for g in range(NP):
                pool.wait_ge(y_full, g + 1)
                pool.wait_ge(idx_done, g + 1)
                for u in range(2):
                    pool.indirect_dma_start(n.y_tok, bass.IndirectOffsetOnAxis(ap=idx[:, g % YR, u:u + 1], axis=0),
                                            ye[:, g % YR, u, :], None, bounds_check=TOK - 1,
                                            oob_is_err=False).then_inc(sent[g % YR], 16)
            for k in range(YR):
                pool.wait_ge(sent[k], n_sent(k, NP))


def kernel(x, L0_conv_w1, L0_conv_w2, L0_conv_w3, L0_conv_g1, L0_conv_b1, L0_conv_g2, L0_conv_b2, L0_conv_g3,
           L0_conv_b3, L1_attn_Wqkv, L1_attn_Wproj, L1_attn_bproj, L1_ffn_gate_w, L1_ffn_gate_b, L1_ffn_w1,
           L1_ffn_b1, L1_ffn_w2, L1_ffn_b2):
    import numpy as _np
    import concourse.bacc as _bacc
    from concourse import mybir as _mybir
    from concourse.bass_utils import run_bass_kernel_spmd as _run

    a = _np.asarray
    arrays = {
        "x": a(x).reshape(NIMG, CIN, PIX),
        "w1": a(L0_conv_w1).reshape(CB, CIN).T,
        "w2": a(L0_conv_w2).transpose(1, 2, 3, 0).reshape(CB, 9, CB),
        "w3": a(L0_conv_w3).reshape(CIN, CB).T,
        "gb12": _np.stack([a(v).reshape(CB) for v in (L0_conv_g1, L0_conv_b1, L0_conv_g2, L0_conv_b2)], 1),
        "g3": a(L0_conv_g3).reshape(1, CIN),
        "b3": a(L0_conv_b3).reshape(1, CIN),
        "w_qkv": a(L1_attn_Wqkv),
        "w_proj": a(L1_attn_Wproj),
        "b_proj": a(L1_attn_bproj).reshape(1, CIN),
        "gate_w": a(L1_ffn_gate_w),
        "gate_bias": a(L1_ffn_gate_b).reshape(1, E),
        "e_w1": a(L1_ffn_w1),
        "e_b1": a(L1_ffn_b1).reshape(E, 2, P).transpose(0, 2, 1),
        "e_w2": a(L1_ffn_w2),
        "e_b2": a(L1_ffn_b2).reshape(E, CIN, 1),
    }
    arrays = {k: _np.ascontiguousarray(v) for k, v in arrays.items()}
    nc = _bacc.Bacc("TRN2", target_bir_lowering=False, num_devices=1)
    aps = {k: nc.dram_tensor(f"in_{k}", v.shape, _mybir.dt.from_np(v.dtype), kind="ExternalInput").ap()
           for k, v in arrays.items()}
    aps["out"] = nc.dram_tensor("out_0", (NIMG, CIN, PIX), F32, kind="ExternalOutput").ap()
    build(nc, aps)
    r = _run(nc, [{f"in_{k}": v for k, v in arrays.items()}], core_ids=[0])
    return r.results[0]["out_0"].reshape(NIMG, CIN, H, W)
```

```python
from contextlib import ExitStack

import concourse.bass as bass
from concourse import mybir

ALU = mybir.AluOpType
ACT = mybir.ActivationFunctionType
AX = mybir.AxisListType
F32 = mybir.dt.float32
BF16 = mybir.dt.bfloat16
F16 = mybir.dt.float16
I32 = mybir.dt.int32

P = 128
NIMG, CIN, H, W = 16, 64, 56, 56
PIX = H * W
TOK = NIMG * PIX
CB = 16
NQ = 4
HC = 448
RPC = HC // W
NCH = 2 * PIX // HC
HEADS, HD, WIN, RADIUS = 4, 16, 64, 32
SCALE = HD ** -0.5
NEG = -1e30
VW = HD + 1
NB = 7
GT = 2 * NB
GW = NB * P
NG = TOK // (GT * P)
E, F = 8, 256
CAP = -(-5 * TOK // (4 * E))
TPE = -(-CAP // (2 * P)) * 2
ES = TPE * P
SLOTS = E * ES
NOWHERE = 1048576.0
ROW = CIN + 2
RP, RI = CIN, CIN + 1
CHUNKS = ((0, 4), (4, 3))
BN_EPS = LN_EPS = 1e-5


def pieces(start, length):
    out, at = [], 0
    while at < length:
        image, pixel = divmod(start + at, PIX)
        n = min(length - at, PIX - pixel)
        out.append((image, pixel, at, n))
        at += n
    return out


def spread(a, axis, count):
    a = a.unsqueeze(axis)
    shape = list(a.shape)
    shape[axis] = count
    return a.broadcast_to(shape)


ARRAYS = ("x", "w1", "w2", "w3", "gb12", "g3", "b3", "w_qkv", "w_proj", "b_proj", "gate_w", "gate_bias",
          "e_w1", "e_b1", "e_w2", "e_b2", "out")


class Net:

    def __init__(self, a):
        (self.x, self.w1, self.w2, self.w3, self.gb12, self.g3, self.b3, self.w_qkv, self.w_proj, self.b_proj,
         self.gate_w, self.gate_bias, self.e_w1, self.e_b1, self.e_w2, self.e_b2, self.out) = (a[k] for k in ARRAYS)


def conv_stage(nc, n):
    with ExitStack() as ctx:
        def sb(name, shape, dt=F32):
            return ctx.enter_context(nc.sbuf_tensor(name, shape, dt))

        def sem(name):
            return ctx.enter_context(nc.semaphore(name))

        XR = 3
        xc = sb("xc", [P, XR, NQ, HC])
        xs = sb("xs", [P, 2, NQ, HC], BF16)
        y = sb("y", [P, NCH, HC], BF16)
        sp_ = sb("signs_padded", [P, 2, H + 2, W + 2], BF16)
        s2 = sb("s2", [P, NCH * HC], BF16)
        s2T = sb("s2T", [P, 2, NB, P], BF16)
        w1f = sb("w1f", [P, 32])
        w1s = sb("w1s", [P, 32], BF16)
        w2f = sb("w2f", [P, 9, P])
        w2s = sb("w2s", [P, 9, P], BF16)
        w3f = sb("w3f", [P, CIN])
        w3s = sb("w3s", [P, CIN])
        gb = sb("gb", [P, 4])
        gb3 = sb("gb3", [P, 2, CIN])
        same = sb("same_channel", [P, P])
        pi = sb("pi", [P, P])
        pj = sb("pj", [P, 1])
        blk = sb("same_group", [P, P])
        st = sb("st", [P, NCH, 6])
        agg = sb("agg", [P, 2])
        mom = sb("mom", [P, 2])
        mv = sb("mv", [P, 6])
        ab = sb("ab", [P, 2])
        s2sum = sb("s2sum", [P, NCH])
        s2tot = sb("s2tot", [P, 1])
        gram = sb("gram", [P, P])
        t1 = sb("t1", [P, CIN])
        t3 = sb("t3", [P, CIN])
        row = sb("row", [P, 8, CIN])
        ones = sb("ones", [P, P])
        junk = sb("empty_rows", [P, 16, ROW])
        zero = sb("zero_rows", [P, 16, CIN])
        c1 = sb("c1", [P, 3, P])
        pmod = sb("pmod", [P, 1])
        ps = [ctx.enter_context(nc.psum_tensor(f"cps{i}", [P, 512], F32)) for i in range(4)]
        psT = [ctx.enter_context(nc.psum_tensor(f"cpt{i}", [P, NB * P], BF16)) for i in range(2)]
        psG = ctx.enter_context(nc.psum_tensor("cpg", [P, 512], F32))
        psS = ctx.enter_context(nc.psum_tensor("cpsm", [P, 512], F32))

        xin = [sem(f"x_in{i}") for i in range(XR)]
        w_in, zeroed, iot, cst = sem("w_in"), sem("w_zeroed"), sem("iota_done"), sem("consts")
        w_signs, x_signs, conv_done, y_done = sem("w_signs"), sem("x_signs"), sem("conv_done"), sem("y_done")
        bn_step, bn_pow, bn_mm, act_sign = sem("bn_step"), sem("bn_pow"), sem("bn_mm"), sem("act_sign")
        tr, trc, gdone, s2_out, init = sem("s2_transposed"), sem("s2T_done"), sem("gram_done"), sem("s2_out"), sem("init")
        pconst = sem("pool_const")
        tail = sem("tail")
        block = ctx.enter_context(nc.Block())

        @block.sync
        def _(sp):
            for c in range(NCH):
                if c >= XR:
                    sp.wait_ge(x_signs, c - XR + 1)
                image, pixel = divmod(c * HC, PIX)
                for j in range(2):
                    sp.dma_start(xc[64 * j:64 * j + 64, c % XR, :, :],
                                 n.x.rearrange("(q j i) c p -> j i c q p", q=NQ, j=2)[j, image, :, :, pixel:pixel + HC]
                                 ).then_inc(xin[c % XR], 16)
                if c == 1:
                    sp.wait_ge(zeroed, 2)
                    for j in range(2):
                        sp.dma_start(w1f[64 * j:64 * j + 64, 16 * j:16 * j + 16], n.w1).then_inc(w_in, 16)
                    for g in range(8):
                        r = slice(16 * g, 16 * g + 16)
                        sp.dma_start(w2f[r, :, r], n.w2).then_inc(w_in, 16)
                        sp.dma_start(w3f[r, :], n.w3).then_inc(w_in, 16)
                        sp.dma_start(gb[r, :], n.gb12).then_inc(w_in, 16)
                    sp.dma_start(gb3[:, 0, :], n.g3.broadcast_to([P, n.g3.shape[1]])).then_inc(w_in, 16)
                    sp.dma_start(gb3[:, 1, :], n.b3.broadcast_to([P, n.b3.shape[1]])).then_inc(w_in, 16)
            sp.wait_ge(pconst, 5)
            for k in range(SLOTS // (P * 16)):
                sp.dma_start(n.slots[k * P * 16:(k + 1) * P * 16, :].rearrange("(p r) d -> p (r d)", p=P),
                             junk[:, :, :].rearrange("p r d -> p (r d)")).then_inc(init, 16)
            rows, k = P * 16, 0
            while k < TOK:
                m = min(rows, TOK - k) // P
                sp.dma_start(n.y_tok[k:k + m * P, :].rearrange("(p r) d -> p (r d)", p=P),
                             zero[:, 0:m, :].rearrange("p r d -> p (r d)")).then_inc(init, 16)
                k += m * P
            n_init = SLOTS // rows + -(-TOK // rows)
            for q in range(2):
                sp.wait_ge(act_sign, 2 + 7 * (q + 1))
                w = slice(q * PIX, (q + 1) * PIX)
                for i in range(8):
                    sp.dma_start(n.s2_dram[2 * i + q, :, :], s2[16 * i:16 * i + 16, w]).then_inc(s2_out, 16)
            sp.wait_ge(s2_out, 16 * 16)
            sp.wait_ge(init, 16 * n_init)

        @block.gpsimd
        def _(pool):
            pool.memset(w2f[:, :, :], 0.0).then_inc(zeroed, 1)
            pool.memset(w1f[:, :], 0.0).then_inc(zeroed, 1)
            pool.memset(junk[:, :, :], 0.0).then_inc(pconst, 1)
            pool.memset(zero[:, :, :], 0.0).then_inc(pconst, 1)
            pool.memset(sp_[:, :, :, :], 0.0).then_inc(pconst, 1)
            pool.wait_ge(pconst, 3)
            pool.memset(junk[:, :, RI:RI + 1], NOWHERE).then_inc(pconst, 1)
            pool.memset(ones[:, :], 1.0).then_inc(pconst, 1)
            pool.iota(c1[:, 0, :], [[0, 8], [1, 16]], base=0, channel_multiplier=0,
                      allow_small_or_imprecise_dtypes=True).then_inc(iot, 1)
            pool.iota(c1[:, 1, :], [[1, 8], [0, 16]], base=0, channel_multiplier=0,
                      allow_small_or_imprecise_dtypes=True).then_inc(iot, 1)
            pool.iota(pj[:, :], [[0, 1]], base=0, channel_multiplier=1,
                      allow_small_or_imprecise_dtypes=True).then_inc(iot, 1)
            for k in range(3):
                pool.wait_ge(bn_step, (4, 10, 19)[k])
                if k < 2:
                    pool.tensor_tensor(mv[:, 3:4], mv[:, 2:3], n.mhalf[:, 0:1], ALU.pow).then_inc(bn_pow, 1)
                else:
                    pool.tensor_tensor(row[:, 3, :], row[:, 2, :], n.mhalf[:, 0:CIN], ALU.pow).then_inc(bn_pow, 1)

        @block.tensor
        def _(pe):
            pe.wait_ge(w_signs, 1)
            for c in range(NCH):
                pe.wait_ge(x_signs, c + 1)
                if c >= 2:
                    pe.wait_ge(y_done, c - 1)
                for q in range(NQ):
                    mm = pe.matmul(ps[c % 2][32 * q:32 * q + 32, 0:HC], w1s[:, :], xs[:, c % 2, q, :],
                                   start=True, stop=True)
                mm.then_inc(conv_done, 1)
            pe.wait_ge(cst, 2)
            pe.wait_ge(bn_step, 2)
            pe.matmul(psS[:, 0:2], same[:, :], mom[:, :], start=True, stop=True).then_inc(bn_mm, 1)
            pe.wait_ge(w_signs, 2)
            for c in range(NCH):
                pe.wait_ge(act_sign, 1 + (1 if c < 7 else 2) - 1)
                pe.wait_ge(y_done, NCH + max(c - 1, 0))
                for k in range(9):
                    dy, dx = divmod(k, 3)
                    i, r = divmod(c * RPC, H)
                    mm = pe.matmul(ps[c % 2][:, 0:HC], w2s[:, k, :], sp_[:, i, r + dy:r + dy + RPC, dx:dx + W],
                                   start=(k == 0), stop=(k == 8))
                mm.then_inc(conv_done, 1)
            pe.wait_ge(bn_step, 8)
            pe.matmul(psS[:, 2:4], same[:, :], mom[:, :], start=True, stop=True).then_inc(bn_mm, 1)

            def transposes(g):
                pe.wait_ge(act_sign, 2 + 2 * g + 2)
                if g >= 2:
                    pe.wait_ge(trc, g - 1)
                for b in range(NB):
                    mm = pe.transpose(psT[g % 2][:, b * P:(b + 1) * P], s2[:, (g * NB + b) * P:(g * NB + b + 1) * P],
                                      n.ident_b[:, :])
                mm.then_inc(tr, 1)

            transposes(0)
            for g in range(NB):
                if g + 1 < NB:
                    transposes(g + 1)
                pe.wait_ge(trc, g + 1)
                for b in range(NB):
                    mm = pe.matmul(psG[:, 0:P], s2T[:, g % 2, b, :], s2T[:, g % 2, b, :],
                                   start=(g == 0 and b == 0), stop=(g == NB - 1 and b == NB - 1))
                mm.then_inc(gdone, 1)
            pe.wait_ge(bn_step, 13)
            pe.matmul(psS[:, 64:128], gram[:, :], w3s[:, :], start=True, stop=True).then_inc(bn_mm, 1)
            pe.wait_ge(bn_step, 15)
            pe.matmul(psS[:, 128:192], ones[:, :], t1[:, :], start=True, stop=True)
            pe.matmul(psS[:, 192:256], ones[:, :], t3[:, :], start=True, stop=True).then_inc(bn_mm, 1)

        @block.scalar
        def _(act):
            act.wait_ge(w_in, 16 * 28)
            act.activation(w1s[:, :], w1f[:, :], ACT.Sign).then_inc(w_signs, 1)
            act.activation(w2s[:, :, :], w2f[:, :, :], ACT.Sign).then_inc(w_signs, 1)
            act.activation(w3s[:, :], w3f[:, :], ACT.Sign).then_inc(w_signs, 1)
            for c in range(NCH):
                act.wait_ge(xin[c % XR], 32 * (c // XR + 1))
                if c >= 2:
                    act.wait_ge(conv_done, c - 1)
                act.activation(xs[:, c % 2, :, :], xc[:, c % XR, :, :], ACT.Sign).then_inc(x_signs, 1)
            act.wait_ge(pconst, 3)
            act.wait_ge(bn_step, 6)
            for i in range(2):
                act.activation(sp_[:, i, 1:H + 1, 1:W + 1],
                               y[:, 7 * i:7 * i + 7, :].rearrange("p c (r w) -> p (c r) w", w=W),
                               ACT.Sign, bias=ab[:, 1:2], scale=ab[:, 0:1]).then_inc(act_sign, 1)
            act.wait_ge(bn_step, 12)
            for c in range(NCH):
                act.activation(s2[:, c * HC:(c + 1) * HC], y[:, c, :], ACT.Sign, bias=ab[:, 1:2], scale=ab[:, 0:1],
                               accum_out=s2sum[:, c:c + 1]).then_inc(act_sign, 1)

        @block.vector
        def _(dve):
            step = [0]

            def link(ins):
                step[0] += 1
                ins.then_inc(bn_step, 1)
                dve.wait_ge(bn_step, step[0])

            dve.wait_ge(iot, 3)
            k = [0]

            def local(ins):
                k[0] += 1
                ins.then_inc(tail, 1)
                dve.wait_ge(tail, k[0])

            local(dve.tensor_scalar(blk[:, :], c1[:, 1, :], 16.0, None, ALU.mult))
            local(dve.tensor_scalar(pi[:, :], blk[:, :], pj[:, 0:1], -1.0, ALU.subtract, ALU.mult))
            local(dve.tensor_scalar(blk[:, :], pi[:, :], 15.5, None, ALU.is_lt))
            local(dve.scalar_tensor_tensor(blk[:, :], pi[:, :], -0.5, blk[:, :], ALU.is_gt, ALU.mult))
            local(dve.tensor_tensor(pi[:, :], pi[:, :], blk[:, :], ALU.mult))
            local(dve.tensor_reduce(pmod[:, :], pi[:, :], AX.X, ALU.add))
            local(dve.tensor_scalar(pmod[:, :], pmod[:, :], 1.0 / 16, None, ALU.mult))
            dve.tensor_scalar(same[:, :], c1[:, 0, :], pmod[:, 0:1], 0.125, ALU.is_equal, ALU.mult).then_inc(cst, 1)
            dve.memset(t1[:, :], 0.0).then_inc(cst, 1)

            for conv in range(2):
                for c in range(NCH):
                    dve.wait_ge(conv_done, NCH * conv + c + 1)
                    if conv and c == 0:
                        dve.wait_ge(act_sign, 2)
                    dve.bn_stats(st[:, c, :], ps[c % 2][:, 0:HC]).then_inc(tail, 1)
                    dve.tensor_copy(y[:, c, :], ps[c % 2][:, 0:HC]).then_inc(y_done, 1)
                k[0] += NCH
                dve.wait_ge(tail, k[0])
                link(dve.bn_aggr(agg[:, :], st[:, :, :]))
                local(dve.tensor_tensor(mv[:, 5:6], agg[:, 0:1], agg[:, 0:1], ALU.mult))
                local(dve.tensor_copy(mom[:, 0:1], agg[:, 0:1]))
                link(dve.tensor_tensor(mom[:, 1:2], agg[:, 1:2], mv[:, 5:6], ALU.add))
                dve.wait_ge(bn_mm, conv + 1)
                local(dve.tensor_copy(mv[:, 0:2], psS[:, 2 * conv:2 * conv + 2]))
                local(dve.tensor_tensor(mv[:, 4:5], mv[:, 0:1], mv[:, 0:1], ALU.mult))
                link(dve.tensor_tensor(mv[:, 2:3], mv[:, 1:2], mv[:, 4:5], ALU.subtract))
                link(dve.tensor_scalar(mv[:, 2:3], mv[:, 2:3], BN_EPS, None, ALU.add))
                dve.wait_ge(bn_pow, conv + 1)
                if conv:
                    dve.wait_ge(act_sign, 2)
                link(dve.tensor_tensor(ab[:, 0:1], mv[:, 3:4], gb[:, 2 * conv:2 * conv + 1], ALU.mult))
                local(dve.tensor_tensor(mv[:, 5:6], ab[:, 0:1], mv[:, 0:1], ALU.mult))
                link(dve.tensor_tensor(ab[:, 1:2], gb[:, 2 * conv + 1:2 * conv + 2], mv[:, 5:6], ALU.subtract))
            for g in range(NB):
                dve.wait_ge(tr, g + 1)
                if g >= 2:
                    dve.wait_ge(gdone, g - 1)
                dve.tensor_copy(s2T[:, g % 2, :, :].rearrange("p b t -> p (b t)"), psT[g % 2][:, :]).then_inc(trc, 1)
            dve.wait_ge(gdone, NB)
            dve.wait_ge(w_signs, 3)
            dve.wait_ge(act_sign, 2 + NCH)
            local(dve.tensor_reduce(s2tot[:, :], s2sum[:, :], AX.X, ALU.add))
            link(dve.tensor_tensor(gram[:, :], psG[:, 0:P], blk[:, :], ALU.mult))
            dve.wait_ge(bn_mm, 3)
            link(dve.tensor_tensor(t1[:, :], psS[:, 64:128], w3s[:, :], ALU.mult))
            link(dve.tensor_scalar(t3[:, :], w3s[:, :], s2tot[:, 0:1], None, ALU.mult))
            dve.wait_ge(bn_mm, 4)
            link(dve.tensor_scalar(row[:, 0, :], psS[:, 192:256], 1.0 / TOK, None, ALU.mult))
            link(dve.tensor_tensor(row[:, 1, :], row[:, 0, :], row[:, 0, :], ALU.mult))
            link(dve.scalar_tensor_tensor(row[:, 2, :], psS[:, 128:192], 1.0 / TOK, row[:, 1, :],
                                          ALU.mult, ALU.subtract))
            link(dve.tensor_scalar(row[:, 2, :], row[:, 2, :], BN_EPS, None, ALU.add))
            dve.wait_ge(bn_pow, 3)
            link(dve.tensor_tensor(row[:, 4, :], row[:, 3, :], gb3[:, 0, :], ALU.mult))
            link(dve.tensor_tensor(row[:, 5, :], row[:, 4, :], row[:, 0, :], ALU.mult))
            link(dve.tensor_tensor(row[:, 5, :], gb3[:, 1, :], row[:, 5, :], ALU.subtract))
            link(dve.tensor_tensor(row[:, 6, :], w3s[:, :], row[:, 4, :], ALU.mult))
            link(dve.tensor_scalar(row[:, 6, :], row[:, 6, :], n.pcol[:, 2:3], None, ALU.mult))
            link(dve.scalar_tensor_tensor(row[:, 6, :], row[:, 5, :], n.pcol[:, 3:4], row[:, 6, :], ALU.mult, ALU.add))
            for part in range(3):
                for j in range(2):
                    link(dve.tensor_scalar(n.w3p[:, part, CIN * j:CIN * j + CIN], row[0:33, 6, :],
                                           n.pcol[0:33, j:j + 1], None, ALU.mult))
                link(dve.tensor_copy(row[:, 7, :], row[:, 6, :]))
                link(dve.tensor_copy(n.part_b[:, :], row[:, 7, :]))
                link(dve.tensor_tensor(row[:, 6, :], row[:, 7, :], n.part_b[:, :], ALU.subtract))


def build(nc, a):
    with ExitStack() as ctx:
        def sb(name, shape, dt=F32):
            return ctx.enter_context(nc.sbuf_tensor(name, shape, dt))

        def sem(name):
            return ctx.enter_context(nc.semaphore(name))

        n = Net(a)
        n.slots = nc.dram_tensor("slots", (SLOTS, ROW), F32, kind="Internal").ap()
        n.y_tok = nc.dram_tensor("y_tok", (TOK, CIN), F32, kind="Internal").ap()
        n.s2_dram = nc.dram_tensor("s2_dram", (NIMG, CB, PIX), BF16, kind="Internal").ap()
        n.ident = sb("ident", [P, P])
        n.ident_b = sb("ident_b", [P, P], BF16)
        n.ident_h = sb("ident_h", [P, P], F16)
        n.mhalf = sb("minus_half", [P, CIN])
        n.pcol = sb("pcol", [P, 4])
        n.w3p = sb("w3p", [33, 3, P], BF16)
        n.part_b = sb("part_b", [P, CIN], BF16)
        n.mask = sb("mask", [P, 2, HEADS, WIN], BF16)
        n.hmask = sb("hmask", [P, HEADS])
        n.jmask = sb("jmask", [P, 2])
        n.wqkv = sb("wqkv", [P, 3, P])
        n.wp = sb("wp", [P, P])
        n.gate = sb("gate", [P, 2 * E])
        n.bp = sb("bp", [3, 4 * P], BF16)
        n.ones3 = sb("ones3", [3, P], BF16)
        n.gate_b = sb("gate_b", [P, E])
        n.tri = sb("tri", [P, P], BF16)
        n.ones_b = sb("ones_b", [P, P], BF16)
        n.em8 = sb("em8", [P, E])
        n.t2 = sb("t2", [P, NG, NB, 2, CIN])
        const_stage(nc, n)
        conv_stage(nc, n)
        attention_stage(nc, n)
        expert_stage(nc, n)


def const_stage(nc, n):
    with ExitStack() as ctx:
        def sb(name, shape, dt=F32):
            return ctx.enter_context(nc.sbuf_tensor(name, shape, dt))

        def sem(name):
            return ctx.enter_context(nc.semaphore(name))

        brow = sb("brow", [1, 2, P])
        bpart = sb("bpart", [1, 3, 4, P], BF16)
        z, s, dz, w_in, d, moved = sem("k_memsets"), sem("k_selects"), sem("k_zeroed"), sem("k_weights"), sem("k_dve"), sem("k_moved")
        block = ctx.enter_context(nc.Block())

        @block.vector
        def _(dve):
            for t in (n.wqkv[:, :, :], n.wp[:, :], n.gate[:, :]):
                dve.memset(t, 0.0).then_inc(dz, 1)
            dve.memset(n.ones3[:, :], 1.0).then_inc(dz, 1)
            dve.wait_ge(w_in, 16 * 12)
            k = 0
            for part in range(3):
                ins = dve.tensor_copy(bpart[:, part, 0, :], brow[:, 0, :])
                k += 1
                ins.then_inc(d, 1)
                dve.wait_ge(d, k)
                for r in range(1, 4):
                    dve.tensor_copy(bpart[:, part, r, :], bpart[:, part, 0, :]).then_inc(d, 1)
                k += 3
                dve.tensor_tensor(brow[:, 1, :], brow[:, 0, :], bpart[:, part, 0, :], ALU.subtract).then_inc(d, 1)
                k += 1
                dve.wait_ge(d, k)
                dve.tensor_copy(brow[:, 0, :], brow[:, 1, :]).then_inc(d, 1)
                k += 1
                dve.wait_ge(d, k)

        @block.sync
        def _(sp):
            sp.wait_ge(dz, 3)
            for j in range(2):
                r = slice(64 * j, 64 * j + 64)
                for k in range(3):
                    sp.dma_start(n.wqkv[r, k, r], n.w_qkv[:, 64 * k:64 * k + 64]).then_inc(w_in, 16)
                sp.dma_start(n.wp[r, r], n.w_proj).then_inc(w_in, 16)
                sp.dma_start(n.gate[r, E * j:E * j + E], n.gate_w).then_inc(w_in, 16)
                sp.dma_start(brow[:, 0, r], n.b_proj).then_inc(w_in, 16)
            sp.dma_start(n.gate_b[:, :], n.gate_bias.broadcast_to([P, n.gate_bias.shape[1]])).then_inc(moved, 16)
            sp.wait_ge(d, 18)
            for part in range(3):
                sp.dma_start(n.bp[part:part + 1, :], bpart[:, part, :, :].rearrange("o r c -> o (r c)")).then_inc(moved, 16)
            sp.wait_ge(moved, 16 * 4)

        @block.gpsimd
        def _(pool):
            def select(out, pattern, op, base, mult, fill):
                select.k += 1
                pool.affine_select(out=out, in_=out, compare_op=op, fill=fill, base=base, pattern=pattern,
                                   channel_multiplier=mult).then_inc(s, 1)
                pool.wait_ge(s, select.k)
            select.k = 0
            ts = [(n.ident[:, :], 0.0), (n.ident_b[:, :], 0.0), (n.ident_h[:, :], 0.0), (n.mhalf[:, :], -0.5), (n.mask[:, :, :, :], 0.0),
                  (n.hmask[:, :], 1.0), (n.tri[:, :], 1.0), (n.ones_b[:, :], 1.0), (n.pcol[:, :], 1.0), (n.jmask[:, :], 1.0)]
            for t, v in ts:
                pool.memset(t, v).then_inc(z, 1)
            pool.wait_ge(z, len(ts))
            for t in (n.ident, n.ident_b, n.ident_h):
                select(t[:, :], [[-1, P]], ALU.not_equal, 0, 1, 1.0)
            for w in range(2):
                m = n.mask[64 * w:64 * w + 64, :, :, :]
                select(m, [[0, 2], [0, HEADS], [-1, WIN]], ALU.is_ge, 0, 1, NEG)
                select(m, [[0, 2], [0, HEADS], [1, WIN]], ALU.is_ge, RADIUS, -1, NEG)
            for j in range(2):
                m = n.hmask[64 * j:64 * j + 64, :]
                select(m, [[-HD, HEADS]], ALU.is_ge, 0, 1, 0.0)
                select(m, [[HD, HEADS]], ALU.is_ge, HD - 1, -1, 0.0)
            select(n.jmask[:, 0:1], [[0, 1]], ALU.is_ge, 63, -1, 0.0)
            select(n.jmask[:, 1:2], [[0, 1]], ALU.is_ge, -64, 1, 0.0)
            select(n.tri[:, :], [[1, P]], ALU.is_gt, 0, -1, 0.0)
            select(n.pcol[:, 0:1], [[0, 1]], ALU.is_ge, CB - 1, -1, 0.0)
            select(n.pcol[:, 0:1], [[0, 1]], ALU.not_equal, -32, 1, 1.0)
            select(n.pcol[:, 1:2], [[0, 1]], ALU.is_ge, -CB, 1, 0.0)
            select(n.pcol[:, 1:2], [[0, 1]], ALU.is_ge, 32, -1, 0.0)
            select(n.pcol[:, 2:3], [[0, 1]], ALU.is_ge, 31, -1, 0.0)
            select(n.pcol[:, 3:4], [[0, 1]], ALU.is_ge, -32, 1, 0.0)
            pool.iota(n.em8[:, :], [[1, E]], base=-E, channel_multiplier=0,
                      allow_small_or_imprecise_dtypes=True).then_inc(s, 1)
            pool.wait_ge(s, select.k + 1)


ORDER = ("t0", "t1", "rank", "ot0", "ot1", "xt0", "xt1", "pr0", "pr1", "q0", "q1", "k0", "k1", "v0", "v1",
         "zt0", "zt1", "gate")


def part_of(op):
    return "R" if op == "rank" else "Z" if op[:2] in ("ot", "pr", "zt", "ga") else "X"


def attention_stage(nc, n):
    with ExitStack() as ctx:
        def sb(name, shape, dt=F32):
            return ctx.enter_context(nc.sbuf_tensor(name, shape, dt))

        def sem(name):
            return ctx.enter_context(nc.semaphore(name))

        xg = sb("xg", [P, GW])
        s2g = sb("s2g", [33, GW], BF16)
        xn = sb("xn", [P, NB, 2, CIN])
        sq = sb("sq", [P, NB, 2, CIN])
        xrow = sb("xrow", [P, 2, NB, 2, ROW])
        xnT = sb("xnT", [P, GW])
        actT = sb("actT", [P, GW])
        qT = sb("qT", [P, 2, 2, GW])
        kx = sb("kx", [P, 2, HEADS, GW])
        vs = sb("vs", [P, NB, 2, 2, 2, HD])
        vw = sb("vw", [P, NB, 2, 2, 2, HD])
        vb = sb("vb", [P, 2, NB, 2, 2, 2, VW])
        pb = sb("pb", [P, 2, 2, HEADS, WIN])
        pT = sb("pT", [P, 2, 4, P])
        ob = sb("ob", [P, 2, NB, 2 * HEADS, HD])
        mx = sb("mx", [P, 2, 2 * HEADS])
        rl = sb("rl", [P, 2, 2 * HEADS])
        sx = sb("sx", [P, 6, GT])
        sz = sb("sz", [P, 6, GT])
        lg = sb("lg", [P, GT, E])
        lw = sb("lw", [P, 2, GT, E])
        sd = lw[:, 1, :, :].rearrange("p t e -> p (t e)").rearrange("p (e t) -> p e t", e=E)
        rt = sb("rt", [P, 6, GT])
        oh = sb("oh", [P, GT, E], BF16)
        ohf = sb("ohf", [P, GT, E])
        cnt = sb("cnt", [P, E, GT])
        inc = sb("inc", [P, E, GT])
        notfirst = sb("notfirst", [P, E, GT])
        carry = sb("carry", [P, E])
        ids = sb("ids", [P, NB, 2])
        dest = sb("dest", [P, 2, NB, 2], I32)
        S = [ctx.enter_context(nc.psum_tensor(f"S{i}", [P, 512], F32)) for i in range(2)]
        PT = ctx.enter_context(nc.psum_tensor("PT", [P, 512], F32))
        O = [ctx.enter_context(nc.psum_tensor(f"O{i}", [P, 512], F32)) for i in range(2)]
        M = [ctx.enter_context(nc.psum_tensor(f"M{i}", [P, 512], F32)) for i in range(3)]

        x_in, s_in, const = sem("x_in"), sem("s_in"), sem("a_const")
        s_ready, s_max, s_sub, s_exp = sem("s_ready"), sem("s_max"), sem("s_sub"), sem("s_exp")
        pt_ready, pt_copied, o_ready, o_recip, o_done = (sem("pt_ready"), sem("pt_copied"), sem("o_ready"),
                                                         sem("o_recip"), sem("o_done"))
        ready = {op: sem(f"{op}_ready") for op in ("t", "rank", "ot", "xt", "pr", "q", "k", "v", "zt", "gate")}
        taken = {op: sem(f"{op}_taken") for op in ("t", "rank", "ot", "xt", "pr", "q", "kd", "ka", "v", "zt", "gate")}
        ln = {(w, k): sem(f"{w}_{k}") for w in ("x", "z") for k in ("sum", "mean", "centered", "square", "sum2", "var", "rstd", "norm")}
        v_sw, v_built = sem("v_swapped"), sem("v_built")
        logit, r_step, r_exp, ranked, ids_step, scat = (sem("logit"), sem("r_step"), sem("r_exp"), sem("ranked"),
                                                        sem("ids_step"), [sem("scattered0"), sem("scattered1")])
        rank_q, numbered = sem("rank_wanted"), sem("numbered")
        high, low = sem("high_parts"), sem("low_parts")
        block = ctx.enter_context(nc.Block())

        NBLK = NG * NB
        BODIES = range(-1, NG + 2)
        R_STEPS = 19

        def has_x(i):
            return i + 1 < NG

        def has_z(i):
            return 0 <= i - 1 < NG

        def has_r(i):
            return 0 <= i - 2 < NG

        def chunk(c):
            b0, nb = CHUNKS[c]
            return b0, nb, nb * P

        plan, last = {}, [None, None, None]
        turn = 0
        for i in BODIES:
            for op in ORDER:
                part = part_of(op)
                if not {"X": has_x, "Z": has_z, "R": has_r}[part](i):
                    continue
                g = {"X": i + 1, "Z": i - 1, "R": i - 2}[part]
                bank = turn % 3
                turn += 1
                plan[(op, g)] = (bank, last[bank])
                if op[0] == "k":
                    last[bank] = ("kd" if op == "k0" else "ka", g + 1)
                elif op in ("rank", "gate"):
                    last[bank] = (op, g + 1)
                else:
                    last[bank] = (op[:-1], 2 * g + int(op[-1]) + 1)

        def bank_of(op, g):
            return M[plan[(op, g)][0]]

        def swap(sp, g):
            sp.wait_ge(taken["v"], 2 * g + 2)
            if g >= 1:
                sp.wait_ge(v_built, 4 * g)
            for w in range(2):
                sp.dma_start(vw[64 * w:64 * w + 64, :, :, :, :, :].rearrange("p b j r h d -> p (b j r h d)"),
                             vs[64 - 64 * w:128 - 64 * w, :, :, :, :, :].rearrange("p b j r h d -> p (b j r h d)")
                             ).then_inc(v_sw, 16)

        @block.sync
        def _(sp):
            for g in range(NG):
                if g >= 1:
                    sp.wait_ge(ready["t"], 2 * g)
                for j in range(2):
                    for image, pixel, at, m in pieces((2 * g + j) * GW, GW):
                        sp.dma_start(xg[64 * j:64 * j + 64, at:at + m], n.x[image, :, pixel:pixel + m]).then_inc(x_in, 16)
                        sp.dma_start(s2g[16 * j:16 * j + 16, at:at + m],
                                     n.s2_dram[image, :, pixel:pixel + m]).then_inc(s_in, 16)
                if g >= 1:
                    swap(sp, g - 1)
            swap(sp, NG - 1)

        n_pieces = [sum(len(pieces((2 * g + j) * GW, GW)) for j in range(2)) for g in range(NG)]

        def loaded(eng, g):
            eng.wait_ge(x_in, 16 * sum(n_pieces[:g + 1]))
            eng.wait_ge(s_in, 16 * sum(n_pieces[:g + 1]))

        @block.tensor
        def _(pe):
            def free(op, g):
                before = plan[(op, g)][1]
                if before:
                    pe.wait_ge(taken[before[0]], before[1])
                return bank_of(op, g)

            def t(g, c):
                b0, nb, w = chunk(c)
                bank = free(f"t{c}", g)
                if c == 0:
                    loaded(pe, g)
                    pe.wait_ge(const, 3)
                for b in range(nb):
                    cols = slice((b0 + b) * P, (b0 + b + 1) * P)
                    out = bank[:, b * P:(b + 1) * P]
                    pe.matmul(out, xg[:, cols], n.ident[:, :], start=True, stop=False)
                    for part in range(3):
                        mm = pe.matmul(out, s2g[:, cols], n.w3p[:, part, :], start=False, stop=(part == 2))
                mm.then_inc(ready["t"], 1)

            def transposed(op, src, g, c, wait):
                b0, nb, w = chunk(c)
                bank = free(f"{op}{c}", g)
                if c == 0:
                    wait()
                for b in range(nb):
                    mm = pe.transpose(bank[:, b * P:(b + 1) * P], src(b0 + b), n.ident[:, :])
                mm.then_inc(ready[op], 1)

            def qk(g, c, which):
                b0, nb, w = chunk(c)
                bank = free(f"{'qk'[which]}{c}", g)
                pe.wait_ge(taken["xt"], 2 * g + c + 1)
                pe.matmul(bank[:, 0:w], n.wqkv[:, which, :], xnT[:, b0 * P:b0 * P + w],
                          start=True, stop=True).then_inc(ready["qk"[which]], 1)

            def v(g, c):
                b0, nb, w = chunk(c)
                bank = free(f"v{c}", g)
                pe.wait_ge(taken["xt"], 2 * g + c + 1)
                for b in range(nb):
                    mm = pe.matmul(bank[:, b * P:(b + 1) * P], xnT[:, (b0 + b) * P:(b0 + b + 1) * P], n.wqkv[:, 2, :],
                                   start=True, stop=True)
                mm.then_inc(ready["v"], 1)

            def pr(g, c):
                b0, nb, w = chunk(c)
                bank = free(f"pr{c}", g)
                pe.wait_ge(taken["ot"], 2 * g + c + 1)
                pe.matmul(bank[:, 0:w], n.ones3[:, :], n.bp[:, 0:w], start=True, stop=False, skip_group_check=True)
                for b in range(nb):
                    mm = pe.matmul(bank[:, b * P:(b + 1) * P], actT[:, (b0 + b) * P:(b0 + b + 1) * P], n.wp[:, :],
                                   start=False, stop=(b == nb - 1), skip_group_check=True)
                mm.then_inc(ready["pr"], 1)

            def gate(g):
                bank = free("gate", g)
                pe.wait_ge(taken["zt"], 2 * g + 2)
                for b in range(NB):
                    mm = pe.matmul(bank[:, b * 2 * E:(b + 1) * 2 * E], actT[:, b * P:(b + 1) * P], n.gate[:, :],
                                   start=True, stop=True)
                mm.then_inc(ready["gate"], 1)

            def rank(g):
                bank = free("rank", g)
                pe.wait_ge(rank_q, g + 1)
                flat = oh[:, :, :].rearrange("p t e -> p (t e)")
                pe.matmul(bank[:, 0:GT * E], n.tri[:, :], flat, start=True, stop=True)
                pe.matmul(bank[:, GT * E:2 * GT * E], n.ones_b[:, :], flat, start=True, stop=True)\
                    .then_inc(ready["rank"], 1)

            def scores(B):
                g, b = divmod(B, NB)
                if b == 0:
                    pe.wait_ge(taken["q"], 2 * g + 2)
                    pe.wait_ge(taken["kd"], g + 1)
                    pe.wait_ge(taken["ka"], g + 1)
                if B >= 2:
                    pe.wait_ge(s_sub, B - 1)
                bank = S[B % 2]
                pe.matmul(bank[:, :], n.ident_b[:, :], n.mask[:, :, :, :].rearrange("p j h k -> p (j h k)"),
                          start=True, stop=False, skip_group_check=True)
                for j in range(2):
                    for w in range(2):
                        cols = slice(b * P + 64 * w, b * P + 64 * w + 64)
                        mm = pe.matmul(bank[64 * w:64 * w + 64, 256 * j:256 * j + 256], qT[:, g % 2, j, cols],
                                       kx[:, g % 2, :, cols], start=False, stop=(j == 1), skip_group_check=True)
                mm.then_inc(s_ready, 1)

            def turn_probs(B):
                pe.wait_ge(s_exp, B + 1)
                if B >= 1:
                    pe.wait_ge(pt_copied, B)
                for j in range(2):
                    for r in range(2):
                        mm = pe.transpose(PT[:, (2 * j + r) * P:(2 * j + r + 1) * P],
                                          pb[:, B % 2, j, 2 * r:2 * r + 2, :], n.ident[:, :])
                mm.then_inc(pt_ready, 1)

            def values(B):
                g, b = divmod(B, NB)
                if b == 0:
                    pe.wait_ge(v_built, 4 * g + 4)
                pe.wait_ge(pt_copied, B + 1)
                if B >= 2:
                    pe.wait_ge(o_done, B - 1)
                for w in range(2):
                    for j in range(2):
                        for r in range(2):
                            at = (2 * j + r) * 2 * VW
                            mm = pe.matmul(O[B % 2][64 * w:64 * w + 64, at:at + 2 * VW],
                                           pT[:, B % 2, 2 * j + r, 64 * w:64 * w + 64],
                                           vb[:, w, b, j, r, :, :], start=True, stop=True)
                mm.then_inc(o_ready, 1)

            for i in BODIES:
                for s in range(NB):
                    B = i * NB + s
                    if 0 <= B < NBLK:
                        scores(B)
                    if 0 < B <= NBLK:
                        turn_probs(B - 1)
                    if s == 0 and has_x(i):
                        t(i + 1, 0)
                        t(i + 1, 1)
                    if s == 1 and has_r(i):
                        rank(i - 2)
                    if s == 2 and has_z(i):
                        for c in range(2):
                            transposed("ot", lambda b: ob[:, (i - 1) % 2, b, :, :].rearrange("p h d -> p (h d)"), i - 1, c,
                                       lambda: pe.wait_ge(o_done, i * NB))
                    if s == 3:
                        if has_x(i):
                            for c in range(2):
                                transposed("xt", lambda b: xn[:, b, :, :].rearrange("p j c -> p (j c)"), i + 1, c,
                                           lambda: pe.wait_ge(ln["x", "norm"], i + 2))
                        if has_z(i):
                            pr(i - 1, 0)
                            pr(i - 1, 1)
                    if s == 4 and has_x(i):
                        for which in range(2):
                            for c in range(2):
                                qk(i + 1, c, which)
                    if s == 5 and has_x(i):
                        v(i + 1, 0)
                        v(i + 1, 1)
                    if s == 6 and has_z(i):
                        for c in range(2):
                            transposed("zt", lambda b: xn[:, b, :, :].rearrange("p j c -> p (j c)"), i - 1, c,
                                       lambda: pe.wait_ge(ln["z", "norm"], i))
                    if 0 < B <= NBLK:
                        values(B - 1)
                    if s == 6 and has_z(i):
                        gate(i - 1)

        @block.scalar
        def _(act):
            def build_values(g):
                act.wait_ge(v_sw, 32 * (g + 1))
                act.wait_ge(ids_step, 4)
                if g >= 1:
                    act.wait_ge(o_ready, NB * g)
                for hh in range(2):
                    for w in range(2):
                        r = slice(64 * hh, 64 * hh + 64)
                        src = (vs if hh == w else vw)[r, :, :, :, hh, :].rearrange("p b j r d -> p (b j r) d")
                        act.activation(vb[r, w, :, :, :, hh, 0:HD].rearrange("p b j r d -> p (b j r) d"),
                                       src, ACT.Copy).then_inc(v_built, 1)

            def take(op, g, c, dst, wait=None):
                b0, nb, w = chunk(c)
                act.wait_ge(ready[op], 2 * g + c + 1)
                if wait:
                    act.wait_ge(*wait)
                act.activation(dst(b0, nb, w), bank_of(f"{op}{c}", g)[:, 0:w], ACT.Copy).then_inc(taken[op], 1)

            def cols(t):
                return lambda b0, nb, w: t[:, b0 * P:b0 * P + w]

            for i in BODIES:
                for s in range(NB):
                    B = i * NB + s
                    if 0 < B <= NBLK:
                        act.wait_ge(pt_ready, B)
                        if B >= 3:
                            act.wait_ge(o_ready, B - 2)
                        act.activation(pT[:, (B - 1) % 2, :, :].rearrange("p r t -> p (r t)"), PT[:, :],
                                       ACT.Copy).then_inc(pt_copied, 1)
                    if 0 <= B < NBLK:
                        act.wait_ge(s_sub, B + 1)
                        act.activation(pb[:, B % 2, :, :, :], pb[:, B % 2, :, :, :], ACT.Exp,
                                       scale=SCALE).then_inc(s_exp, 1)
                    if s == 0 and 0 <= i < NG:
                        build_values(i)
                    if s == 1 and has_x(i):
                        act.wait_ge(ln["x", "centered"], i + 2)
                        if i >= 1:
                            act.wait_ge(ln["z", "sum2"], i - 1)
                        act.activation(sq[:, :, :, :], xn[:, :, :, :], ACT.Square).then_inc(ln["x", "square"], 1)
                    if s == 2 and has_z(i):
                        for c in range(2):
                            take("ot", i - 1, c, cols(actT), (ready["gate"], i - 1))
                    if s == 3 and has_x(i):
                        for c in range(2):
                            take("xt", i + 1, c, cols(xnT), (ready["v"], 2 * i + 2))
                    if s == 4 and has_x(i):
                        if i >= 1:
                            act.wait_ge(s_ready, i * NB)
                        for c in range(2):
                            b0, nb, w = chunk(c)
                            act.wait_ge(ready["q"], 2 * (i + 1) + c + 1)
                            for j in range(2):
                                ins = act.activation(qT[:, (i + 1) % 2, j, b0 * P:b0 * P + w],
                                                     bank_of(f"q{c}", i + 1)[:, 0:w], ACT.Copy,
                                                     scale=n.jmask[:, j:j + 1])
                            ins.then_inc(taken["q"], 1)
                        b0, nb, w = chunk(1)
                        act.wait_ge(ready["k"], 2 * (i + 1) + 2)
                        for h in range(HEADS):
                            ins = act.activation(kx[:, (i + 1) % 2, h, b0 * P:b0 * P + w], bank_of("k1", i + 1)[:, 0:w],
                                                 ACT.Copy, scale=n.hmask[:, h:h + 1])
                        ins.then_inc(taken["ka"], 1)
                    if s == 5:
                        if has_z(i):
                            act.wait_ge(ln["z", "centered"], i)
                            if has_x(i):
                                act.wait_ge(ln["x", "sum2"], i + 2)
                            else:
                                act.wait_ge(ln["z", "sum2"], i - 1)
                            act.activation(sq[:, :, :, :], xn[:, :, :, :], ACT.Square).then_inc(ln["z", "square"], 1)
                        if has_x(i):
                            for c in range(2):
                                take("v", i + 1, c,
                                     lambda b0, nb, w: vs[:, b0:b0 + nb, :, :, :, :].rearrange("p b j r h d -> p (b j r h d)"),
                                     (v_built, 4 * (i + 1)) if c == 0 else None)
                    if s == 6 and has_z(i):
                        act.wait_ge(ln["z", "norm"], i)
                        if i >= 3:
                            act.wait_ge(scat[(i - 1) % 2], 16 * GT * ((i - 1) // 2))
                        act.activation(xrow[:, (i - 1) % 2, :, :, 0:CIN // 2].bitcast(F16), xn[:, :, :, :],
                                       ACT.Copy).then_inc(high, 1)
                        for c in range(2):
                            take("zt", i - 1, c, cols(actT), (ready["pr"], 2 * i))
                    if s == 0 and has_r(i):
                        act.wait_ge(r_step, R_STEPS * (i - 2) + 3)
                        act.activation(lw[:, 0, :, :], lw[:, 0, :, :], ACT.Exp).then_inc(r_exp, 1)

        @block.vector
        def _(dve):
            dve.memset(notfirst[:, :, :], 1.0).then_inc(const, 1)
            dve.memset(carry[:, :], 0.0).then_inc(const, 1)
            dve.memset(s2g[32:33, :], 1.0).then_inc(const, 1)
            dve.wait_ge(const, 3)
            dve.memset(notfirst[:, :, 0:1], 0.0).then_inc(const, 1)
            dve.wait_ge(const, 4)

            def ln_mean(w, src, st, g):
                dve.wait_ge(ln[w, "rstd"], g)
                dve.tensor_reduce(st[:, 0, :].rearrange("p (b j) -> p b j", j=2), src, AX.X, ALU.add)\
                    .then_inc(ln[w, "sum"], 1)
                dve.wait_ge(ln[w, "sum"], g + 1)
                dve.wait_ge(ln[w, "norm"], g)
                dve.tensor_scalar(st[:, 1, :], st[:, 0, :], 1.0 / CIN, None, ALU.mult).then_inc(ln[w, "mean"], 1)

            def ln_var(w, st, g):
                dve.wait_ge(ln[w, "square"], g + 1)
                dve.tensor_reduce(st[:, 2, :].rearrange("p (b j) -> p b j", j=2), sq[:, :, :, :], AX.X, ALU.add)\
                    .then_inc(ln[w, "sum2"], 1)
                dve.wait_ge(ln[w, "sum2"], g + 1)
                dve.tensor_scalar(st[:, 3, :], st[:, 2, :], 1.0 / CIN, LN_EPS, ALU.mult, ALU.add)\
                    .then_inc(ln[w, "var"], 1)

            def t_clip(g):
                for c in range(2):
                    b0, nb, w = chunk(c)
                    dve.wait_ge(ready["t"], 2 * g + c + 1)
                    dve.tensor_scalar(n.t2[:, g, b0:b0 + nb, :, :],
                                      bank_of(f"t{c}", g)[:, 0:w].rearrange("p (b j c) -> p b j c", j=2, c=CIN),
                                      -1.0, 1.0, ALU.max, ALU.min).then_inc(taken["t"], 1)
                dve.wait_ge(taken["t"], 2 * g + 2)
                ln_mean("x", n.t2[:, g, :, :, :], sx, g)

            def residual(g):
                for c in range(2):
                    b0, nb, w = chunk(c)
                    dve.wait_ge(ready["pr"], 2 * g + c + 1)
                    tt = n.t2[:, g, b0:b0 + nb, :, :]
                    dve.tensor_tensor(tt, bank_of(f"pr{c}", g)[:, 0:w].rearrange("p (b j c) -> p b j c", j=2, c=CIN),
                                      tt, ALU.add).then_inc(taken["pr"], 1)
                dve.wait_ge(taken["pr"], 2 * g + 2)
                ln_mean("z", n.t2[:, g, :, :, :], sz, g)

            def keys(g):
                b0, nb, w = chunk(0)
                dve.wait_ge(ready["k"], 2 * g + 1)
                src = spread(bank_of("k0", g)[:, 0:w], 1, HEADS)
                dve.tensor_tensor(kx[:, g % 2, :, b0 * P:b0 * P + w], src,
                                  spread(n.hmask[:, :], 2, w), ALU.mult).then_inc(taken["kd"], 1)

            step = [0]

            def link(ins):
                step[0] += 1
                ins.then_inc(r_step, 1)
                dve.wait_ge(r_step, step[0])

            def route_a(g):
                assert step[0] == R_STEPS * g
                L = lg[:, :, :]
                dve.wait_ge(ready["gate"], g + 1)
                dve.tensor_tensor(L, bank_of("gate", g)[:, 0:GT * E].rearrange("p (t e) -> p t e", e=E),
                                  spread(n.gate_b[:, :], 1, GT), ALU.add).then_inc(taken["gate"], 1)
                dve.wait_ge(taken["gate"], g + 1)

            def route_b(g):
                L = lg[:, :, :]
                top = rt[:, 0, :]
                link(dve.tensor_reduce(top, L, AX.X, ALU.max))
                link(dve.tensor_tensor(lw[:, 1, :, :], L, spread(top, 2, E), ALU.is_ge))
                link(dve.tensor_tensor(lw[:, 0, :, :], L, spread(top, 2, E), ALU.subtract))
                link(dve.tensor_tensor(lw[:, 1, :, :], lw[:, 1, :, :], spread(n.em8[:, :], 1, GT), ALU.mult))
                link(dve.tensor_reduce(rt[:, 1, :], lw[:, 1, :, :], AX.X, ALU.min))
                link(dve.tensor_tensor(ohf[:, :, :], spread(n.em8[:, :], 1, GT),
                                       spread(rt[:, 1, :], 2, E), ALU.is_equal))
                dve.tensor_copy(oh[:, :, :], ohf[:, :, :]).then_inc(rank_q, 1)
                dve.wait_ge(r_exp, g + 1)
                link(dve.tensor_reduce(rt[:, 2, :], lw[:, 0, :, :], AX.X, ALU.add))
                link(dve.reciprocal(xrow[:, g % 2, :, :, RP], rt[:, 2, :].rearrange("p (b j) -> p b j", j=2)))

            def route_c(g):
                dve.wait_ge(ready["rank"], g + 1)
                bank = bank_of("rank", g)

                def by_expert(a):
                    return a.rearrange("p (b j e) -> p e j b", b=NB, j=2)

                def ordered(a):
                    return a.rearrange("p e (j b) -> p e j b", j=2)
                link(dve.tensor_copy(flat4(cnt), by_expert(bank[:, GT * E:2 * GT * E])))
                link(dve.tensor_copy(sd[:, :, :], cnt[:, :, :]))
                link(dve.tensor_tensor(sd[:, :, 0], sd[:, :, 0], carry[:, :], ALU.add))
                link(dve.tensor_tensor_scan(inc[:, :, :].rearrange("p e t -> p (e t)"),
                                            notfirst[:, :, :].rearrange("p e t -> p (e t)"),
                                            sd[:, :, :].rearrange("p e t -> p (e t)"), 0.0, ALU.mult, ALU.add))
                link(dve.tensor_copy(carry[:, :], inc[:, :, GT - 1]))
                link(dve.tensor_tensor(cnt[:, :, :], inc[:, :, :], cnt[:, :, :], ALU.subtract))
                dve.tensor_tensor(flat4(sd), by_expert(bank[:, 0:GT * E]), flat4(cnt), ALU.add).then_inc(taken["rank"], 1)
                dve.wait_ge(taken["rank"], g + 1)
                link(dve.tensor_tensor(flat4(sd), flat4(sd), by_expert(ohf[:, :, :].rearrange("p t e -> p (t e)")), ALU.mult))
                link(dve.tensor_reduce(rt[:, 3, :], sd[:, :, :].rearrange("p e t -> p t e"), AX.X, ALU.add))
                link(dve.tensor_scalar(rt[:, 4, :], rt[:, 3, :], CAP - 0.5, NOWHERE, ALU.is_gt, ALU.mult))
                link(dve.tensor_tensor(rt[:, 4, :], rt[:, 4, :], rt[:, 3, :], ALU.add))
                link(dve.tensor_scalar(rt[:, 5, :], rt[:, 1, :], float(ES), float(E * ES), ALU.mult, ALU.add))
                if g >= 2:
                    dve.wait_ge(scat[g % 2], 16 * GT * (g // 2))
                dve.tensor_tensor(dest[:, g % 2, :, :], rt[:, 5, :].rearrange("p (b j) -> p b j", j=2),
                                  rt[:, 4, :].rearrange("p (j b) -> p b j", j=2), ALU.add).then_inc(ranked, 1)

            def flat4(t):
                return t[:, :, :].rearrange("p e (j b) -> p e j b", j=2)

            def low_parts(g):
                dve.wait_ge(high, g + 1)
                dve.tensor_tensor(xrow[:, g % 2, :, :, CIN // 2:CIN].bitcast(F16), xn[:, :, :, :],
                                  xrow[:, g % 2, :, :, 0:CIN // 2].bitcast(F16), ALU.subtract).then_inc(low, 1)

            def norm(B):
                g, b = divmod(B, NB)
                dve.wait_ge(o_ready, B + 1)
                if b == 0 and g >= 2:
                    dve.wait_ge(ready["ot"], 2 * (g - 1))
                o = O[B % 2][:, 0:8 * VW].rearrange("p (h v) -> p h v", v=VW)
                if B >= 2:
                    dve.wait_ge(o_done, B - 1)
                dve.reciprocal(rl[:, B % 2, :], o[:, :, HD]).then_inc(o_recip, 1)
                dve.wait_ge(o_recip, B + 1)
                dve.tensor_tensor(ob[:, g % 2, b, :, :], o[:, :, 0:HD], spread(rl[:, B % 2, :], 2, HD),
                                  ALU.mult).then_inc(o_done, 1)

            for i in BODIES:
                for s in range(NB):
                    B = i * NB + s
                    if 0 <= B < NBLK:
                        sc = S[B % 2][:, :].rearrange("p (h k) -> p h k", k=WIN)
                        dve.wait_ge(s_ready, B + 1)
                        if B >= 2:
                            dve.wait_ge(s_sub, B - 1)
                        dve.tensor_reduce(mx[:, B % 2, :], sc, AX.X, ALU.max).then_inc(s_max, 1)
                        if B >= 2:
                            dve.wait_ge(pt_ready, B - 1)
                        dve.wait_ge(s_max, B + 1)
                        dve.tensor_tensor(pb[:, B % 2, :, :, :].rearrange("p j h k -> p (j h) k"), sc,
                                          spread(mx[:, B % 2, :], 2, WIN), ALU.subtract).then_inc(s_sub, 1)
                    if 0 <= B - 2 < NBLK:
                        norm(B - 2)
                    if s == 0:
                        if has_r(i):
                            route_a(i - 2)
                        if has_x(i):
                            t_clip(i + 1)
                        if has_r(i):
                            route_b(i - 2)
                    if s == 1:
                        if has_r(i):
                            route_c(i - 2)
                    if s == 2 and has_x(i):
                        ln_var("x", sx, i + 1)
                    if s == 3 and has_z(i):
                        residual(i - 1)
                    if s == 4 and has_x(i):
                        keys(i + 1)
                    if s == 5 and has_z(i):
                        ln_var("z", sz, i - 1)
                    if s == 6 and has_z(i):
                        low_parts(i - 1)

        @block.gpsimd
        def _(pool):
            pool.memset(vb[:, :, :, :, :, :, :], 0.0).then_inc(ids_step, 1)
            pool.iota(ids[:, :, :], [[P, NB], [GW, 2]], base=0, channel_multiplier=1,
                      allow_small_or_imprecise_dtypes=True).then_inc(ids_step, 1)
            pool.wait_ge(ids_step, 2)
            for hh in range(2):
                pool.memset(vb[64 * hh:64 * hh + 64, :, :, :, :, hh, HD:VW].rearrange("p w b j r o -> p (w b j r) o"),
                            1.0).then_inc(ids_step, 1)
            pool.wait_ge(ids_step, 4)

            def center(w, g, dst, st):
                pool.wait_ge(ln[w, "mean"], g + 1)
                if w == "z":
                    pool.wait_ge(ready["xt"], 2 * min(g + 3, NG))
                elif g >= 3:
                    pool.wait_ge(ready["zt"], 2 * (g - 2))
                    pool.wait_ge(low, g - 2)
                if w == "z" and g >= 1:
                    pool.wait_ge(ready["zt"], 2 * g)
                    pool.wait_ge(low, g)
                pool.tensor_tensor(dst[:, :, :, :], n.t2[:, g, :, :, :],
                                   spread(st[:, 1, :].rearrange("p (b j) -> p b j", j=2), 3, CIN),
                                   ALU.subtract).then_inc(ln[w, "centered"], 1)

            def scale(w, g, dst, st):
                pool.wait_ge(ln[w, "var"], g + 1)
                pool.tensor_tensor(st[:, 4, :], st[:, 3, :], n.mhalf[:, 0:GT], ALU.pow).then_inc(ln[w, "rstd"], 1)
                pool.wait_ge(ln[w, "rstd"], g + 1)
                pool.tensor_tensor(dst[:, :, :, :], dst[:, :, :, :],
                                   spread(st[:, 4, :].rearrange("p (b j) -> p b j", j=2), 3, CIN),
                                   ALU.mult).then_inc(ln[w, "norm"], 1)

            def scatter(g, lo, hi):
                if lo == 0:
                    if g >= 2:
                        pool.wait_ge(scat[g % 2], 16 * GT * (g // 2))
                    pool.tensor_scalar(xrow[:, g % 2, :, :, RI], ids[:, :, :], float(g * GT * P), None,
                                       ALU.add).then_inc(numbered, 1)
                    pool.wait_ge(numbered, g + 1)
                    pool.wait_ge(ranked, g + 1)
                for k in range(lo, hi):
                    b, j = divmod(k, 2)
                    pool.indirect_dma_start(n.slots, bass.IndirectOffsetOnAxis(ap=dest[:, g % 2, b, j:j + 1], axis=0),
                                            xrow[:, g % 2, b, j, :], None, bounds_check=SLOTS - 1,
                                            oob_is_err=False).then_inc(scat[g % 2], 16)

            for i in BODIES:
                for s in range(NB):
                    if s == 0 and has_x(i):
                        center("x", i + 1, xn, sx)
                    if s == 2 and has_x(i):
                        scale("x", i + 1, xn, sx)
                    if s == 3 and has_z(i):
                        center("z", i - 1, xn, sz)
                    if s == 5 and has_z(i):
                        scale("z", i - 1, xn, sz)
                    if has_r(i):
                        lo, hi = {1: (0, 2), 2: (2, 5), 3: (5, 8), 4: (8, 11), 5: (11, 12), 6: (12, 14)}.get(s, (0, 0))
                        if hi > lo:
                            scatter(i - 2, lo, hi)
            for q in range(2):
                pool.wait_ge(scat[q], 16 * GT * ((NG + 1 - q) // 2))


def expert_stage(nc, n):
    with ExitStack() as ctx:
        def sb(name, shape, dt=F32):
            return ctx.enter_context(nc.sbuf_tensor(name, shape, dt))

        def sem(name):
            return ctx.enter_context(nc.semaphore(name))

        QUADS = [(e, e * ES + s * P, min(4, TPE - s)) for e in range(E) for s in range(0, TPE, 4)]
        NQD, QPE = len(QUADS), -(-TPE // 4)
        RR, YR, YT = 4, 3, 4
        rows = sb("rows", [P, RR, 4, ROW])
        xT = sb("xT", [P, 2, 4 * P], F16)
        idx = sb("idx", [P, YR, 4], I32)
        w1f = sb("w1f_e", [P, F])
        w2f = sb("w2f_e", [P, 2, CIN])
        w1 = sb("w1_parts", [P, 2, 2, F], F16)
        w2 = sb("w2_parts", [P, 2, 2, 2, CIN], F16)
        bf = sb("bias_row", [1, E * (F + CIN)])
        bp = sb("bias_parts", [1, 2, E * (F + CIN)], F16)
        bias = sb("bias", [2, E * (F + CIN)], F16)
        ones = sb("ones2", [2, 4 * P], F16)
        hh = sb("h_high", [P, 2, 2, 4 * P], F16)
        hl = sb("h_low", [P, 2, 2, 4 * P], F16)
        ye = sb("ye", [P, YR, 4, CIN])
        lim = sb("lim", [P, 4, CIN])
        bad = sb("bad", [P, 2, 4, CIN], I32)
        zero = sb("zero", [P, 4, CIN])
        yt = sb("yt", [P, YT, NB, 2, CIN])
        fin = sb("fin", [P, 2, NB, 2, CIN])
        out = sb("out", [P, 2, GW])
        A = [ctx.enter_context(nc.psum_tensor(f"A{i}", [P, 1024], F16)) for i in range(2)]
        Hb = [[ctx.enter_context(nc.psum_tensor(f"H{i}{c}", [P, 512], F32)) for c in range(2)] for i in range(2)]
        Y = [ctx.enter_context(nc.psum_tensor(f"Y{i}", [P, 512], F32)) for i in range(2)]

        row_in = [sem(f"row_in{k}") for k in range(RR)]
        w_in, w_split, b_in, b_split, b_moved = sem("ew_in"), sem("w_split"), sem("b_in"), sem("b_split"), sem("b_moved")
        xt_ready, xt_taken = sem("xT_ready"), sem("xT_taken")
        h_ready, hh_done, hl_done = sem("h_ready"), sem("hh_done"), sem("hl_done")
        y_ready, y_taken, y_checked, y_full = sem("y_ready"), sem("y_taken"), sem("y_checked"), sem("y_full")
        idx_done, zeroed = sem("idx_done"), sem("zeroed")
        sent = [sem(f"sent{k}") for k in range(YR)]
        yt_in = [sem(f"yt_in{k}") for k in range(YT)]
        summed, o_ready, o_taken = sem("summed"), sem("out_ready"), sem("out_taken")
        stored = [sem("stored0"), sem("stored1")]
        block = ctx.enter_context(nc.Block())

        def n_sent(k, upto):
            return 16 * sum(QUADS[g][2] for g in range(k, upto, YR))

        n_out = [sum(len(pieces((2 * g + j) * GW, GW)) for j in range(2)) for g in range(NG)]

        @block.sync
        def _(sp):
            def weights(e):
                if e >= 1:
                    sp.wait_ge(w_split, 4 * e)
                for u in range(2):
                    sp.dma_start(w1f[64 * u:64 * u + 64, :], n.e_w1[e]).then_inc(w_in, 16)
                sp.dma_start(w2f[:, :, :], n.e_w2[e].rearrange("(c f) d -> f c d", c=2)).then_inc(w_in, 16)

            def load_rows(g):
                e, s0, nt = QUADS[g]
                if g >= RR:
                    sp.wait_ge(y_taken, g - RR + 1)
                    sp.wait_ge(idx_done, g - RR + 1)
                sp.dma_start(rows[:, g % RR, 0:nt, :],
                             n.slots[s0:s0 + nt * P, :].rearrange("(p u) d -> p u d", u=nt)
                             ).then_inc(row_in[g % RR], 16)

            sp.dma_start(bf[:, 0:E * F], n.e_b1).then_inc(b_in, 16)
            sp.dma_start(bf[:, E * F:], n.e_b2).then_inc(b_in, 16)
            weights(0)
            load_rows(0)
            sp.wait_ge(b_split, 2)
            for part in range(2):
                sp.dma_start(bias[part:part + 1, :], bp[:, part, :]).then_inc(b_moved, 16)
            for g in range(1, NQD):
                e, k = divmod(g, QPE)
                load_rows(g)
                if k == 4 and e + 1 < E:
                    weights(e + 1)
            for k in range(YR):
                sp.wait_ge(sent[k], n_sent(k, NQD))

            def load(g):
                if g >= YT:
                    sp.wait_ge(summed, g - YT + 1)
                for j in range(2):
                    sp.dma_start(yt[:, g % YT, :, j, :],
                                 n.y_tok[(2 * g + j) * GW:(2 * g + j + 1) * GW, :].rearrange("(b p) d -> p b d", p=P)
                                 ).then_inc(yt_in[g % YT], 16)

            for g in range(YT - 1):
                load(g)
            for g in range(NG):
                if g + YT - 1 < NG:
                    load(g + YT - 1)
                sp.wait_ge(o_taken, 2 * g + 2)
                for j in range(2):
                    for image, pixel, at, m in pieces((2 * g + j) * GW, GW):
                        sp.dma_start(n.out[image, :, pixel:pixel + m],
                                     out[64 * j:64 * j + 64, g % 2, at:at + m]).then_inc(stored[g % 2], 16)
            for q in range(2):
                sp.wait_ge(stored[q], 16 * sum(n_out[q::2]))

        @block.tensor
        def _(pe):
            def turn(g):
                nt = QUADS[g][2]
                pe.wait_ge(row_in[g % RR], 16 * (g // RR + 1))
                if g >= 2:
                    pe.wait_ge(xt_taken, g - 1)
                for u in range(nt):
                    mm = pe.transpose(A[g % 2][:, u * P:(u + 1) * P], rows[:, g % RR, u, 0:CIN].bitcast(F16),
                                      n.ident_h[:, :])
                mm.then_inc(xt_ready, 1)

            def first(g):
                e, _, nt = QUADS[g]
                w = nt * P
                if g % QPE == 0:
                    pe.wait_ge(w_split, 4 * e + 4)
                if g == 0:
                    pe.wait_ge(zeroed, 2)
                    pe.wait_ge(b_moved, 32)
                pe.wait_ge(xt_taken, g + 1)
                for c in range(2):
                    if g >= 2:
                        pe.wait_ge(hl_done, 2 * (g - 2) + c + 1)
                    at = e * F + c * P
                    bank = Hb[g % 2][c][:, 0:w]
                    pe.matmul(bank, bias[:, at:at + P], ones[:, 0:w], start=True, stop=False)
                    for part in range(2):
                        mm = pe.matmul(bank, w1[:, e % 2, part, c * P:(c + 1) * P], xT[:, g % 2, 0:w],
                                       start=False, stop=(part == 1))
                    mm.then_inc(h_ready, 1)

            def second(g):
                e, _, nt = QUADS[g]
                bank = Y[g % 2]
                if g >= 2:
                    pe.wait_ge(y_taken, g - 1)
                at = E * F + e * CIN
                pe.matmul(bank[:, 0:nt * CIN].rearrange("p (u c) -> p u c", c=CIN), ones[:, 0:P],
                          spread(bias[:, at:at + CIN], 1, nt), start=True, stop=False, skip_group_check=True)
                for c in range(2):
                    pe.wait_ge(hl_done, 2 * g + c + 1)
                    for u in range(nt):
                        for h in (hh, hl):
                            for part in range(2):
                                mm = pe.matmul(bank[:, u * CIN:(u + 1) * CIN], h[:, g % 2, c, u * P:(u + 1) * P],
                                               w2[:, e % 2, part, c, :], start=False, stop=(c == 1 and part == 1 and h is hl),
                                               skip_group_check=True)
                mm.then_inc(y_ready, 1)

            for k in range(-2, NQD):
                if k + 2 < NQD:
                    turn(k + 2)
                if 0 <= k + 1 < NQD:
                    first(k + 1)
                if 0 <= k:
                    second(k)
            for g in range(NG):
                pe.wait_ge(summed, g + 1)
                for c, (b0, nb) in enumerate(CHUNKS):
                    if g >= 2:
                        pe.wait_ge(o_taken, 2 * (g - 2) + c + 1)
                    for b in range(nb):
                        mm = pe.transpose(Hb[g % 2][c][:, b * P:(b + 1) * P],
                                          fin[:, g % 2, b0 + b, :, :].rearrange("p j c -> p (j c)"), n.ident[:, :])
                    mm.then_inc(o_ready, 1)

        @block.scalar
        def _(act):
            for k in range(-2, NQD):
                if k + 2 < NQD:
                    g = k + 2
                    w = QUADS[g][2] * P
                    act.wait_ge(xt_ready, g + 1)
                    if g >= 2:
                        act.wait_ge(h_ready, 2 * (g - 1))
                    act.activation(xT[:, g % 2, 0:w], A[g % 2][:, 0:w], ACT.Copy).then_inc(xt_taken, 1)
                if 0 <= k + 1 < NQD:
                    g = k + 1
                    w = QUADS[g][2] * P
                    for c in range(2):
                        act.wait_ge(h_ready, 2 * g + c + 1)
                        if g >= 2 and c == 0:
                            act.wait_ge(y_ready, g - 1)
                        act.activation(hh[:, g % 2, c, 0:w], Hb[g % 2][c][:, 0:w], ACT.Relu).then_inc(hh_done, 1)
            for g in range(NG):
                if g >= 2:
                    act.wait_ge(stored[g % 2], 16 * sum(n_out[g % 2:g:2]))
                for c, (b0, nb) in enumerate(CHUNKS):
                    act.wait_ge(o_ready, 2 * g + c + 1)
                    act.activation(out[:, g % 2, b0 * P:(b0 + nb) * P], Hb[g % 2][c][:, 0:nb * P],
                                   ACT.Copy).then_inc(o_taken, 1)

        @block.vector
        def _(dve):
            dve.memset(zero[:, :, :], 0.0).then_inc(zeroed, 1)
            dve.memset(ones[:, :], 1.0).then_inc(zeroed, 1)

            def split_weights(e):
                q = e % 2
                dve.wait_ge(w_in, 48 * (e + 1))
                if e >= 2:
                    dve.wait_ge(y_ready, (e - 1) * QPE)
                dve.tensor_copy(w1[:, q, 0, :], w1f[:, :]).then_inc(w_split, 1)
                dve.tensor_copy(w2[:, q, 0, :, :], w2f[:, :, :]).then_inc(w_split, 1)
                dve.wait_ge(w_split, 4 * e + 2)
                dve.tensor_tensor(w1[:, q, 1, :], w1f[:, :], w1[:, q, 0, :], ALU.subtract).then_inc(w_split, 1)
                dve.tensor_tensor(w2[:, q, 1, :, :], w2f[:, :, :], w2[:, q, 0, :, :], ALU.subtract).then_inc(w_split, 1)

            dve.wait_ge(b_in, 32)
            dve.tensor_copy(bp[:, 0, :], bf[:, :]).then_inc(b_split, 1)
            dve.wait_ge(b_split, 1)
            dve.tensor_tensor(bp[:, 1, :], bf[:, :], bp[:, 0, :], ALU.subtract).then_inc(b_split, 1)
            split_weights(0)
            dve.wait_ge(zeroed, 2)
            checked = 0
            for k in range(-1, NQD):
                if k + 1 < NQD:
                    g = k + 1
                    w = QUADS[g][2] * P
                    if g % QPE == 8 and g // QPE + 1 < E:
                        split_weights(g // QPE + 1)
                    for c in range(2):
                        dve.wait_ge(hh_done, 2 * g + c + 1)
                        if g >= 2 and c == 0:
                            dve.wait_ge(y_ready, g - 1)
                        dve.scalar_tensor_tensor(hl[:, g % 2, c, 0:w], Hb[g % 2][c][:, 0:w], 0.0, hh[:, g % 2, c, 0:w],
                                                 ALU.max, ALU.subtract).then_inc(hl_done, 1)
                if 0 <= k:
                    g = k
                    nt = QUADS[g][2]
                    r = rows[:, g % RR, 0:nt, :]
                    yy = ye[:, g % YR, 0:nt, :]
                    if g >= YR:
                        dve.wait_ge(sent[g % YR], n_sent(g % YR, g))
                    dve.tensor_copy(idx[:, g % YR, 0:nt], r[:, :, RI]).then_inc(idx_done, 1)
                    dve.wait_ge(y_ready, g + 1)
                    dve.tensor_tensor(yy, Y[g % 2][:, 0:nt * CIN].rearrange("p (u c) -> p u c", c=CIN),
                                      spread(r[:, :, RP], 2, CIN), ALU.mult).then_inc(y_taken, 1)
                    dve.wait_ge(y_taken, g + 1)
                    dve.tensor_scalar(bad[:, 0, 0:nt, :], yy, 0.0, 0.0, ALU.mult, ALU.not_equal).then_inc(y_checked, 1)
                    dve.tensor_scalar(lim[:, 0:nt, :], yy, -1e4, 1e4, ALU.max, ALU.min).then_inc(y_checked, 1)
                    dve.tensor_tensor(bad[:, 1, 0:nt, :], yy, yy, ALU.not_equal).then_inc(y_checked, 1)
                    dve.wait_ge(y_checked, checked + 3)
                    dve.copy_predicated(yy, bad[:, 0, 0:nt, :], lim[:, 0:nt, :]).then_inc(y_checked, 1)
                    checked += 4
                    dve.wait_ge(y_checked, checked)
                    dve.copy_predicated(yy, bad[:, 1, 0:nt, :], zero[:, 0:nt, :]).then_inc(y_full, 1)
            for g in range(NG):
                dve.wait_ge(yt_in[g % YT], 32 * (g // YT + 1))
                if g >= 2:
                    dve.wait_ge(o_ready, 2 * (g - 1))
                dve.tensor_tensor(fin[:, g % 2, :, :, :], n.t2[:, g, :, :, :], yt[:, g % YT, :, :, :],
                                  ALU.add).then_inc(summed, 1)

        @block.gpsimd
        def _(pool):
            for g in range(NQD):
                pool.wait_ge(y_full, g + 1)
                pool.wait_ge(idx_done, g + 1)
                for u in range(QUADS[g][2]):
                    pool.indirect_dma_start(n.y_tok, bass.IndirectOffsetOnAxis(ap=idx[:, g % YR, u:u + 1], axis=0),
                                            ye[:, g % YR, u, :], None, bounds_check=TOK - 1,
                                            oob_is_err=False).then_inc(sent[g % YR], 16)
            for k in range(YR):
                pool.wait_ge(sent[k], n_sent(k, NQD))


def kernel(x, L0_conv_w1, L0_conv_w2, L0_conv_w3, L0_conv_g1, L0_conv_b1, L0_conv_g2, L0_conv_b2, L0_conv_g3,
           L0_conv_b3, L1_attn_Wqkv, L1_attn_Wproj, L1_attn_bproj, L1_ffn_gate_w, L1_ffn_gate_b, L1_ffn_w1,
           L1_ffn_b1, L1_ffn_w2, L1_ffn_b2):
    import numpy as _np
    import concourse.bacc as _bacc
    from concourse import mybir as _mybir
    from concourse.bass_utils import run_bass_kernel_spmd as _run

    a = _np.asarray
    arrays = {
        "x": a(x).reshape(NIMG, CIN, PIX),
        "w1": a(L0_conv_w1).reshape(CB, CIN).T,
        "w2": a(L0_conv_w2).transpose(1, 2, 3, 0).reshape(CB, 9, CB),
        "w3": a(L0_conv_w3).reshape(CIN, CB).T,
        "gb12": _np.stack([a(v).reshape(CB) for v in (L0_conv_g1, L0_conv_b1, L0_conv_g2, L0_conv_b2)], 1),
        "g3": a(L0_conv_g3).reshape(1, CIN),
        "b3": a(L0_conv_b3).reshape(1, CIN),
        "w_qkv": a(L1_attn_Wqkv),
        "w_proj": a(L1_attn_Wproj),
        "b_proj": a(L1_attn_bproj).reshape(1, CIN),
        "gate_w": a(L1_ffn_gate_w),
        "gate_bias": a(L1_ffn_gate_b).reshape(1, E),
        "e_w1": a(L1_ffn_w1),
        "e_b1": a(L1_ffn_b1).reshape(1, E * F),
        "e_w2": a(L1_ffn_w2),
        "e_b2": a(L1_ffn_b2).reshape(1, E * CIN),
    }
    arrays = {k: _np.ascontiguousarray(v) for k, v in arrays.items()}
    nc = _bacc.Bacc("TRN2", target_bir_lowering=False, num_devices=1)
    aps = {k: nc.dram_tensor(f"in_{k}", v.shape, _mybir.dt.from_np(v.dtype), kind="ExternalInput").ap()
           for k, v in arrays.items()}
    aps["out"] = nc.dram_tensor("out_0", (NIMG, CIN, PIX), F32, kind="ExternalOutput").ap()
    build(nc, aps)
    r = _run(nc, [{f"in_{k}": v for k, v in arrays.items()}], core_ids=[0])
    return r.results[0]["out_0"].reshape(NIMG, CIN, H, W)
```

```python
from contextlib import ExitStack

import concourse.bass as bass
from concourse import mybir

ALU = mybir.AluOpType
ACT = mybir.ActivationFunctionType
AX = mybir.AxisListType
F32 = mybir.dt.float32
BF16 = mybir.dt.bfloat16
F16 = mybir.dt.float16
I32 = mybir.dt.int32

P = 128
NIMG, CIN, H, W = 16, 64, 56, 56
PIX = H * W
TOK = NIMG * PIX
CB = 16
NQ = 4
HC = 448
RPC = HC // W
NCH = 2 * PIX // HC
HEADS, HD, WIN, RADIUS = 4, 16, 64, 32
SCALE = HD ** -0.5
NEG = -1e30
VW = HD + 1
NB = 7
GT = 2 * NB
GW = NB * P
NG = TOK // (GT * P)
E, F = 8, 256
CAP = -(-5 * TOK // (4 * E))
TPE = -(-CAP // (2 * P)) * 2
ES = TPE * P
SLOTS = E * ES
NOWHERE = 1048576.0
ROW = CIN + 2
RP, RI = CIN, CIN + 1
CHUNKS = ((0, 4), (4, 3))
BN_EPS = LN_EPS = 1e-5


def pieces(start, length):
    out, at = [], 0
    while at < length:
        image, pixel = divmod(start + at, PIX)
        n = min(length - at, PIX - pixel)
        out.append((image, pixel, at, n))
        at += n
    return out


def spread(a, axis, count):
    a = a.unsqueeze(axis)
    shape = list(a.shape)
    shape[axis] = count
    return a.broadcast_to(shape)


ARRAYS = ("x", "w1", "w2", "w3", "w3n", "gb12", "gb3", "w_qkv", "w_proj", "b_proj", "gate_w", "gate_bias",
          "e_w1", "e_w2", "e_b", "out")


class Net:

    def __init__(self, a):
        (self.x, self.w1, self.w2, self.w3, self.w3n, self.gb12, self.gb3, self.w_qkv, self.w_proj, self.b_proj,
         self.gate_w, self.gate_bias, self.e_w1, self.e_w2, self.e_b, self.out) = (a[k] for k in ARRAYS)


def conv_stage(nc, n):
    with ExitStack() as ctx:
        def sb(name, shape, dt=F32):
            return ctx.enter_context(nc.sbuf_tensor(name, shape, dt))

        def sem(name):
            return ctx.enter_context(nc.semaphore(name))

        XR = 3
        xc = sb("xc", [P, XR, NQ, HC])
        xs = sb("xs", [P, 2, NQ, HC], BF16)
        y = sb("y", [P, NCH, HC], BF16)
        sp_ = sb("signs_padded", [P, 2, H + 2, W + 2], BF16)
        s2 = sb("s2", [P, NCH * HC], BF16)
        s2T = sb("s2T", [P, 2, NB, P], BF16)
        w1f = sb("w1f", [P, 32])
        w1s = sb("w1s", [P, 32], BF16)
        w2f = sb("w2f", [P, 9, CB])
        w2g = sb("w2g", [P, 9, CB], BF16)
        w2s = sb("w2s", [P, 9, P], BF16)
        w3f = sb("w3f", [P, CIN])
        w3s = sb("w3s", [P, CIN])
        gb = sb("gb", [P, 4])
        gb3 = sb("gb3", [CIN, 2])
        w3c = sb("w3c", [CIN, 2, CB])
        w3cs = sb("w3cs", [CIN, 2 * CB])
        w3col = sb("w3col", [CIN, 33])
        c3 = sb("c3", [CIN, 8])
        same = sb("same_channel", [P, P])
        pi = sb("pi", [P, P])
        pj = sb("pj", [P, 1])
        blk = sb("same_group", [P, P])
        st = sb("st", [P, NCH, 6])
        agg = sb("agg", [P, 2])
        mom = sb("mom", [P, 2])
        mv = sb("mv", [P, 6])
        ab = sb("ab", [P, 2])
        s2sum = sb("s2sum", [P, NCH])
        s2tot = sb("s2tot", [P, 1])
        gram = sb("gram", [P, P])
        t1 = sb("t1", [P, CIN])
        t3 = sb("t3", [P, CIN])
        part_b = sb("part_b", [33, 3, CIN], BF16)
        masked = sb("w3_masked", [33, 3, P], BF16)
        rest = sb("w3_rest", [33, 2, CIN])
        ones = sb("ones", [P, 1])
        junk = sb("empty_rows", [P, 16, ROW])
        c1 = sb("c1", [P, 3, P])
        brow = sb("brow", [1, 2, P])
        bpart = sb("bpart", [1, 3, P], BF16)
        pmod = sb("pmod", [P, 1])
        ps = [ctx.enter_context(nc.psum_tensor(f"cps{i}", [P, 512], F32)) for i in range(4)]
        psT = [ctx.enter_context(nc.psum_tensor(f"cpt{i}", [P, NB * P], BF16)) for i in range(2)]
        psG = ctx.enter_context(nc.psum_tensor("cpg", [P, 512], F32))
        psS = ctx.enter_context(nc.psum_tensor("cpsm", [P, 512], F32))

        xin = [sem(f"x_in{i}") for i in range(XR)]
        w_in, zeroed, iot, cst = sem("w_in"), sem("w_zeroed"), sem("iota_done"), sem("consts")
        w_signs, x_signs, conv_done, y_done = sem("w_signs"), sem("x_signs"), sem("conv_done"), sem("y_done")
        bn_step, bn_pow, bn_mm, act_sign = sem("bn_step"), sem("bn_pow"), sem("bn_mm"), sem("act_sign")
        tr, trc, gdone, s2_out, init = sem("s2_transposed"), sem("s2T_done"), sem("gram_done"), sem("s2_out"), sem("init")
        pconst = sem("pool_const")
        tail = sem("tail")
        z, s, d, moved = sem("k_memsets"), sem("k_selects"), sem("bias_step"), sem("k_moved")
        w3_done = sem("w3_done")
        w2_in, brow_in = sem("w2_in"), sem("brow_in")
        block = ctx.enter_context(nc.Block())

        MEMSETS = [(n.ident[:, :], 0.0), (n.ident_b[:, :], 0.0), (n.ident_h[:, :], 0.0), (n.mhalf[:, :], -0.5),
                   (n.mask[:, :, :], 0.0), (n.hmask[:, :], 1.0), (n.tri[:, :], 1.0), (n.ones_b[:, :], 1.0),
                   (n.pcol[:, :], 1.0), (n.jmask[:, :], 1.0), (n.wqkv[:, :, :], 0.0), (n.wp[:, :], 0.0),
                   (n.gate[:, :], 0.0), (n.ones3[:, :], 1.0)]

        def parts_of_bias(dve):
            dve.wait_ge(brow_in, 32)
            k = 0
            for part in range(3):
                for ins in (lambda: dve.tensor_copy(bpart[:, part, :], brow[:, 0, :]),
                            lambda: dve.tensor_tensor(brow[:, 1, :], brow[:, 0, :], bpart[:, part, :], ALU.subtract),
                            lambda: dve.tensor_copy(brow[:, 0, :], brow[:, 1, :])):
                    k += 1
                    ins().then_inc(d, 1)
                    dve.wait_ge(d, k)

        def const_loads(sp):
            sp.wait_ge(z, len(MEMSETS))
            for j in range(2):
                r = slice(64 * j, 64 * j + 64)
                sp.dma_start(n.wqkv[r, :, r], n.w_qkv.rearrange("c (k d) -> c k d", k=3)).then_inc(moved, 16)
                sp.dma_start(n.wp[r, r], n.w_proj).then_inc(moved, 16)
                sp.dma_start(n.gate[r, E * j:E * j + E], n.gate_w).then_inc(moved, 16)
            sp.dma_start(n.gate_b[:, :], n.gate_bias.broadcast_to([P, n.gate_bias.shape[1]])).then_inc(moved, 16)
            sp.wait_ge(d, 9)
            for part in range(3):
                sp.dma_start(n.bp[part:part + 1, :], bpart[:, part, :]).then_inc(moved, 16)

        def constants(pool):
            def select(out, pattern, op, base, mult, fill):
                select.k += 1
                pool.affine_select(out=out, in_=out, compare_op=op, fill=fill, base=base, pattern=pattern,
                                   channel_multiplier=mult).then_inc(s, 1)
                pool.wait_ge(s, select.k)
            select.k = 0
            for t, v in MEMSETS:
                pool.memset(t, v).then_inc(z, 1)
            pool.wait_ge(z, len(MEMSETS))
            for t in (n.ident, n.ident_b, n.ident_h):
                select(t[:, :], [[-1, P]], ALU.not_equal, 0, 1, 1.0)
            for w in range(2):
                m = n.mask[64 * w:64 * w + 64, :, :]
                select(m, [[0, HEADS], [-1, WIN]], ALU.is_ge, 0, 1, NEG)
                select(m, [[0, HEADS], [1, WIN]], ALU.is_ge, RADIUS, -1, NEG)
            for j in range(2):
                m = n.hmask[64 * j:64 * j + 64, :]
                select(m, [[-HD, HEADS]], ALU.is_ge, 0, 1, 0.0)
                select(m, [[HD, HEADS]], ALU.is_ge, HD - 1, -1, 0.0)
            select(n.jmask[:, 0:1], [[0, 1]], ALU.is_ge, 63, -1, 0.0)
            select(n.jmask[:, 1:2], [[0, 1]], ALU.is_ge, -64, 1, 0.0)
            select(n.tri[:, :], [[1, P]], ALU.is_gt, 0, -1, 0.0)
            select(n.pcol[:, 0:1], [[0, 1]], ALU.is_ge, CB - 1, -1, 0.0)
            select(n.pcol[:, 0:1], [[0, 1]], ALU.not_equal, -32, 1, 1.0)
            select(n.pcol[:, 1:2], [[0, 1]], ALU.is_ge, -CB, 1, 0.0)
            select(n.pcol[:, 1:2], [[0, 1]], ALU.is_ge, 32, -1, 0.0)
            pool.iota(n.em8[:, :], [[1, E]], base=-E, channel_multiplier=0,
                      allow_small_or_imprecise_dtypes=True).then_inc(s, 1)
            pool.wait_ge(s, select.k + 1)

        @block.sync
        def _(sp):
            for c in range(NCH):
                if c >= XR:
                    sp.wait_ge(x_signs, c - XR + 1)
                image, pixel = divmod(c * HC, PIX)
                for j in range(2):
                    sp.dma_start(xc[64 * j:64 * j + 64, c % XR, :, :],
                                 n.x.rearrange("(q j i) c p -> j i c q p", q=NQ, j=2)[j, image, :, :, pixel:pixel + HC]
                                 ).then_inc(xin[c % XR], 16)
                if c == 0:
                    for j in range(2):
                        sp.dma_start(brow[:, 0, 64 * j:64 * j + 64], n.b_proj).then_inc(brow_in, 16)
                    sp.wait_ge(zeroed, 1)
                    for j in range(2):
                        sp.dma_start(w1f[64 * j:64 * j + 64, 16 * j:16 * j + 16], n.w1).then_inc(w_in, 16)
                if c == 2:
                    for k in range(8):
                        r = slice(16 * k, 16 * k + 16)
                        sp.dma_start(w2f[r, :, :], n.w2).then_inc(w2_in, 16)
                if c == 3:
                    for k in range(8):
                        r = slice(16 * k, 16 * k + 16)
                        sp.dma_start(gb[r, :], n.gb12).then_inc(w2_in, 16)
                if c == 4:
                    for k in range(8):
                        r = slice(16 * k, 16 * k + 16)
                        sp.dma_start(w3f[r, :], n.w3).then_inc(w2_in, 16)
                    for j in range(2):
                        sp.dma_start(w3c[:, j, :], n.w3n).then_inc(w2_in, 16)
                    sp.dma_start(gb3[:, :], n.gb3).then_inc(w2_in, 16)
                if c == 5:
                    const_loads(sp)
            sp.wait_ge(pconst, 4)
            for k in range(SLOTS // (P * 16)):
                sp.dma_start(n.slots[k * P * 16:(k + 1) * P * 16, :].rearrange("(p r) d -> p (r d)", p=P),
                             junk[:, :, :].rearrange("p r d -> p (r d)")).then_inc(init, 16)
            n_init = SLOTS // (P * 16)
            for q in range(2):
                sp.wait_ge(act_sign, 2 + 7 * (q + 1))
                w = slice(q * PIX, (q + 1) * PIX)
                for i in range(8):
                    sp.dma_start(n.s2_dram[2 * i + q, :, :], s2[16 * i:16 * i + 16, w]).then_inc(s2_out, 16)
            sp.wait_ge(w3_done, 1)
            for part in range(3):
                sp.dma_start(n.w3p[32 * part:32 * part + 32, :], masked[0:32, part, :]).then_inc(moved, 16)
                sp.dma_start(n.w3p[96 + part:97 + part, :], masked[32:33, part, :]).then_inc(moved, 16)
            sp.wait_ge(s2_out, 16 * 16)
            sp.wait_ge(moved, 16 * 16)
            sp.wait_ge(init, 16 * n_init)

        @block.gpsimd
        def _(pool):
            pool.memset(w1f[:, :], 0.0).then_inc(zeroed, 1)
            pool.memset(junk[:, :, :], 0.0).then_inc(pconst, 1)
            pool.memset(sp_[:, :, :, :], 0.0).then_inc(pconst, 1)
            pool.wait_ge(pconst, 2)
            pool.memset(junk[:, :, RI:RI + 1], NOWHERE).then_inc(pconst, 1)
            pool.memset(ones[:, :], 1.0).then_inc(pconst, 1)
            constants(pool)
            pool.iota(c1[:, 0, :], [[0, 8], [1, 16]], base=0, channel_multiplier=0,
                      allow_small_or_imprecise_dtypes=True).then_inc(iot, 1)
            pool.iota(c1[:, 1, :], [[1, 8], [0, 16]], base=0, channel_multiplier=0,
                      allow_small_or_imprecise_dtypes=True).then_inc(iot, 1)
            pool.iota(pj[:, :], [[0, 1]], base=0, channel_multiplier=1,
                      allow_small_or_imprecise_dtypes=True).then_inc(iot, 1)
            for k in range(3):
                pool.wait_ge(bn_step, (4, 10, 19)[k])
                v = mv[:, 2:4] if k < 2 else c3[:, 2:4]
                pool.tensor_tensor(v[:, 1:2], v[:, 0:1], n.mhalf[0:v.shape[0], 0:1], ALU.pow).then_inc(bn_pow, 1)

        @block.tensor
        def _(pe):
            pe.wait_ge(w_signs, 1)
            for c in range(NCH):
                pe.wait_ge(x_signs, c + 1)
                if c >= 2:
                    pe.wait_ge(y_done, c - 1)
                for q in range(NQ):
                    mm = pe.matmul(ps[c % 2][32 * q:32 * q + 32, 0:HC], w1s[:, :], xs[:, c % 2, q, :],
                                   start=True, stop=True)
                mm.then_inc(conv_done, 1)
            pe.wait_ge(cst, 2)
            pe.wait_ge(bn_step, 2)
            pe.matmul(psS[:, 0:2], same[:, :], mom[:, :], start=True, stop=True).then_inc(bn_mm, 1)
            pe.wait_ge(cst, 3)
            for c in range(NCH):
                pe.wait_ge(act_sign, 1 + (1 if c < 7 else 2) - 1)
                pe.wait_ge(y_done, NCH + max(c - 1, 0))
                for k in range(9):
                    dy, dx = divmod(k, 3)
                    i, r = divmod(c * RPC, H)
                    mm = pe.matmul(ps[c % 2][:, 0:HC], w2s[:, k, :], sp_[:, i, r + dy:r + dy + RPC, dx:dx + W],
                                   start=(k == 0), stop=(k == 8))
                mm.then_inc(conv_done, 1)
            pe.wait_ge(bn_step, 8)
            pe.matmul(psS[:, 2:4], same[:, :], mom[:, :], start=True, stop=True).then_inc(bn_mm, 1)

            def transposes(g):
                pe.wait_ge(act_sign, 2 + 2 * g + 2)
                if g >= 2:
                    pe.wait_ge(trc, g - 1)
                for b in range(NB):
                    mm = pe.transpose(psT[g % 2][:, b * P:(b + 1) * P], s2[:, (g * NB + b) * P:(g * NB + b + 1) * P],
                                      n.ident_b[:, :])
                mm.then_inc(tr, 1)

            transposes(0)
            for g in range(NB):
                if g + 1 < NB:
                    transposes(g + 1)
                pe.wait_ge(trc, g + 1)
                for b in range(NB):
                    mm = pe.matmul(psG[:, 0:P], s2T[:, g % 2, b, :], s2T[:, g % 2, b, :],
                                   start=(g == 0 and b == 0), stop=(g == NB - 1 and b == NB - 1))
                mm.then_inc(gdone, 1)
            pe.wait_ge(bn_step, 13)
            pe.matmul(psS[:, 64:128], gram[:, :], w3s[:, :], start=True, stop=True).then_inc(bn_mm, 1)
            pe.wait_ge(bn_step, 15)
            pe.matmul(psS[0:CIN, 128:129], t1[:, :], ones[:, :], start=True, stop=True)
            pe.matmul(psS[0:CIN, 129:130], t3[:, :], ones[:, :], start=True, stop=True).then_inc(bn_mm, 1)
            pe.wait_ge(bn_step, 23)
            pe.transpose(psS[0:33, 192:256], w3col[:, :], n.ident[0:CIN, 0:CIN]).then_inc(bn_mm, 1)

        @block.scalar
        def _(act):
            act.wait_ge(w_in, 32)
            act.activation(w1s[:, :], w1f[:, :], ACT.Sign).then_inc(w_signs, 1)
            for c in range(NCH):
                act.wait_ge(xin[c % XR], 32 * (c // XR + 1))
                if c >= 2:
                    act.wait_ge(conv_done, c - 1)
                act.activation(xs[:, c % 2, :, :], xc[:, c % XR, :, :], ACT.Sign).then_inc(x_signs, 1)
                if c == 8:
                    act.wait_ge(w2_in, 16 * 27)
                    act.activation(w2g[:, :, :], w2f[:, :, :], ACT.Sign).then_inc(w_signs, 1)
                    act.activation(w3s[:, :], w3f[:, :], ACT.Sign).then_inc(w_signs, 1)
                    act.activation(w3cs[:, :], w3c[:, :, :].rearrange("p j c -> p (j c)"), ACT.Sign).then_inc(w_signs, 1)
            act.wait_ge(pconst, 2)
            act.wait_ge(bn_step, 6)
            for i in range(2):
                act.activation(sp_[:, i, 1:H + 1, 1:W + 1],
                               y[:, 7 * i:7 * i + 7, :].rearrange("p c (r w) -> p (c r) w", w=W),
                               ACT.Sign, bias=ab[:, 1:2], scale=ab[:, 0:1]).then_inc(act_sign, 1)
            act.wait_ge(bn_step, 12)
            for c in range(NCH):
                act.activation(s2[:, c * HC:(c + 1) * HC], y[:, c, :], ACT.Sign, bias=ab[:, 1:2], scale=ab[:, 0:1],
                               accum_out=s2sum[:, c:c + 1]).then_inc(act_sign, 1)

        @block.vector
        def _(dve):
            step = [0]

            def link(ins):
                step[0] += 1
                ins.then_inc(bn_step, 1)
                dve.wait_ge(bn_step, step[0])

            dve.wait_ge(iot, 3)
            k = [0]

            def local(ins):
                k[0] += 1
                ins.then_inc(tail, 1)
                dve.wait_ge(tail, k[0])

            local(dve.tensor_scalar(blk[:, :], c1[:, 1, :], 16.0, None, ALU.mult))
            local(dve.tensor_scalar(pi[:, :], blk[:, :], pj[:, 0:1], -1.0, ALU.subtract, ALU.mult))
            local(dve.tensor_scalar(blk[:, :], pi[:, :], 15.5, None, ALU.is_lt))
            local(dve.scalar_tensor_tensor(blk[:, :], pi[:, :], -0.5, blk[:, :], ALU.is_gt, ALU.mult))
            local(dve.tensor_tensor(pi[:, :], pi[:, :], blk[:, :], ALU.mult))
            local(dve.tensor_reduce(pmod[:, :], pi[:, :], AX.X, ALU.add))
            local(dve.tensor_scalar(pmod[:, :], pmod[:, :], 1.0 / 16, None, ALU.mult))
            dve.tensor_scalar(same[:, :], c1[:, 0, :], pmod[:, 0:1], 0.125, ALU.is_equal, ALU.mult).then_inc(cst, 1)
            dve.memset(t1[:, :], 0.0).then_inc(cst, 1)
            parts_of_bias(dve)

            for conv in range(2):
                for c in range(NCH):
                    dve.wait_ge(conv_done, NCH * conv + c + 1)
                    if conv and c == 0:
                        dve.wait_ge(act_sign, 2)
                    if not conv and c == 10:
                        dve.wait_ge(w_signs, 2)
                        dve.tensor_tensor(w2s[:, :, :].rearrange("p k (g c) -> p k g c", c=CB), spread(w2g[:, :, :], 2, 8),
                                          spread(blk[:, :].rearrange("p (g c) -> p g c", c=CB), 1, 9),
                                          ALU.mult).then_inc(cst, 1)
                    dve.bn_stats(st[:, c, :], ps[c % 2][:, 0:HC]).then_inc(tail, 1)
                    dve.tensor_copy(y[:, c, :], ps[c % 2][:, 0:HC]).then_inc(y_done, 1)
                k[0] += NCH
                dve.wait_ge(tail, k[0])
                link(dve.bn_aggr(agg[:, :], st[:, :, :]))
                local(dve.tensor_tensor(mv[:, 5:6], agg[:, 0:1], agg[:, 0:1], ALU.mult))
                local(dve.tensor_copy(mom[:, 0:1], agg[:, 0:1]))
                link(dve.tensor_tensor(mom[:, 1:2], agg[:, 1:2], mv[:, 5:6], ALU.add))
                dve.wait_ge(bn_mm, conv + 1)
                local(dve.tensor_copy(mv[:, 0:2], psS[:, 2 * conv:2 * conv + 2]))
                local(dve.tensor_tensor(mv[:, 4:5], mv[:, 0:1], mv[:, 0:1], ALU.mult))
                link(dve.tensor_tensor(mv[:, 2:3], mv[:, 1:2], mv[:, 4:5], ALU.subtract))
                link(dve.tensor_scalar(mv[:, 2:3], mv[:, 2:3], BN_EPS, None, ALU.add))
                dve.wait_ge(bn_pow, conv + 1)
                if conv:
                    dve.wait_ge(act_sign, 2)
                link(dve.tensor_tensor(ab[:, 0:1], mv[:, 3:4], gb[:, 2 * conv:2 * conv + 1], ALU.mult))
                local(dve.tensor_tensor(mv[:, 5:6], ab[:, 0:1], mv[:, 0:1], ALU.mult))
                link(dve.tensor_tensor(ab[:, 1:2], gb[:, 2 * conv + 1:2 * conv + 2], mv[:, 5:6], ALU.subtract))
            for g in range(NB):
                dve.wait_ge(tr, g + 1)
                if g >= 2:
                    dve.wait_ge(gdone, g - 1)
                dve.tensor_copy(s2T[:, g % 2, :, :].rearrange("p b t -> p (b t)"), psT[g % 2][:, :]).then_inc(trc, 1)
            dve.wait_ge(gdone, NB)
            dve.wait_ge(w_signs, 4)
            dve.wait_ge(act_sign, 2 + NCH)
            local(dve.tensor_reduce(s2tot[:, :], s2sum[:, :], AX.X, ALU.add))
            link(dve.tensor_tensor(gram[:, :], psG[:, 0:P], blk[:, :], ALU.mult))
            dve.wait_ge(bn_mm, 3)
            link(dve.tensor_tensor(t1[:, :], psS[:, 64:128], w3s[:, :], ALU.mult))
            link(dve.tensor_scalar(t3[:, :], w3s[:, :], s2tot[:, 0:1], None, ALU.mult))
            dve.wait_ge(bn_mm, 4)
            link(dve.tensor_scalar(c3[:, 0:1], psS[0:CIN, 129:130], 1.0 / TOK, None, ALU.mult))
            link(dve.tensor_tensor(c3[:, 1:2], c3[:, 0:1], c3[:, 0:1], ALU.mult))
            link(dve.scalar_tensor_tensor(c3[:, 4:5], psS[0:CIN, 128:129], 1.0 / TOK, c3[:, 1:2],
                                          ALU.mult, ALU.subtract))
            link(dve.tensor_scalar(c3[:, 2:3], c3[:, 4:5], BN_EPS, None, ALU.add))
            dve.wait_ge(bn_pow, 3)
            link(dve.tensor_tensor(c3[:, 5:6], c3[:, 3:4], gb3[:, 0:1], ALU.mult))
            link(dve.tensor_tensor(c3[:, 6:7], c3[:, 5:6], c3[:, 0:1], ALU.mult))
            link(dve.tensor_tensor(w3col[:, 32:33], gb3[:, 1:2], c3[:, 6:7], ALU.subtract))
            link(dve.tensor_scalar(w3col[:, 0:32], w3cs[:, :], c3[:, 5:6], None, ALU.mult))
            dve.wait_ge(bn_mm, 5)
            link(dve.tensor_copy(rest[:, 0, :], psS[0:33, 192:256]))
            for part in range(3):
                link(dve.tensor_copy(part_b[:, part, :], rest[:, part % 2, :]))
                if part < 2:
                    link(dve.tensor_tensor(rest[:, 1 - part % 2, :], rest[:, part % 2, :], part_b[:, part, :],
                                           ALU.subtract))
            for part in range(3):
                for j in range(2):
                    ins = dve.tensor_scalar(masked[:, part, CIN * j:CIN * j + CIN], part_b[:, part, :],
                                            n.pcol[0:33, j:j + 1], None, ALU.mult)
            ins.then_inc(w3_done, 1)


def build(nc, a):
    with ExitStack() as ctx:
        def sb(name, shape, dt=F32):
            return ctx.enter_context(nc.sbuf_tensor(name, shape, dt))

        def sem(name):
            return ctx.enter_context(nc.semaphore(name))

        n = Net(a)
        n.slots = nc.dram_tensor("slots", (SLOTS, ROW), F32, kind="Internal").ap()
        n.y_tok = nc.dram_tensor("y_tok", (TOK, CIN), F32, kind="Internal").ap()
        n.s2_dram = nc.dram_tensor("s2_dram", (NIMG, CB, PIX), BF16, kind="Internal").ap()
        n.ident = sb("ident", [P, P])
        n.ident_b = sb("ident_b", [P, P], BF16)
        n.ident_h = sb("ident_h", [P, P], F16)
        n.mhalf = sb("minus_half", [P, GT])
        n.pcol = sb("pcol", [P, 2])
        n.w3p = sb("w3p", [99, P], BF16)
        n.mask = sb("mask", [P, HEADS, WIN], BF16)
        n.hmask = sb("hmask", [P, HEADS])
        n.jmask = sb("jmask", [P, 2])
        n.wqkv = sb("wqkv", [P, 3, P])
        n.wp = sb("wp", [P, P])
        n.gate = sb("gate", [P, 2 * E])
        n.bp = sb("bp", [3, P], BF16)
        n.ones3 = sb("ones3", [3, P], BF16)
        n.gate_b = sb("gate_b", [P, E])
        n.tri = sb("tri", [P, P], BF16)
        n.ones_b = sb("ones_b", [P, P], BF16)
        n.counts = sb("counts", [1, E], I32)
        n.em8 = sb("em8", [P, E])
        n.t2 = sb("t2", [P, NG, NB, 2, CIN])
        conv_stage(nc, n)
        attention_stage(nc, n)
        expert_stage(nc, n)


ORDER = ("v0", "v1", "zt0", "zt1", "rank", "xt0", "xt1", "gate", "ot0", "ot1", "q0", "q1", "pr0", "k0", "pr1", "k1",
         "t0", "t1")
OFFSET = {"v": 0, "rank": -3, "zt": -2, "gate": -2, "xt": 1, "ot": -1, "q": 1, "pr": -1, "k": 1, "t": 2}


def attention_stage(nc, n):
    with ExitStack() as ctx:
        def sb(name, shape, dt=F32):
            return ctx.enter_context(nc.sbuf_tensor(name, shape, dt))

        def sem(name):
            return ctx.enter_context(nc.semaphore(name))

        xg = sb("xg", [P, GW])
        s2g = sb("s2g", [99, GW], BF16)
        xn = sb("xn", [P, NB, 2, CIN])
        zn = sb("zn", [P, NB, 2, CIN])
        xrow = sb("xrow", [P, 2, NB, 2, ROW])
        xnT = sb("xnT", [P, GW])
        actT = sb("actT", [P, GW])
        qT = sb("qT", [P, 2, 2, GW])
        kx = sb("kx", [P, 2, HEADS, GW])
        vs = sb("vs", [P, NB, 2, 2, 2, HD])
        vw = sb("vw", [P, NB, 2, 2, 2, HD])
        vb = sb("vb", [P, 2, NB, 2, 2, 2, VW])
        ZR = 4
        PR, OR = 3, 10
        zeros = sb("zeros", [P, ZR * CIN])
        pb = sb("pb", [P, PR, 2, HEADS, WIN])
        pT = sb("pT", [P, 2, 4, P])
        ob = sb("ob", [P, OR, 2 * HEADS, HD])
        mx = sb("mx", [P, 2, 2 * HEADS])
        rl = sb("rl", [P, 2, 2 * HEADS])
        bx = sb("bx", [P, NB, 2, 6])
        sx = sb("sx", [P, 6, GT])
        sz = sb("sz", [P, 6, GT])
        lg = sb("lg", [P, GT, E])
        lw = sb("lw", [P, 2, GT, E])
        among, sd = (lw[:, k, :, :].rearrange("p t e -> p (t e)").rearrange("p (e t) -> p e t", e=E) for k in range(2))
        rt = sb("rt", [P, 6, GT])
        oh = sb("oh", [P, GT, E], BF16)
        ohf = sb("ohf", [P, GT, E])
        cnt = sb("cnt", [P, E, GT])
        inc = sb("inc", [P, E, GT])
        notfirst = sb("notfirst", [P, E, GT])
        carry = sb("carry", [P, E])
        ids = sb("ids", [P, NB, 2])
        dest = sb("dest", [P, 2, NB, 2], I32)
        S = [ctx.enter_context(nc.psum_tensor(f"S{i}", [P, 512], F32)) for i in range(2)]
        PT = ctx.enter_context(nc.psum_tensor("PT", [P, 512], F32))
        O = [ctx.enter_context(nc.psum_tensor(f"O{i}", [P, 512], F32)) for i in range(2)]
        M = [ctx.enter_context(nc.psum_tensor(f"M{i}", [P, 512], F32)) for i in range(3)]

        x_in, s_in, const = sem("x_in"), sem("s_in"), sem("a_const")
        s_ready, s_max, s_sub, s_exp = sem("s_ready"), sem("s_max"), sem("s_sub"), sem("s_exp")
        pt_ready, pt_copied, o_ready, o_recip, o_done = (sem("pt_ready"), sem("pt_copied"), sem("o_ready"),
                                                         sem("o_recip"), sem("o_done"))
        ready = {op: sem(f"{op}_ready") for op in ("t", "rank", "ot", "xt", "pr", "q", "k", "v", "zt", "gate")}
        taken = {op: sem(f"{op}_taken") for op in ("t", "rank", "ot", "xt", "pr", "q", "k", "v", "zt", "gate")}
        ln = {(w, k): sem(f"{w}_{k}") for w in ("x", "z") for k in ("mean", "var", "rstd", "norm")}
        cleared, counted = sem("cleared"), sem("counted")
        stat_step, centered = sem("stat_step"), sem("centered")
        v_sw, v_built = sem("v_swapped"), sem("v_built")
        logit, r_step, r_exp, ranked, ids_step, scat = (sem("logit"), sem("r_step"), sem("r_exp"), sem("ranked"),
                                                        sem("ids_step"), [sem("scattered0"), sem("scattered1")])
        rank_q, numbered = sem("rank_wanted"), sem("numbered")
        high, low = sem("high_parts"), sem("low_parts")
        block = ctx.enter_context(nc.Block())

        NBLK = NG * NB
        BODIES = range(-2, NG + 3)
        Z_ROWS = 4 * ZR * P
        R_STEPS = 19

        def real(g):
            return 0 <= g < NG

        def chunk(c):
            b0, nb = CHUNKS[c]
            return b0, nb, nb * P

        plan, last = {}, [None, None, None]
        turn = 0
        for i in BODIES:
            for op in ORDER:
                kind = op.rstrip("01")
                g = i + OFFSET[kind]
                if not real(g):
                    continue
                bank = turn % 3
                turn += 1
                plan[(op, g)] = (bank, last[bank])
                last[bank] = (kind, g + 1) if op == kind else (kind, 2 * g + int(op[-1]) + 1)

        def bank_of(op, g):
            return M[plan[(op, g)][0]]

        def swap(sp, g):
            sp.wait_ge(taken["v"], 2 * g + 2)
            if g >= 1:
                sp.wait_ge(v_built, 4 * g)
            for w in range(2):
                sp.dma_start(vw[64 * w:64 * w + 64, :, :, :, :, :].rearrange("p b j r h d -> p (b j r h d)"),
                             vs[64 - 64 * w:128 - 64 * w, :, :, :, :, :].rearrange("p b j r h d -> p (b j r h d)")
                             ).then_inc(v_sw, 16)

        @block.sync
        def _(sp):
            def load(g):
                if g >= 1:
                    sp.wait_ge(ready["t"], 2 * g)
                for j in range(2):
                    for image, pixel, at, m in pieces((2 * g + j) * GW, GW):
                        sp.dma_start(xg[64 * j:64 * j + 64, at:at + m], n.x[image, :, pixel:pixel + m]).then_inc(x_in, 16)
                        for part in range(3):
                            sp.dma_start(s2g[32 * part + 16 * j:32 * part + 16 * j + 16, at:at + m],
                                         n.s2_dram[image, :, pixel:pixel + m]).then_inc(s_in, 16)

            load(0)
            load(1)
            for g in range(NG):
                if g + 2 < NG:
                    load(g + 2)
                swap(sp, g)
                if g == 0:
                    sp.wait_ge(const, 5)
                k = g * Z_ROWS
                if k < TOK:
                    m = min(Z_ROWS, TOK - k) // (ZR * P)
                    sp.dma_start(n.y_tok[k:k + m * ZR * P, :].rearrange("(p m r) d -> p m (r d)", p=P, m=m),
                                 spread(zeros[:, :], 1, m)).then_inc(cleared, 16)
            sp.wait_ge(cleared, 16 * -(-TOK // Z_ROWS))

        n_pieces = [sum(len(pieces((2 * g + j) * GW, GW)) for j in range(2)) for g in range(NG)]

        def loaded(eng, g):
            eng.wait_ge(x_in, 16 * sum(n_pieces[:g + 1]))
            eng.wait_ge(s_in, 48 * sum(n_pieces[:g + 1]))

        @block.tensor
        def _(pe):
            def free(op, g):
                before = plan[(op, g)][1]
                if before:
                    pe.wait_ge(taken[before[0]], before[1])
                return bank_of(op, g)

            def t(g, c):
                b0, nb, w = chunk(c)
                bank = free(f"t{c}", g)
                if c == 0:
                    loaded(pe, g)
                    pe.wait_ge(const, 3)
                for b in range(nb):
                    cols = slice((b0 + b) * P, (b0 + b + 1) * P)
                    out = bank[:, b * P:(b + 1) * P]
                    pe.matmul(out, xg[:, cols], n.ident[:, :], start=True, stop=False)
                    mm = pe.matmul(out, s2g[:, cols], n.w3p[:, :], start=False, stop=True)
                mm.then_inc(ready["t"], 1)

            def transposed(op, src, g, c, wait):
                b0, nb, w = chunk(c)
                bank = free(f"{op}{c}", g)
                if c == 0:
                    wait()
                for b in range(nb):
                    mm = pe.transpose(bank[:, b * P:(b + 1) * P], src(b0 + b), n.ident[:, :])
                mm.then_inc(ready[op], 1)

            def qk(g, c, which):
                b0, nb, w = chunk(c)
                bank = free(f"{'qk'[which]}{c}", g)
                pe.wait_ge(taken["xt"], 2 * g + c + 1)
                pe.matmul(bank[:, 0:w], n.wqkv[:, which, :], xnT[:, b0 * P:b0 * P + w],
                          start=True, stop=True).then_inc(ready["qk"[which]], 1)

            def v(g, c):
                b0, nb, w = chunk(c)
                bank = free(f"v{c}", g)
                pe.wait_ge(taken["xt"], 2 * g + c + 1)
                for b in range(nb):
                    mm = pe.matmul(bank[:, b * P:(b + 1) * P], xnT[:, (b0 + b) * P:(b0 + b + 1) * P], n.wqkv[:, 2, :],
                                   start=True, stop=True)
                mm.then_inc(ready["v"], 1)

            def pr(g, c):
                b0, nb, w = chunk(c)
                bank = free(f"pr{c}", g)
                pe.wait_ge(taken["ot"], 2 * g + c + 1)
                pe.matmul(bank[:, 0:w].rearrange("p (b c) -> p b c", c=P), n.ones3[:, :], spread(n.bp[:, :], 1, nb),
                          start=True, stop=False, skip_group_check=True)
                for b in range(nb):
                    mm = pe.matmul(bank[:, b * P:(b + 1) * P], actT[:, (b0 + b) * P:(b0 + b + 1) * P], n.wp[:, :],
                                   start=False, stop=(b == nb - 1), skip_group_check=True)
                mm.then_inc(ready["pr"], 1)

            def gate(g):
                bank = free("gate", g)
                pe.wait_ge(taken["zt"], 2 * g + 2)
                for b in range(NB):
                    mm = pe.matmul(bank[:, b * 2 * E:(b + 1) * 2 * E], actT[:, b * P:(b + 1) * P], n.gate[:, :],
                                   start=True, stop=True)
                mm.then_inc(ready["gate"], 1)

            def rank(g):
                bank = free("rank", g)
                pe.wait_ge(rank_q, g + 1)
                flat = oh[:, :, :].rearrange("p t e -> p (t e)")
                pe.matmul(bank[:, 0:GT * E], n.tri[:, :], flat, start=True, stop=True)
                pe.matmul(bank[:, GT * E:2 * GT * E], n.ones_b[:, :], flat, start=True, stop=True)\
                    .then_inc(ready["rank"], 1)

            def scores(B):
                g, b = divmod(B, NB)
                for c in range(2):
                    if b == CHUNKS[c][0]:
                        pe.wait_ge(taken["q"], 2 * g + c + 1)
                        pe.wait_ge(taken["k"], 2 * g + c + 1)
                if B >= 2:
                    pe.wait_ge(s_sub, B - 1)
                bank = S[B % 2]
                pe.matmul(bank[:, :].rearrange("p (j n) -> p j n", j=2), n.ident_b[:, :],
                          spread(n.mask[:, :, :].rearrange("p h k -> p (h k)"), 1, 2),
                          start=True, stop=False, skip_group_check=True)
                for j in range(2):
                    for w in range(2):
                        cols = slice(b * P + 64 * w, b * P + 64 * w + 64)
                        mm = pe.matmul(bank[64 * w:64 * w + 64, 256 * j:256 * j + 256], qT[:, g % 2, j, cols],
                                       kx[:, g % 2, :, cols], start=False, stop=(j == 1), skip_group_check=True)
                mm.then_inc(s_ready, 1)

            def turn_probs(B):
                pe.wait_ge(s_exp, B + 1)
                if B >= 1:
                    pe.wait_ge(pt_copied, B)
                for j in range(2):
                    for r in range(2):
                        mm = pe.transpose(PT[:, (2 * j + r) * P:(2 * j + r + 1) * P],
                                          pb[:, B % PR, j, 2 * r:2 * r + 2, :], n.ident[:, :])
                mm.then_inc(pt_ready, 1)

            def values(B):
                g, b = divmod(B, NB)
                if b == 0:
                    pe.wait_ge(v_built, 4 * g + 4)
                pe.wait_ge(pt_copied, B + 1)
                if B >= 2:
                    pe.wait_ge(o_done, B - 1)
                for w in range(2):
                    for j in range(2):
                        for r in range(2):
                            at = (2 * j + r) * 2 * VW
                            mm = pe.matmul(O[B % 2][64 * w:64 * w + 64, at:at + 2 * VW],
                                           pT[:, B % 2, 2 * j + r, 64 * w:64 * w + 64],
                                           vb[:, w, b, j, r, :, :], start=True, stop=True)
                mm.then_inc(o_ready, 1)

            def shared(i, s):
                if s == 0 and real(i):
                    v(i, 0)
                    v(i, 1)
                if s == 2 and real(i - 2):
                    for c in range(2):
                        transposed("zt", lambda b: zn[:, b, :, :].rearrange("p j c -> p (j c)"), i - 2, c,
                                   lambda: pe.wait_ge(ln["z", "norm"], i - 1))
                if s == 2 and real(i - 3):
                    rank(i - 3)
                if s == 3 and real(i + 1):
                    for c in range(2):
                        transposed("xt", lambda b: xn[:, b, :, :].rearrange("p j c -> p (j c)"), i + 1, c,
                                   lambda: pe.wait_ge(ln["x", "norm"], i + 2))
                if s == 4 and real(i - 1):
                    for c in range(2):
                        transposed("ot", lambda b: ob[:, ((i - 1) * NB + b) % OR, :, :].rearrange("p h d -> p (h d)"),
                                   i - 1, c, lambda: pe.wait_ge(o_done, i * NB))
                if s == 4 and real(i + 1):
                    qk(i + 1, 0, 0)
                    qk(i + 1, 1, 0)
                if s == 5:
                    for c in range(2):
                        if real(i - 1):
                            pr(i - 1, c)
                        if real(i + 1):
                            qk(i + 1, c, 1)
                if s == 6 and real(i + 2):
                    t(i + 2, 0)
                    t(i + 2, 1)

            for i in BODIES:
                for s in range(NB):
                    B = i * NB + s
                    if 0 <= B < NBLK:
                        scores(B)
                    if s == 3:
                        shared(i, s)
                    if 0 <= B - 3 < NBLK:
                        values(B - 3)
                    if s != 3:
                        shared(i, s)
                    elif real(i - 2):
                        gate(i - 2)
                    if 0 <= B - 2 < NBLK:
                        turn_probs(B - 2)

        @block.scalar
        def _(act):
            def build_values(g):
                act.wait_ge(v_sw, 32 * (g + 1))
                act.wait_ge(ids_step, 4)
                if g >= 1:
                    act.wait_ge(o_ready, NB * g)
                for hh in range(2):
                    for w in range(2):
                        r = slice(64 * hh, 64 * hh + 64)
                        src = (vs if hh == w else vw)[r, :, :, :, hh, :].rearrange("p b j r d -> p (b j r) d")
                        act.activation(vb[r, w, :, :, :, hh, 0:HD].rearrange("p b j r d -> p (b j r) d"),
                                       src, ACT.Copy).then_inc(v_built, 1)

            def take(op, g, c, dst, wait=None):
                b0, nb, w = chunk(c)
                act.wait_ge(ready[op], 2 * g + c + 1)
                if wait:
                    act.wait_ge(*wait)
                act.activation(dst(b0, nb, w), bank_of(f"{op}{c}", g)[:, 0:w], ACT.Copy).then_inc(taken[op], 1)

            def cols(t):
                return lambda b0, nb, w: t[:, b0 * P:b0 * P + w]

            def queries(g, c):
                b0, nb, w = chunk(c)
                act.wait_ge(ready["q"], 2 * g + c + 1)
                for j in range(2):
                    ins = act.activation(qT[:, g % 2, j, b0 * P:b0 * P + w], bank_of(f"q{c}", g)[:, 0:w], ACT.Copy,
                                         scale=n.jmask[:, j:j + 1])
                ins.then_inc(taken["q"], 1)

            def keys(g, c):
                b0, nb, w = chunk(c)
                act.wait_ge(ready["k"], 2 * g + c + 1)
                for h in range(HEADS):
                    ins = act.activation(kx[:, g % 2, h, b0 * P:b0 * P + w], bank_of(f"k{c}", g)[:, 0:w],
                                         ACT.Copy, scale=n.hmask[:, h:h + 1])
                ins.then_inc(taken["k"], 1)

            for i in BODIES:
                for s in range(NB):
                    B = i * NB + s
                    V = B - 3
                    if 0 <= V < NBLK:
                        act.wait_ge(pt_ready, V + 1)
                        if V >= 2:
                            act.wait_ge(o_ready, V - 1)
                        act.activation(pT[:, V % 2, :, :].rearrange("p r t -> p (r t)"), PT[:, :],
                                       ACT.Copy).then_inc(pt_copied, 1)
                    X = B - 2
                    if 0 <= X < NBLK:
                        act.wait_ge(s_sub, X + 1)
                        act.activation(pb[:, X % PR, :, :, :], pb[:, X % PR, :, :, :], ACT.Exp,
                                       scale=SCALE).then_inc(s_exp, 1)
                    if s == 0 and real(i):
                        for c in range(2):
                            take("v", i, c,
                                 lambda b0, nb, w: vs[:, b0:b0 + nb, :, :, :, :].rearrange("p b j r h d -> p (b j r h d)"),
                                 (v_built, 4 * i) if c == 0 else None)
                    if s == 2 and real(i):
                        build_values(i)
                    if s == 2 and real(i - 2):
                        for c in range(2):
                            take("zt", i - 2, c, cols(actT), (ready["pr"], 2 * (i - 1)))
                    if s == 3 and real(i - 2):
                        if i >= 4:
                            act.wait_ge(scat[i % 2], 16 * GT * ((i - 2) // 2))
                        act.activation(xrow[:, i % 2, :, :, 0:CIN // 2].bitcast(F16), zn[:, :, :, :],
                                       ACT.Copy).then_inc(high, 1)
                    if s == 3 and real(i + 1):
                        for c in range(2):
                            take("xt", i + 1, c, cols(xnT), (ready["v"], 2 * i + 2))
                    if s == 5 and real(i - 2):
                        act.wait_ge(r_step, R_STEPS * (i - 2) + 3)
                        act.activation(lw[:, 0, :, :], lw[:, 0, :, :], ACT.Exp).then_inc(r_exp, 1)
                    if s == 4 and real(i - 1):
                        for c in range(2):
                            take("ot", i - 1, c, cols(actT), (ready["gate"], i - 1))
                    if s == 4 and real(i + 1):
                        if i >= 1:
                            act.wait_ge(s_ready, i * NB)
                        queries(i + 1, 0)
                    if s == 5 and real(i + 1):
                        queries(i + 1, 1)
                    if s in (5, 6) and real(i + 1):
                        keys(i + 1, s - 5)

        @block.vector
        def _(dve):
            dve.memset(notfirst[:, :, :], 1.0).then_inc(const, 1)
            dve.memset(carry[:, :], 0.0).then_inc(const, 1)
            dve.memset(s2g[96:99, :], 1.0).then_inc(const, 1)
            dve.wait_ge(const, 3)
            dve.memset(notfirst[:, :, 0:1], 0.0).then_inc(const, 1)
            dve.memset(zeros[:, :], 0.0).then_inc(const, 1)
            dve.wait_ge(const, 5)

            stat = [0]

            def chain(ins):
                stat[0] += 1
                ins.then_inc(stat_step, 1)
                dve.wait_ge(stat_step, stat[0])

            def ln_stats(w, st, g):
                dve.wait_ge(ln[w, "norm"], g)
                for b in range(NB):
                    for j in range(2):
                        ins = dve.bn_stats(bx[:, b, j, :], n.t2[:, g, b, j, :])
                chain(ins)
                f = bx[:, :, :, :].rearrange("p b j s -> p (b j) s")
                dve.tensor_tensor(st[:, 0, :], f[:, :, 1], f[:, :, 4], ALU.add)
                dve.tensor_tensor(st[:, 2, :], f[:, :, 1], f[:, :, 4], ALU.subtract)
                chain(dve.tensor_tensor(st[:, 3, :], f[:, :, 2], f[:, :, 5], ALU.add))
                dve.tensor_scalar(st[:, 1, :], st[:, 0, :], 0.5, None, ALU.mult).then_inc(ln[w, "mean"], 1)
                chain(dve.scalar_tensor_tensor(st[:, 2, :], st[:, 2, :], CIN / 4, st[:, 2, :], ALU.mult, ALU.mult))
                chain(dve.tensor_tensor(st[:, 3, :], st[:, 2, :], st[:, 3, :], ALU.add))
                dve.tensor_scalar(st[:, 4, :], st[:, 3, :], 1.0 / CIN, LN_EPS, ALU.mult, ALU.add)\
                    .then_inc(ln[w, "var"], 1)

            def t_clip(g):
                for c in range(2):
                    b0, nb, w = chunk(c)
                    dve.wait_ge(ready["t"], 2 * g + c + 1)
                    dve.tensor_scalar(n.t2[:, g, b0:b0 + nb, :, :],
                                      bank_of(f"t{c}", g)[:, 0:w].rearrange("p (b j c) -> p b j c", j=2, c=CIN),
                                      -1.0, 1.0, ALU.max, ALU.min).then_inc(taken["t"], 1)

            def x_stats(g):
                dve.wait_ge(taken["t"], 2 * g + 2)
                ln_stats("x", sx, g)

            def residual(g):
                for c in range(2):
                    b0, nb, w = chunk(c)
                    dve.wait_ge(ready["pr"], 2 * g + c + 1)
                    tt = n.t2[:, g, b0:b0 + nb, :, :]
                    dve.tensor_tensor(tt, bank_of(f"pr{c}", g)[:, 0:w].rearrange("p (b j c) -> p b j c", j=2, c=CIN),
                                      tt, ALU.add).then_inc(taken["pr"], 1)

            def z_stats(g):
                dve.wait_ge(taken["pr"], 2 * g + 2)
                ln_stats("z", sz, g)

            step = [0]

            def link(ins):
                step[0] += 1
                ins.then_inc(r_step, 1)
                dve.wait_ge(r_step, step[0])

            def route_a(g):
                assert step[0] == R_STEPS * g
                L = lg[:, :, :]
                dve.wait_ge(ready["gate"], g + 1)
                dve.tensor_tensor(L, bank_of("gate", g)[:, 0:GT * E].rearrange("p (t e) -> p t e", e=E),
                                  spread(n.gate_b[:, :], 1, GT), ALU.add).then_inc(taken["gate"], 1)
                dve.wait_ge(taken["gate"], g + 1)

            def route_b(g):
                L = lg[:, :, :]
                top = rt[:, 0, :]
                link(dve.tensor_reduce(top, L, AX.X, ALU.max))
                link(dve.tensor_tensor(lw[:, 1, :, :], L, spread(top, 2, E), ALU.is_ge))
                link(dve.tensor_tensor(lw[:, 0, :, :], L, spread(top, 2, E), ALU.subtract))
                link(dve.tensor_tensor(lw[:, 1, :, :], lw[:, 1, :, :], spread(n.em8[:, :], 1, GT), ALU.mult))
                link(dve.tensor_reduce(rt[:, 1, :], lw[:, 1, :, :], AX.X, ALU.min))
                link(dve.tensor_tensor(ohf[:, :, :], spread(n.em8[:, :], 1, GT),
                                       spread(rt[:, 1, :], 2, E), ALU.is_equal))
                dve.tensor_copy(oh[:, :, :], ohf[:, :, :]).then_inc(rank_q, 1)

            def weight(g):
                dve.wait_ge(r_exp, g + 1)
                link(dve.tensor_reduce(rt[:, 2, :], lw[:, 0, :, :], AX.X, ALU.add))
                link(dve.reciprocal(xrow[:, g % 2, :, :, RP], rt[:, 2, :].rearrange("p (b j) -> p b j", j=2)))

            def route_c(g):
                dve.wait_ge(ready["rank"], g + 1)
                bank = bank_of("rank", g)

                def by_expert(a):
                    return a.rearrange("p (b j e) -> p e j b", b=NB, j=2)

                def ordered(a):
                    return a.rearrange("p e (j b) -> p e j b", j=2)
                dve.tensor_copy(flat4(among), by_expert(bank[:, 0:GT * E]))
                dve.tensor_copy(flat4(cnt), by_expert(bank[:, GT * E:2 * GT * E])).then_inc(taken["rank"], 1)
                dve.wait_ge(taken["rank"], g + 1)
                link(dve.tensor_copy(sd[:, :, :], cnt[:, :, :]))
                link(dve.tensor_tensor(sd[:, :, 0], sd[:, :, 0], carry[:, :], ALU.add))
                link(dve.tensor_tensor_scan(inc[:, :, :].rearrange("p e t -> p (e t)"),
                                            notfirst[:, :, :].rearrange("p e t -> p (e t)"),
                                            sd[:, :, :].rearrange("p e t -> p (e t)"), 0.0, ALU.mult, ALU.add))
                link(dve.tensor_copy(carry[:, :], inc[:, :, GT - 1]))
                link(dve.tensor_tensor(cnt[:, :, :], inc[:, :, :], cnt[:, :, :], ALU.subtract))
                link(dve.tensor_tensor(sd[:, :, :], among[:, :, :], cnt[:, :, :], ALU.add))
                link(dve.tensor_tensor(flat4(sd), flat4(sd), by_expert(ohf[:, :, :].rearrange("p t e -> p (t e)")), ALU.mult))
                link(dve.tensor_reduce(rt[:, 3, :], sd[:, :, :].rearrange("p e t -> p t e"), AX.X, ALU.add))
                link(dve.tensor_scalar(rt[:, 4, :], rt[:, 3, :], CAP - 0.5, NOWHERE, ALU.is_gt, ALU.mult))
                link(dve.tensor_tensor(rt[:, 4, :], rt[:, 4, :], rt[:, 3, :], ALU.add))
                link(dve.tensor_scalar(rt[:, 5, :], rt[:, 1, :], float(ES), float(E * ES), ALU.mult, ALU.add))
                if g >= 2:
                    dve.wait_ge(scat[g % 2], 16 * GT * (g // 2))
                dve.tensor_tensor(dest[:, g % 2, :, :], rt[:, 5, :].rearrange("p (b j) -> p b j", j=2),
                                  rt[:, 4, :].rearrange("p (j b) -> p b j", j=2), ALU.add).then_inc(ranked, 1)

            def flat4(t):
                return t[:, :, :].rearrange("p e (j b) -> p e j b", j=2)

            def low_parts(g):
                dve.wait_ge(high, g + 1)
                dve.tensor_tensor(xrow[:, g % 2, :, :, CIN // 2:CIN].bitcast(F16), zn[:, :, :, :],
                                  xrow[:, g % 2, :, :, 0:CIN // 2].bitcast(F16), ALU.subtract).then_inc(low, 1)

            def norm(B):
                g, b = divmod(B, NB)
                dve.wait_ge(o_ready, B + 1)
                if B >= OR:
                    g0, b0 = divmod(B - OR, NB)
                    dve.wait_ge(ready["ot"], 2 * g0 + (1 if b0 < CHUNKS[1][0] else 2))
                o = O[B % 2][:, 0:8 * VW].rearrange("p (h v) -> p h v", v=VW)
                if B >= 2:
                    dve.wait_ge(o_done, B - 1)
                dve.reciprocal(rl[:, B % 2, :], o[:, :, HD]).then_inc(o_recip, 1)
                dve.wait_ge(o_recip, B + 1)
                dve.tensor_tensor(ob[:, B % OR, :, :], o[:, :, 0:HD], spread(rl[:, B % 2, :], 2, HD),
                                  ALU.mult).then_inc(o_done, 1)

            def soften(B):
                sc = S[B % 2][:, :].rearrange("p (h k) -> p h k", k=WIN)
                dve.wait_ge(s_ready, B + 1)
                if B >= 2:
                    dve.wait_ge(s_sub, B - 1)
                dve.tensor_reduce(mx[:, B % 2, :], sc, AX.X, ALU.max).then_inc(s_max, 1)
                if B >= PR:
                    dve.wait_ge(pt_ready, B - PR + 1)
                dve.wait_ge(s_max, B + 1)
                dve.tensor_tensor(pb[:, B % PR, :, :, :].rearrange("p j h k -> p (j h) k"), sc,
                                  spread(mx[:, B % 2, :], 2, WIN), ALU.subtract).then_inc(s_sub, 1)

            for i in BODIES:
                for s in range(NB):
                    B = i * NB + s
                    if 0 <= B - 1 < NBLK:
                        soften(B - 1)
                    if 0 <= B - 4 < NBLK:
                        norm(B - 4)
                    if s == 0 and real(i + 1):
                        t_clip(i + 1)
                        x_stats(i + 1)
                    if s == 3 and real(i - 3):
                        route_c(i - 3)
                    if s == 4 and real(i - 2):
                        route_a(i - 2)
                        low_parts(i - 2)
                        route_b(i - 2)
                    if s == 5 and real(i - 1):
                        residual(i - 1)
                    if s == 5 and real(i - 2):
                        weight(i - 2)
                    if s == 6 and real(i - 1):
                        z_stats(i - 1)
            dve.tensor_copy(n.counts[:, :], carry[0:1, :]).then_inc(counted, 1)
            dve.wait_ge(counted, 1)

        @block.gpsimd
        def _(pool):
            pool.memset(vb[:, :, :, :, :, :, :], 0.0).then_inc(ids_step, 1)
            pool.iota(ids[:, :, :], [[2, NB], [1, 2]], base=0, channel_multiplier=GT,
                      allow_small_or_imprecise_dtypes=True).then_inc(ids_step, 1)
            pool.wait_ge(ids_step, 2)
            for hh in range(2):
                pool.memset(vb[64 * hh:64 * hh + 64, :, :, :, :, hh, HD:VW].rearrange("p w b j r o -> p (w b j r) o"),
                            1.0).then_inc(ids_step, 1)
            pool.wait_ge(ids_step, 4)

            def layer_norm(w, g, dst, st):
                pool.wait_ge(ln[w, "mean"], g + 1)
                if g >= 1:
                    if w == "x":
                        pool.wait_ge(ready["xt"], 2 * g)
                    else:
                        pool.wait_ge(ready["zt"], 2 * g)
                        pool.wait_ge(low, g)
                pool.tensor_tensor(dst[:, :, :, :], n.t2[:, g, :, :, :],
                                   spread(st[:, 1, :].rearrange("p (b j) -> p b j", j=2), 3, CIN),
                                   ALU.subtract).then_inc(centered, 1)
                pool.wait_ge(ln[w, "var"], g + 1)
                pool.tensor_tensor(st[:, 5, :], st[:, 4, :], n.mhalf[:, 0:GT], ALU.pow).then_inc(ln[w, "rstd"], 1)
                pool.wait_ge(ln[w, "rstd"], g + 1)
                pool.tensor_tensor(dst[:, :, :, :], dst[:, :, :, :],
                                   spread(st[:, 5, :].rearrange("p (b j) -> p b j", j=2), 3, CIN),
                                   ALU.mult).then_inc(ln[w, "norm"], 1)

            def scatter(g, lo, hi):
                if lo == 0:
                    if g >= 2:
                        pool.wait_ge(scat[g % 2], 16 * GT * (g // 2))
                    pool.tensor_scalar(xrow[:, g % 2, :, :, RI], ids[:, :, :], float(g * GT * P), None,
                                       ALU.add).then_inc(numbered, 1)
                    pool.wait_ge(numbered, g + 1)
                    pool.wait_ge(ranked, g + 1)
                for k in range(lo, hi):
                    b, j = divmod(k, 2)
                    pool.indirect_dma_start(n.slots, bass.IndirectOffsetOnAxis(ap=dest[:, g % 2, b, j:j + 1], axis=0),
                                            xrow[:, g % 2, b, j, :], None, bounds_check=SLOTS - 1,
                                            oob_is_err=False).then_inc(scat[g % 2], 16)

            for i in BODIES:
                for s in range(NB):
                    if s == 0 and real(i - 2):
                        layer_norm("z", i - 2, zn, sz)
                    if s == 1 and real(i + 1):
                        layer_norm("x", i + 1, xn, sx)
                    if s == 3 and real(i - 3):
                        scatter(i - 3, 0, GT)
            for q in range(2):
                pool.wait_ge(scat[q], 16 * GT * ((NG + 1 - q) // 2))


def expert_stage(nc, n):
    with ExitStack() as ctx:
        def sb(name, shape, dt=F32):
            return ctx.enter_context(nc.sbuf_tensor(name, shape, dt))

        def sem(name):
            return ctx.enter_context(nc.semaphore(name))

        QUADS = [(e, e * ES + s * P, min(4, TPE - s)) for e in range(E) for s in range(0, TPE, 4)]
        NQD, QPE = len(QUADS), -(-TPE // 4)
        RR, YR, YT = 4, 4, 4
        rows = sb("rows", [P, RR, 4, ROW])
        xT = sb("xT", [P, 2, 4 * P], F16)
        idx = sb("idx", [P, YR, 4], I32)
        w1f = sb("w1f_e", [P, F])
        w2f = sb("w2f_e", [P, 2, CIN])
        w1 = sb("w1_parts", [P, 2, 2, F], F16)
        w2 = sb("w2_parts", [P, 2, 2, 2, CIN], F16)
        BW = F + CIN
        BIAS_SPANS = ((0, BW), (BW, E * BW))
        bf = sb("bias_row", [1, E * (F + CIN)])
        bp = sb("bias_parts", [1, 2, E * (F + CIN)], F16)
        bias = sb("bias", [2, E * (F + CIN)], F16)
        ones = sb("ones2", [2, 4 * P], F16)
        hh = sb("h_high", [P, 2, 2, 4 * P], F16)
        hl = sb("h_low", [P, 2, 2, 4 * P], F16)
        ye = sb("ye", [P, YR, 4, CIN])
        lim = sb("lim", [P, 4, CIN])
        bad = sb("bad", [P, 2, 4, CIN], I32)
        zero = sb("zero", [P, 4, CIN])
        yt = sb("yt", [P, YT, NB, 2, CIN])
        fin = sb("fin", [P, 2, NB, 2, CIN])
        out = sb("out", [P, 2, GW])
        A = [ctx.enter_context(nc.psum_tensor(f"A{i}", [P, 1024], F16)) for i in range(2)]
        Hb = [[ctx.enter_context(nc.psum_tensor(f"H{i}{c}", [P, 512], F32)) for c in range(2)] for i in range(2)]
        Y = [ctx.enter_context(nc.psum_tensor(f"Y{i}", [P, 512], F32)) for i in range(2)]

        row_in = [sem(f"row_in{k}") for k in range(RR)]
        w_in, w_split, b_in, b_split, b_moved = sem("ew_in"), sem("w_split"), sem("b_in"), sem("b_split"), [sem("b_moved0"), sem("b_moved1")]
        xt_ready, xt_taken = sem("xT_ready"), sem("xT_taken")
        h_ready, hh_done, hl_done = sem("h_ready"), sem("hh_done"), sem("hl_done")
        y_ready, y_taken, y_checked, y_full = sem("y_ready"), sem("y_taken"), sem("y_checked"), sem("y_full")
        idx_done, zeroed = sem("idx_done"), sem("zeroed")
        LAG = 2
        sent = [sem(f"sent{k}") for k in range(LAG + 1)]
        sent_late = [[sem(f"sent_late{e}_{k}") for k in range(LAG + 1)] for e in range(E)]
        retired = sem("quads_retired")
        yt_in = [sem(f"yt_in{k}") for k in range(YT)]
        summed, o_ready, o_taken = sem("summed"), sem("out_ready"), sem("out_taken")
        stored = [sem("stored0"), sem("stored1")]
        block = ctx.enter_context(nc.Block())

        def late(g):
            e, s0, _ = QUADS[g]
            return s0 - e * ES >= TOK // E // 2

        def counts(eng):
            return [eng.value_load(n.counts[0:1, e:e + 1]) for e in range(E)]

        def if_filled(eng, count, g, work, *counted):
            if not late(g):
                work(g)
                return
            e, s0, _ = QUADS[g]
            with eng.If(count[e] > s0 - e * ES):
                work(g)
            if counted:
                with eng.If(count[e] <= s0 - e * ES):
                    for done, each in counted:
                        eng.wait_ge(done, each * g)
                        eng.sem_inc(done, each)

        n_out = [sum(len(pieces((2 * g + j) * GW, GW)) for j in range(2)) for g in range(NG)]

        @block.sync
        def _(sp):
            def weights(e):
                if e >= 1:
                    sp.wait_ge(w_split, 4 * e)
                for u in range(2):
                    sp.dma_start(w1f[64 * u:64 * u + 64, :], n.e_w1[e]).then_inc(w_in, 16)
                sp.dma_start(w2f[:, :, :], n.e_w2[e].rearrange("(c f) d -> f c d", c=2)).then_inc(w_in, 16)

            def load_rows(g):
                e, s0, nt = QUADS[g]
                if g >= RR:
                    sp.wait_ge(y_taken, g - RR + 1)
                    sp.wait_ge(idx_done, g - RR + 1)
                    sp.wait_ge(row_in[g % RR], 16 * (g // RR))
                sp.dma_start(rows[:, g % RR, 0:nt, :],
                             n.slots[s0:s0 + nt * P, :].rearrange("(p u) d -> p u d", u=nt)
                             ).then_inc(row_in[g % RR], 16)

            load_rows(0)
            weights(0)
            for lo, hi in BIAS_SPANS:
                sp.dma_start(bf[:, lo:hi], n.e_b[:, lo:hi]).then_inc(b_in, 16)
            load_rows(1)
            for k, (lo, hi) in enumerate(BIAS_SPANS):
                sp.wait_ge(b_split, 2 * k + 2)
                for part in range(2):
                    sp.dma_start(bias[part:part + 1, lo:hi], bp[:, part, lo:hi]).then_inc(b_moved[k], 16)
                if k == 0:
                    load_rows(2)
                    load_rows(3)
            for g in range(4, NQD):
                e, k = divmod(g, QPE)
                load_rows(g)
                if k == 5 and e + 1 < E:
                    weights(e + 1)
            sp.wait_ge(retired, NQD)

            def load(g):
                if g >= YT:
                    sp.wait_ge(summed, g - YT + 1)
                sp.dma_start(yt[:, g % YT, :, :, :].rearrange("p b j d -> p (b j) d"),
                             n.y_tok[g * GT * P:(g + 1) * GT * P, :].rearrange("(p t) d -> p t d", p=P)
                             ).then_inc(yt_in[g % YT], 16)

            for g in range(YT - 1):
                load(g)
            for g in range(NG):
                if g + YT - 1 < NG:
                    load(g + YT - 1)
                sp.wait_ge(o_taken, 2 * g + 2)
                for j in range(2):
                    for image, pixel, at, m in pieces((2 * g + j) * GW, GW):
                        sp.dma_start(n.out[image, :, pixel:pixel + m],
                                     out[64 * j:64 * j + 64, g % 2, at:at + m]).then_inc(stored[g % 2], 16)
            for q in range(2):
                sp.wait_ge(stored[q], 16 * sum(n_out[q::2]))

        @block.tensor
        def _(pe):
            def turn(g):
                nt = QUADS[g][2]
                pe.wait_ge(row_in[g % RR], 16 * (g // RR + 1))
                if g >= 2:
                    pe.wait_ge(xt_taken, g - 1)
                for u in range(nt):
                    mm = pe.transpose(A[g % 2][:, u * P:(u + 1) * P], rows[:, g % RR, u, 0:CIN].bitcast(F16),
                                      n.ident_h[:, :])
                mm.then_inc(xt_ready, 1)

            def first(g):
                e, _, nt = QUADS[g]
                w = nt * P
                if g == 0:
                    pe.wait_ge(zeroed, 2)
                    pe.wait_ge(b_moved[0], 32)
                if g == QPE:
                    pe.wait_ge(b_moved[1], 32)
                pe.wait_ge(xt_taken, g + 1)
                for c in range(2):
                    if g >= 2:
                        pe.wait_ge(hl_done, 2 * (g - 2) + c + 1)
                    at = e * BW + c * P
                    bank = Hb[g % 2][c][:, 0:w]
                    pe.matmul(bank, bias[:, at:at + P], ones[:, 0:w], start=True, stop=False)
                    for part in range(2):
                        mm = pe.matmul(bank, w1[:, e % 2, part, c * P:(c + 1) * P], xT[:, g % 2, 0:w],
                                       start=False, stop=(part == 1))
                    mm.then_inc(h_ready, 1)

            def second(g):
                e, _, nt = QUADS[g]
                bank = Y[g % 2]
                if g >= 2:
                    pe.wait_ge(y_taken, g - 1)
                at = e * BW + F
                pe.matmul(bank[:, 0:nt * CIN].rearrange("p (u c) -> p u c", c=CIN), ones[:, 0:P],
                          spread(bias[:, at:at + CIN], 1, nt), start=True, stop=False, skip_group_check=True)
                for c in range(2):
                    pe.wait_ge(hl_done, 2 * g + c + 1)
                    for u in range(nt):
                        for h in (hh, hl):
                            for part in range(2):
                                mm = pe.matmul(bank[:, u * CIN:(u + 1) * CIN], h[:, g % 2, c, u * P:(u + 1) * P],
                                               w2[:, e % 2, part, c, :], start=False, stop=(c == 1 and part == 1 and h is hl),
                                               skip_group_check=True)
                mm.then_inc(y_ready, 1)

            count = counts(pe)
            for k in range(-2, NQD):
                if k + 2 < NQD:
                    if_filled(pe, count, k + 2, turn, (xt_ready, 1))
                if 0 <= k + 1 < NQD:
                    if (k + 1) % QPE == 0:
                        pe.wait_ge(w_split, 4 * QUADS[k + 1][0] + 4)
                    if_filled(pe, count, k + 1, first, (h_ready, 2))
                if 0 <= k:
                    if_filled(pe, count, k, second, (y_ready, 1))
            for g in range(NG):
                pe.wait_ge(summed, g + 1)
                for c, (b0, nb) in enumerate(CHUNKS):
                    if g >= 2:
                        pe.wait_ge(o_taken, 2 * (g - 2) + c + 1)
                    for b in range(nb):
                        mm = pe.transpose(Hb[g % 2][c][:, b * P:(b + 1) * P],
                                          fin[:, g % 2, b0 + b, :, :].rearrange("p j c -> p (j c)"), n.ident[:, :])
                    mm.then_inc(o_ready, 1)

        @block.scalar
        def _(act):
            def turned(g):
                w = QUADS[g][2] * P
                act.wait_ge(xt_ready, g + 1)
                if g >= 2:
                    act.wait_ge(h_ready, 2 * (g - 1))
                act.activation(xT[:, g % 2, 0:w], A[g % 2][:, 0:w], ACT.Copy).then_inc(xt_taken, 1)

            def high(g):
                w = QUADS[g][2] * P
                for c in range(2):
                    act.wait_ge(h_ready, 2 * g + c + 1)
                    if g >= 2 and c == 0:
                        act.wait_ge(y_ready, g - 1)
                    act.activation(hh[:, g % 2, c, 0:w], Hb[g % 2][c][:, 0:w], ACT.Relu).then_inc(hh_done, 1)

            count = counts(act)
            for k in range(-2, NQD - 1):
                if k + 2 < NQD:
                    if_filled(act, count, k + 2, turned, (xt_taken, 1))
                if 0 <= k + 1:
                    if_filled(act, count, k + 1, high, (hh_done, 2))
            for g in range(NG):
                if g >= 2:
                    act.wait_ge(stored[g % 2], 16 * sum(n_out[g % 2:g:2]))
                for c, (b0, nb) in enumerate(CHUNKS):
                    act.wait_ge(o_ready, 2 * g + c + 1)
                    act.activation(out[:, g % 2, b0 * P:(b0 + nb) * P], Hb[g % 2][c][:, 0:nb * P],
                                   ACT.Copy).then_inc(o_taken, 1)

        @block.vector
        def _(dve):
            dve.memset(zero[:, :, :], 0.0).then_inc(zeroed, 1)
            dve.memset(ones[:, :], 1.0).then_inc(zeroed, 1)

            def split_weights(e):
                q = e % 2
                dve.wait_ge(w_in, 48 * (e + 1))
                if e >= 2:
                    dve.wait_ge(y_ready, (e - 1) * QPE)
                dve.tensor_copy(w1[:, q, 0, :], w1f[:, :]).then_inc(w_split, 1)
                dve.tensor_copy(w2[:, q, 0, :, :], w2f[:, :, :]).then_inc(w_split, 1)
                dve.wait_ge(w_split, 4 * e + 2)
                dve.tensor_tensor(w1[:, q, 1, :], w1f[:, :], w1[:, q, 0, :], ALU.subtract).then_inc(w_split, 1)
                dve.tensor_tensor(w2[:, q, 1, :, :], w2f[:, :, :], w2[:, q, 0, :, :], ALU.subtract).then_inc(w_split, 1)

            split_weights(0)
            for k, (lo, hi) in enumerate(BIAS_SPANS):
                dve.wait_ge(b_in, 32)
                dve.tensor_copy(bp[:, 0, lo:hi], bf[:, lo:hi]).then_inc(b_split, 1)
                dve.wait_ge(b_split, 2 * k + 1)
                dve.tensor_tensor(bp[:, 1, lo:hi], bf[:, lo:hi], bp[:, 0, lo:hi], ALU.subtract).then_inc(b_split, 1)
            dve.wait_ge(zeroed, 2)

            def low(g):
                w = QUADS[g][2] * P
                for c in range(2):
                    dve.wait_ge(hh_done, 2 * g + c + 1)
                    if g >= 2 and c == 0:
                        dve.wait_ge(y_ready, g - 1)
                    dve.scalar_tensor_tensor(hl[:, g % 2, c, 0:w], Hb[g % 2][c][:, 0:w], 0.0, hh[:, g % 2, c, 0:w],
                                             ALU.max, ALU.subtract).then_inc(hl_done, 1)

            def weigh(g):
                nt = QUADS[g][2]
                r = rows[:, g % RR, 0:nt, :]
                yy = ye[:, g % YR, 0:nt, :]
                if g >= YR:
                    dve.wait_ge(retired, g - YR + 1)
                dve.tensor_copy(idx[:, g % YR, 0:nt], r[:, :, RI]).then_inc(idx_done, 1)
                dve.wait_ge(y_ready, g + 1)
                dve.tensor_tensor(yy, Y[g % 2][:, 0:nt * CIN].rearrange("p (u c) -> p u c", c=CIN),
                                  spread(r[:, :, RP], 2, CIN), ALU.mult).then_inc(y_taken, 1)
                dve.wait_ge(y_taken, g + 1)
                dve.tensor_scalar(bad[:, 0, 0:nt, :], yy, 0.0, 0.0, ALU.mult, ALU.not_equal).then_inc(y_checked, 1)
                dve.tensor_scalar(lim[:, 0:nt, :], yy, -1e4, 1e4, ALU.max, ALU.min).then_inc(y_checked, 1)
                dve.tensor_tensor(bad[:, 1, 0:nt, :], yy, yy, ALU.not_equal).then_inc(y_checked, 1)
                dve.wait_ge(y_checked, 4 * g + 3)
                dve.copy_predicated(yy, bad[:, 0, 0:nt, :], lim[:, 0:nt, :]).then_inc(y_checked, 1)
                dve.wait_ge(y_checked, 4 * g + 4)
                dve.copy_predicated(yy, bad[:, 1, 0:nt, :], zero[:, 0:nt, :]).then_inc(y_full, 1)

            count = counts(dve)
            for k in range(-1, NQD):
                if k + 1 < NQD:
                    if (k + 1) % QPE == 7 and QUADS[k + 1][0] + 1 < E:
                        split_weights(QUADS[k + 1][0] + 1)
                    if_filled(dve, count, k + 1, low, (hl_done, 2))
                if 0 <= k:
                    if_filled(dve, count, k, weigh, (idx_done, 1), (y_taken, 1), (y_checked, 4), (y_full, 1))
            for g in range(NG):
                dve.wait_ge(yt_in[g % YT], 16 * (g // YT + 1))
                if g >= 2:
                    dve.wait_ge(o_ready, 2 * (g - 1))
                dve.tensor_tensor(fin[:, g % 2, :, :, :], n.t2[:, g, :, :, :], yt[:, g % YT, :, :, :],
                                  ALU.add).then_inc(summed, 1)

        @block.gpsimd
        def _(pool):
            def done(g):
                e = QUADS[g][0]
                same = [h for h in range(g + 1) if h % (LAG + 1) == g % (LAG + 1) and late(h) == late(g)
                        and (not late(g) or QUADS[h][0] == e)]
                return (sent_late[e] if late(g) else sent)[g % (LAG + 1)], 16 * sum(QUADS[h][2] for h in same)

            def scatter(g):
                for u in range(QUADS[g][2]):
                    pool.indirect_dma_start(n.y_tok, bass.IndirectOffsetOnAxis(ap=idx[:, g % YR, u:u + 1], axis=0),
                                            ye[:, g % YR, u, :], None, bounds_check=TOK - 1,
                                            oob_is_err=False).then_inc(done(g)[0], 16)

            def retire(g):
                if_filled(pool, count, g, lambda h: pool.wait_ge(*done(h)))
                pool.sem_inc(retired, 1)

            count = counts(pool)
            for g in range(NQD):
                pool.wait_ge(y_full, g + 1)
                pool.wait_ge(idx_done, g + 1)
                if_filled(pool, count, g, scatter)
                if g >= LAG:
                    retire(g - LAG)
            for g in range(NQD - LAG, NQD):
                retire(g)


def kernel(x, L0_conv_w1, L0_conv_w2, L0_conv_w3, L0_conv_g1, L0_conv_b1, L0_conv_g2, L0_conv_b2, L0_conv_g3,
           L0_conv_b3, L1_attn_Wqkv, L1_attn_Wproj, L1_attn_bproj, L1_ffn_gate_w, L1_ffn_gate_b, L1_ffn_w1,
           L1_ffn_b1, L1_ffn_w2, L1_ffn_b2):
    import numpy as _np
    import concourse.bacc as _bacc
    from concourse import mybir as _mybir
    from concourse.bass_utils import run_bass_kernel_spmd as _run

    a = _np.asarray
    arrays = {
        "x": a(x).reshape(NIMG, CIN, PIX),
        "w1": a(L0_conv_w1).reshape(CB, CIN).T,
        "w2": a(L0_conv_w2).transpose(1, 2, 3, 0).reshape(CB, 9, CB),
        "w3": a(L0_conv_w3).reshape(CIN, CB).T,
        "gb12": _np.stack([a(v).reshape(CB) for v in (L0_conv_g1, L0_conv_b1, L0_conv_g2, L0_conv_b2)], 1),
        "w3n": a(L0_conv_w3).reshape(CIN, CB),
        "gb3": _np.stack([a(v).reshape(CIN) for v in (L0_conv_g3, L0_conv_b3)], 1),
        "w_qkv": a(L1_attn_Wqkv),
        "w_proj": a(L1_attn_Wproj),
        "b_proj": a(L1_attn_bproj).reshape(1, CIN),
        "gate_w": a(L1_ffn_gate_w),
        "gate_bias": a(L1_ffn_gate_b).reshape(1, E),
        "e_w1": a(L1_ffn_w1),
        "e_w2": a(L1_ffn_w2),
        "e_b": _np.concatenate([a(L1_ffn_b1), a(L1_ffn_b2)], 1).reshape(1, E * (F + CIN)),
    }
    arrays = {k: _np.ascontiguousarray(v) for k, v in arrays.items()}
    nc = _bacc.Bacc("TRN2", target_bir_lowering=False, num_devices=1)
    aps = {k: nc.dram_tensor(f"in_{k}", v.shape, _mybir.dt.from_np(v.dtype), kind="ExternalInput").ap()
           for k, v in arrays.items()}
    aps["out"] = nc.dram_tensor("out_0", (NIMG, CIN, PIX), F32, kind="ExternalOutput").ap()
    build(nc, aps)
    r = _run(nc, [{f"in_{k}": v for k, v in arrays.items()}], core_ids=[0])
    return r.results[0]["out_0"].reshape(NIMG, CIN, H, W)
```
